# Optimizing a Trainium2 kernel written in Bass

```python
import numpy as np
import jax
import jax.numpy as jnp

def _softmax(x, axis=-1):
    return jax.nn.softmax(x, axis=axis)

def _gelu(x):
    return jax.nn.gelu(x, approximate=True)

def _silu(x):
    return jax.nn.silu(x)

def _sigmoid(x):
    return jax.nn.sigmoid(x)

def _layernorm(x, axis=-1, eps=1e-05):
    m = jnp.mean(x, axis=axis, keepdims=True)
    v = jnp.var(x, axis=axis, keepdims=True)
    return (x - m) / jnp.sqrt(v + eps)

def _scatter_add(tgt, idx, src, axis=0):
    return tgt.at[idx].add(src)

def _segment_sum(src, seg, n):
    return jax.ops.segment_sum(src, seg, n)
kernel_name = 'mk_sandwich_d4_jaxref_r4_70bab6'

def setup_inputs(seed: int=0):
    np.random.seed(seed)
    _w = jnp.asarray

    def _L0_attn_setup():
        import jax, jax.numpy as jnp
        import numpy as np
        E = 256
        H = 16
        D = E // H
        WIN = 64
        STRIDE = 128
        G = 1
        B = 2
        L = 4097
        key = jax.random.key(seed)
        ks = jax.random.split(key, 9)
        s = 0.02
        return {'hidden_states': jax.random.normal(ks[0], (B, L, E), jnp.float32), 'Wq': jax.random.normal(ks[1], (E, E), jnp.float32) * s, 'bq': jnp.zeros((E,), jnp.float32), 'Wk': jax.random.normal(ks[2], (E, E), jnp.float32) * s, 'bk': jnp.zeros((E,), jnp.float32), 'Wv': jax.random.normal(ks[3], (E, E), jnp.float32) * s, 'bv': jnp.zeros((E,), jnp.float32), 'Wo': jax.random.normal(ks[4], (E, E), jnp.float32) * s, 'bo': jnp.zeros((E,), jnp.float32)}
    _L0_attn_in = _L0_attn_setup()

    def _L0_ffn_setup():
        import jax, jax.numpy as jnp
        import numpy as np
        EMB = 256
        FF = 4 * EMB

        def _ternary(w):
            scale = jnp.maximum(jnp.mean(jnp.abs(w)), 1e-08)
            w_t = jnp.clip(jnp.round(w / scale), -1.0, 1.0)
            return w + jax.lax.stop_gradient(w_t - w)
        key = jax.random.key(seed)
        kx, k1, k2, kb1, kb2 = jax.random.split(key, 5)
        x = jax.random.normal(kx, (4, 512, EMB), dtype=jnp.float32)
        lim1 = 1.0 / np.sqrt(EMB)
        lim2 = 1.0 / np.sqrt(FF)
        W1 = jax.random.uniform(k1, (FF, EMB), jnp.float32, -lim1, lim1)
        b1 = jax.random.uniform(kb1, (FF,), jnp.float32, -lim1, lim1)
        W2 = jax.random.uniform(k2, (EMB, FF), jnp.float32, -lim2, lim2)
        b2 = jax.random.uniform(kb2, (EMB,), jnp.float32, -lim2, lim2)
        return {'x': x, 'W1': W1, 'b1': b1, 'W2': W2, 'b2': b2}
    _L0_ffn_in = _L0_ffn_setup()

    def _L1_attn_setup():
        import jax, jax.numpy as jnp
        import numpy as np
        import math
        D_MODEL = 256
        D_STATE = 64
        EXPAND = 2
        D_CONV = 4
        D_INNER = D_MODEL * EXPAND
        NHEADS = D_INNER // D_STATE
        HEADDIM = D_INNER // NHEADS
        D_PROJ = 2 * D_INNER + NHEADS * (2 * D_STATE + 1)
        BATCH, SEQLEN = (2, 256)

        def _ssm_forward(x, W_in, conv_w, conv_b, A_log, D, dt_bias, W_out):
            B, L, _ = x.shape
            d, n, s = (D_INNER, NHEADS, D_STATE)
            proj = x @ W_in.T
            x_inner = proj[..., :d]
            z = proj[..., d:2 * d]
            bc_dt = proj[..., 2 * d:].reshape(B, L, n, 2 * s + 1)
            B_proj = bc_dt[..., :s]
            C_proj = bc_dt[..., s:2 * s]
            dt_proj = bc_dt[..., 2 * s]
            xc = jax.lax.conv_general_dilated(jnp.transpose(x_inner, (0, 2, 1)), conv_w, window_strides=(1,), padding=[(D_CONV - 1, 0)], feature_group_count=d, dimension_numbers=('NCH', 'OIH', 'NCH'))
            xc = xc + conv_b[None, :, None]
            x_conv = jax.nn.silu(jnp.transpose(xc, (0, 2, 1)))
            x_heads = x_conv.reshape(B, L, n, HEADDIM)
            A = -jnp.exp(A_log)
            dt = jax.nn.softplus(dt_proj + dt_bias)
            dA = jnp.exp(A[None, None] * dt[..., None])
            dB = B_proj * dt[..., None]

            def step(h, inp):
                dA_t, dB_t, C_t, x_t = inp
                h = dA_t[..., None] * h + dB_t[..., None] * x_t[:, :, None, :]
                y_t = jnp.einsum('bns,bnsd->bnd', C_t, h)
                return (h, y_t)
            h0 = jnp.zeros((B, n, s, HEADDIM), dtype=x.dtype)
            xs = (jnp.moveaxis(dA, 1, 0), jnp.moveaxis(dB, 1, 0), jnp.moveaxis(C_proj, 1, 0), jnp.moveaxis(x_heads, 1, 0))
            _, y_scan = jax.lax.scan(step, h0, xs)
            y_heads = jnp.moveaxis(y_scan, 0, 1)
            y_heads = y_heads + D[None, None, :, None] * x_heads
            y = y_heads.reshape(B, L, d) * jax.nn.silu(z)
            return y @ W_out.T
        key = jax.random.key(seed)
        ks = jax.random.split(key, 6)
        x = jax.random.normal(ks[0], (BATCH, SEQLEN, D_MODEL), dtype=jnp.float32)
        W_in = jax.random.normal(ks[1], (D_PROJ, D_MODEL), dtype=jnp.float32) * 0.02
        conv_w = jax.random.normal(ks[2], (D_INNER, 1, D_CONV), dtype=jnp.float32) * (1.0 / math.sqrt(D_CONV))
        conv_b = jnp.zeros((D_INNER,), dtype=jnp.float32)
        A_log = jnp.tile(jnp.log(jnp.arange(1, D_STATE + 1, dtype=jnp.float32))[None, :], (NHEADS, 1))
        D = jnp.ones((NHEADS,), dtype=jnp.float32)
        u = jax.random.uniform(ks[3], (NHEADS,), dtype=jnp.float32)
        dt_bias = u * (math.log(0.1) - math.log(0.001)) + math.log(0.001)
        W_out = jax.random.normal(ks[4], (D_MODEL, D_INNER), dtype=jnp.float32) * (0.02 / math.sqrt(2))
        return {'x': x, 'W_in': W_in, 'conv_w': conv_w, 'conv_b': conv_b, 'A_log': A_log, 'D': D, 'dt_bias': dt_bias, 'W_out': W_out}
    _L1_attn_in = _L1_attn_setup()

    def _L1_ffn_setup():
        import jax, jax.numpy as jnp
        import numpy as np
        DIM = 256

        def _reference_tuple_inner(x, W_r, W_k, W_v, mu_r, mu_k):
            B, T, C = x.shape
            x_prev = jnp.concatenate([jnp.zeros((B, 1, C), x.dtype), x[:, :-1, :]], axis=1)
            xr = mu_r * x + (1.0 - mu_r) * x_prev
            xk = mu_k * x + (1.0 - mu_k) * x_prev
            r = jax.nn.sigmoid(jnp.einsum('btc,dc->btd', xr, W_r))
            k = jnp.einsum('btc,dc->btd', xk, W_k)
            k_act = jnp.square(jax.nn.relu(k))
            out = r * jnp.einsum('btc,dc->btd', k_act, W_v)
            new_state = x[:, -1, :]
            return (out, new_state)
        key = jax.random.key(seed)
        ks = jax.random.split(key, 6)
        B, T, C = (8, 512, DIM)
        x = jax.random.normal(ks[0], (B, T, C), dtype=jnp.float32)
        s = 1.0 / np.sqrt(C)
        W_r = jax.random.uniform(ks[1], (C, C), jnp.float32, -s, s)
        W_k = jax.random.uniform(ks[2], (C, C), jnp.float32, -s, s)
        W_v = jax.random.uniform(ks[3], (C, C), jnp.float32, -s, s)
        mu_r = jax.random.uniform(ks[4], (C,), jnp.float32)
        mu_k = jax.random.uniform(ks[5], (C,), jnp.float32)
        return {'x': x, 'W_r': W_r, 'W_k': W_k, 'W_v': W_v, 'mu_r': mu_r, 'mu_k': mu_k}
    _L1_ffn_in = _L1_ffn_setup()

    def _L2_attn_setup():
        import jax, jax.numpy as jnp
        import numpy as np
        import math
        B, S, E, H = (2, 512, 256, 16)
        D = E // H
        SCALE = 1.0 / math.sqrt(D)
        key = jax.random.key(seed)
        ks = jax.random.split(key, 5)
        std = 0.02
        return {'q': jax.random.normal(ks[0], (B, S, E), dtype=jnp.float32), 'Wq': jax.random.normal(ks[1], (E, H * D), dtype=jnp.float32) * std, 'Wk': jax.random.normal(ks[2], (E, H * D), dtype=jnp.float32) * std, 'Wv': jax.random.normal(ks[3], (E, H * D), dtype=jnp.float32) * std, 'Wo': jax.random.normal(ks[4], (H * D, E), dtype=jnp.float32) * std, 'gamma': jnp.ones((H,), dtype=jnp.float32)}
    _L2_attn_in = _L2_attn_setup()

    def _L2_ffn_setup():
        import jax, jax.numpy as jnp
        import numpy as np
        DIM = 256

        def _reference_tuple_inner(x, W_r, W_k, W_v, mu_r, mu_k):
            B, T, C = x.shape
            x_prev = jnp.concatenate([jnp.zeros((B, 1, C), x.dtype), x[:, :-1, :]], axis=1)
            xr = mu_r * x + (1.0 - mu_r) * x_prev
            xk = mu_k * x + (1.0 - mu_k) * x_prev
            r = jax.nn.sigmoid(jnp.einsum('btc,dc->btd', xr, W_r))
            k = jnp.einsum('btc,dc->btd', xk, W_k)
            k_act = jnp.square(jax.nn.relu(k))
            out = r * jnp.einsum('btc,dc->btd', k_act, W_v)
            new_state = x[:, -1, :]
            return (out, new_state)
        key = jax.random.key(seed)
        ks = jax.random.split(key, 6)
        B, T, C = (8, 512, DIM)
        x = jax.random.normal(ks[0], (B, T, C), dtype=jnp.float32)
        s = 1.0 / np.sqrt(C)
        W_r = jax.random.uniform(ks[1], (C, C), jnp.float32, -s, s)
        W_k = jax.random.uniform(ks[2], (C, C), jnp.float32, -s, s)
        W_v = jax.random.uniform(ks[3], (C, C), jnp.float32, -s, s)
        mu_r = jax.random.uniform(ks[4], (C,), jnp.float32)
        mu_k = jax.random.uniform(ks[5], (C,), jnp.float32)
        return {'x': x, 'W_r': W_r, 'W_k': W_k, 'W_v': W_v, 'mu_r': mu_r, 'mu_k': mu_k}
    _L2_ffn_in = _L2_ffn_setup()

    def _L3_attn_setup():
        import jax, jax.numpy as jnp
        import numpy as np
        PI = float(np.pi)
        EPS = 1e-06
        key = jax.random.key(seed)
        k1, k2, k3, k4, k5 = jax.random.split(key, 5)
        B, T, D, H, Dh = (4, 1024, 256, 16, 64)

        def xavier(k, shape):
            fan_in, fan_out = (shape[-2], shape[-1])
            lim = float(np.sqrt(6.0 / (fan_in + fan_out)))
            return jax.random.uniform(k, shape, jnp.float32, -lim, lim)
        return {'query': jax.random.normal(k1, (B, T, D), jnp.float32), 'W_Q': xavier(k2, (H, D, 1)), 'W_K': xavier(k3, (H, D, 1)), 'W_V': xavier(k4, (H, D, Dh)), 'W_O': xavier(k5, (D, Dh, H))}
    _L3_attn_in = _L3_attn_setup()

    def _L3_ffn_setup():
        import jax, jax.numpy as jnp
        import numpy as np
        import math
        BETA = 0.9
        THRESHOLD = 1.0
        NUM_STEPS = 5
        ALPHA = 2.0

        @jax.custom_vjp
        def spike_fn(u):
            return (u > 0).astype(u.dtype)

        def _spike_fwd(u):
            return (spike_fn(u), u)

        def _spike_bwd(u, g):
            s = jnp.pi / 2.0 * ALPHA * u
            return (g * (ALPHA / 2.0) / (1.0 + s * s),)
        spike_fn.defvjp(_spike_fwd, _spike_bwd)
        key = jax.random.key(seed)
        k1, k2, k3 = jax.random.split(key, 3)
        n_embd = 256
        x = jax.random.normal(k1, (4, 512, n_embd), dtype=jnp.float32)
        W_fc = jax.random.normal(k2, (4 * n_embd, n_embd), dtype=jnp.float32) / math.sqrt(n_embd)
        W_proj = jax.random.normal(k3, (n_embd, 4 * n_embd), dtype=jnp.float32) / math.sqrt(4 * n_embd)
        return {'x': x, 'W_fc': W_fc, 'W_proj': W_proj}
    _L3_ffn_in = _L3_ffn_setup()
    _d = {'L0_attn_hidden_states': _L0_attn_in['hidden_states'], 'L0_attn_Wq': _L0_attn_in['Wq'], 'L0_attn_bq': _L0_attn_in['bq'], 'L0_attn_Wk': _L0_attn_in['Wk'], 'L0_attn_bk': _L0_attn_in['bk'], 'L0_attn_Wv': _L0_attn_in['Wv'], 'L0_attn_bv': _L0_attn_in['bv'], 'L0_attn_Wo': _L0_attn_in['Wo'], 'L0_attn_bo': _L0_attn_in['bo'], 'L0_ffn_W1': _L0_ffn_in['W1'], 'L0_ffn_b1': _L0_ffn_in['b1'], 'L0_ffn_W2': _L0_ffn_in['W2'], 'L0_ffn_b2': _L0_ffn_in['b2'], 'L1_attn_W_in': _L1_attn_in['W_in'], 'L1_attn_conv_w': _L1_attn_in['conv_w'], 'L1_attn_conv_b': _L1_attn_in['conv_b'], 'L1_attn_A_log': _L1_attn_in['A_log'], 'L1_attn_D': _L1_attn_in['D'], 'L1_attn_dt_bias': _L1_attn_in['dt_bias'], 'L1_attn_W_out': _L1_attn_in['W_out'], 'L1_ffn_W_r': _L1_ffn_in['W_r'], 'L1_ffn_W_k': _L1_ffn_in['W_k'], 'L1_ffn_W_v': _L1_ffn_in['W_v'], 'L1_ffn_mu_r': _L1_ffn_in['mu_r'], 'L1_ffn_mu_k': _L1_ffn_in['mu_k'], 'L2_attn_Wq': _L2_attn_in['Wq'], 'L2_attn_Wk': _L2_attn_in['Wk'], 'L2_attn_Wv': _L2_attn_in['Wv'], 'L2_attn_Wo': _L2_attn_in['Wo'], 'L2_attn_gamma': _L2_attn_in['gamma'], 'L2_ffn_W_r': _L2_ffn_in['W_r'], 'L2_ffn_W_k': _L2_ffn_in['W_k'], 'L2_ffn_W_v': _L2_ffn_in['W_v'], 'L2_ffn_mu_r': _L2_ffn_in['mu_r'], 'L2_ffn_mu_k': _L2_ffn_in['mu_k'], 'L3_attn_W_Q': _L3_attn_in['W_Q'], 'L3_attn_W_K': _L3_attn_in['W_K'], 'L3_attn_W_V': _L3_attn_in['W_V'], 'L3_attn_W_O': _L3_attn_in['W_O'], 'L3_ffn_W_fc': _L3_ffn_in['W_fc'], 'L3_ffn_W_proj': _L3_ffn_in['W_proj']}
    _x0 = _d['L0_attn_hidden_states']
    _d['L0_attn_hidden_states'] = jax.random.normal(jax.random.fold_in(jax.random.key(seed), 1), (8, 512, 256), dtype=_x0.dtype)
    del _x0
    return _d

def reference(L0_attn_hidden_states, L0_attn_Wq, L0_attn_bq, L0_attn_Wk, L0_attn_bk, L0_attn_Wv, L0_attn_bv, L0_attn_Wo, L0_attn_bo, L0_ffn_W1, L0_ffn_b1, L0_ffn_W2, L0_ffn_b2, L1_attn_W_in, L1_attn_conv_w, L1_attn_conv_b, L1_attn_A_log, L1_attn_D, L1_attn_dt_bias, L1_attn_W_out, L1_ffn_W_r, L1_ffn_W_k, L1_ffn_W_v, L1_ffn_mu_r, L1_ffn_mu_k, L2_attn_Wq, L2_attn_Wk, L2_attn_Wv, L2_attn_Wo, L2_attn_gamma, L2_ffn_W_r, L2_ffn_W_k, L2_ffn_W_v, L2_ffn_mu_r, L2_ffn_mu_k, L3_attn_W_Q, L3_attn_W_K, L3_attn_W_V, L3_attn_W_O, L3_ffn_W_fc, L3_ffn_W_proj):

    def _L0_attn_ref(hidden_states, Wq, bq, Wk, bk, Wv, bv, Wo, bo):
        import jax, jax.numpy as jnp
        import numpy as np
        E = 256
        H = 16
        D = E // H
        WIN = 64
        STRIDE = 128
        G = 1
        B = 2
        L = 4097
        b, seq_len, e = hidden_states.shape
        scale = 1.0 / jnp.sqrt(jnp.asarray(D, hidden_states.dtype))
        q = (hidden_states @ Wq + bq).reshape(b, seq_len, H, D)
        k = (hidden_states @ Wk + bk).reshape(b, seq_len, H, D)
        v = (hidden_states @ Wv + bv).reshape(b, seq_len, H, D)
        qg = q[:, :G]
        gw = jnp.einsum('bghd,bshd->bhgs', qg, k) * scale
        gp = jax.nn.softmax(gw, axis=-1)
        gctx = jnp.einsum('bhgs,bshd->bghd', gp, v).reshape(b, G, e)
        ql, kl, vl = (q[:, G:], k[:, G:], v[:, G:])
        Lc = seq_len - G
        num_windows = max(1, (Lc - WIN) // STRIDE + 1)
        starts = jnp.arange(num_windows) * STRIDE
        widx = starts[:, None] + jnp.arange(WIN)
        qw = ql[:, widx]
        kw = kl[:, widx]
        vw = vl[:, widx]
        aw = jnp.einsum('bwqhd,bwkhd->bwhqk', qw, kw) * scale
        ap = jax.nn.softmax(aw, axis=-1)
        ctx = jnp.einsum('bwhqk,bwkhd->bwqhd', ap, vw)
        ctx = ctx.reshape(b, num_windows * WIN, e)
        flat = widx.reshape(-1)
        local = jnp.zeros((b, Lc, e), hidden_states.dtype).at[:, flat].add(ctx)
        counts = jnp.zeros((Lc,), hidden_states.dtype).at[flat].add(1.0)
        counts = jnp.maximum(counts, 1.0)
        local = local / counts[None, :, None]
        out = jnp.concatenate([gctx, local], axis=1)
        return out @ Wo + bo

    def _L0_ffn_ref(x, W1, b1, W2, b2):
        import jax, jax.numpy as jnp
        import numpy as np
        EMB = 256
        FF = 4 * EMB

        def _ternary(w):
            scale = jnp.maximum(jnp.mean(jnp.abs(w)), 1e-08)
            w_t = jnp.clip(jnp.round(w / scale), -1.0, 1.0)
            return w + jax.lax.stop_gradient(w_t - w)
        h = jnp.einsum('bsd,fd->bsf', x, _ternary(W1)) + b1
        h = jax.nn.gelu(h, approximate=False)
        out = jnp.einsum('bsf,df->bsd', h, _ternary(W2)) + b2
        return out

    def _L1_attn_ref(x, W_in, conv_w, conv_b, A_log, D, dt_bias, W_out):
        import jax, jax.numpy as jnp
        import numpy as np
        import math
        D_MODEL = 256
        D_STATE = 64
        EXPAND = 2
        D_CONV = 4
        D_INNER = D_MODEL * EXPAND
        NHEADS = D_INNER // D_STATE
        HEADDIM = D_INNER // NHEADS
        D_PROJ = 2 * D_INNER + NHEADS * (2 * D_STATE + 1)
        BATCH, SEQLEN = (2, 256)

        def _ssm_forward(x, W_in, conv_w, conv_b, A_log, D, dt_bias, W_out):
            B, L, _ = x.shape
            d, n, s = (D_INNER, NHEADS, D_STATE)
            proj = x @ W_in.T
            x_inner = proj[..., :d]
            z = proj[..., d:2 * d]
            bc_dt = proj[..., 2 * d:].reshape(B, L, n, 2 * s + 1)
            B_proj = bc_dt[..., :s]
            C_proj = bc_dt[..., s:2 * s]
            dt_proj = bc_dt[..., 2 * s]
            xc = jax.lax.conv_general_dilated(jnp.transpose(x_inner, (0, 2, 1)), conv_w, window_strides=(1,), padding=[(D_CONV - 1, 0)], feature_group_count=d, dimension_numbers=('NCH', 'OIH', 'NCH'))
            xc = xc + conv_b[None, :, None]
            x_conv = jax.nn.silu(jnp.transpose(xc, (0, 2, 1)))
            x_heads = x_conv.reshape(B, L, n, HEADDIM)
            A = -jnp.exp(A_log)
            dt = jax.nn.softplus(dt_proj + dt_bias)
            dA = jnp.exp(A[None, None] * dt[..., None])
            dB = B_proj * dt[..., None]

            def step(h, inp):
                dA_t, dB_t, C_t, x_t = inp
                h = dA_t[..., None] * h + dB_t[..., None] * x_t[:, :, None, :]
                y_t = jnp.einsum('bns,bnsd->bnd', C_t, h)
                return (h, y_t)
            h0 = jnp.zeros((B, n, s, HEADDIM), dtype=x.dtype)
            xs = (jnp.moveaxis(dA, 1, 0), jnp.moveaxis(dB, 1, 0), jnp.moveaxis(C_proj, 1, 0), jnp.moveaxis(x_heads, 1, 0))
            _, y_scan = jax.lax.scan(step, h0, xs)
            y_heads = jnp.moveaxis(y_scan, 0, 1)
            y_heads = y_heads + D[None, None, :, None] * x_heads
            y = y_heads.reshape(B, L, d) * jax.nn.silu(z)
            return y @ W_out.T
        return _ssm_forward(x, W_in, conv_w, conv_b, A_log, D, dt_bias, W_out)

    def _L1_ffn_ref(x, W_r, W_k, W_v, mu_r, mu_k):
        import jax, jax.numpy as jnp
        import numpy as np
        DIM = 256

        def _reference_tuple_inner(x, W_r, W_k, W_v, mu_r, mu_k):
            B, T, C = x.shape
            x_prev = jnp.concatenate([jnp.zeros((B, 1, C), x.dtype), x[:, :-1, :]], axis=1)
            xr = mu_r * x + (1.0 - mu_r) * x_prev
            xk = mu_k * x + (1.0 - mu_k) * x_prev
            r = jax.nn.sigmoid(jnp.einsum('btc,dc->btd', xr, W_r))
            k = jnp.einsum('btc,dc->btd', xk, W_k)
            k_act = jnp.square(jax.nn.relu(k))
            out = r * jnp.einsum('btc,dc->btd', k_act, W_v)
            new_state = x[:, -1, :]
            return (out, new_state)
        return _reference_tuple_inner(x, W_r, W_k, W_v, mu_r, mu_k)[0]

    def _L2_attn_ref(q, Wq, Wk, Wv, Wo, gamma):
        import jax, jax.numpy as jnp
        import numpy as np
        import math
        B, S, E, H = (2, 512, 256, 16)
        D = E // H
        SCALE = 1.0 / math.sqrt(D)
        Bq, Sq, _ = q.shape
        qh = (q @ Wq).reshape(Bq, Sq, H, D).transpose(0, 2, 1, 3)
        kh = (q @ Wk).reshape(Bq, Sq, H, D).transpose(0, 2, 1, 3)
        vh = (q @ Wv).reshape(Bq, Sq, H, D).transpose(0, 2, 1, 3)
        q_norm = jnp.sum(qh * qh, axis=-1, keepdims=True)
        k_norm = jnp.sum(kh * kh, axis=-1, keepdims=True)
        qk = jnp.einsum('bhsd,bhtd->bhst', qh, kh)
        dist = jnp.maximum(q_norm - 2.0 * qk + jnp.swapaxes(k_norm, -2, -1), 0.0)
        scores = jnp.exp(-gamma[None, :, None, None] * SCALE * dist)
        mask = jnp.triu(jnp.ones((Sq, Sq), dtype=bool), k=1)
        scores = jnp.where(mask, scores, 0.0)
        out = jnp.einsum('bhst,bhtd->bhsd', scores, vh)
        out = out.transpose(0, 2, 1, 3).reshape(Bq, Sq, H * D)
        return out @ Wo

    def _L2_ffn_ref(x, W_r, W_k, W_v, mu_r, mu_k):
        import jax, jax.numpy as jnp
        import numpy as np
        DIM = 256

        def _reference_tuple_inner(x, W_r, W_k, W_v, mu_r, mu_k):
            B, T, C = x.shape
            x_prev = jnp.concatenate([jnp.zeros((B, 1, C), x.dtype), x[:, :-1, :]], axis=1)
            xr = mu_r * x + (1.0 - mu_r) * x_prev
            xk = mu_k * x + (1.0 - mu_k) * x_prev
            r = jax.nn.sigmoid(jnp.einsum('btc,dc->btd', xr, W_r))
            k = jnp.einsum('btc,dc->btd', xk, W_k)
            k_act = jnp.square(jax.nn.relu(k))
            out = r * jnp.einsum('btc,dc->btd', k_act, W_v)
            new_state = x[:, -1, :]
            return (out, new_state)
        return _reference_tuple_inner(x, W_r, W_k, W_v, mu_r, mu_k)[0]

    def _L3_attn_ref(query, W_Q, W_K, W_V, W_O):
        import jax, jax.numpy as jnp
        import numpy as np
        PI = float(np.pi)
        EPS = 1e-06
        q = jnp.einsum('btd,hdo->btho', query, W_Q)
        k = jnp.einsum('btd,hdo->btho', query, W_K)
        V = jnp.einsum('btd,hde->bthe', query, W_V)
        q = jnp.tanh(q) * (PI / 4)
        k = jnp.tanh(k) * (PI / 4)
        cos_k, sin_k = (jnp.cos(k), jnp.sin(k))
        cos_q, sin_q = (jnp.cos(q), jnp.sin(q))
        cos_KV = jnp.cumsum(cos_k * V, axis=1)
        sin_KV = jnp.cumsum(sin_k * V, axis=1)
        heads = cos_q * cos_KV + sin_q * sin_KV
        cos_K = jnp.cumsum(cos_k, axis=1)
        sin_K = jnp.cumsum(sin_k, axis=1)
        denom = cos_q * cos_K + sin_q * sin_K + EPS
        heads = heads / denom
        return jnp.einsum('deh,bthe->btd', W_O, heads)

    def _L3_ffn_ref(x, W_fc, W_proj):
        import jax, jax.numpy as jnp
        import numpy as np
        import math
        BETA = 0.9
        THRESHOLD = 1.0
        NUM_STEPS = 5
        ALPHA = 2.0

        @jax.custom_vjp
        def spike_fn(u):
            return (u > 0).astype(u.dtype)

        def _spike_fwd(u):
            return (spike_fn(u), u)

        def _spike_bwd(u, g):
            s = jnp.pi / 2.0 * ALPHA * u
            return (g * (ALPHA / 2.0) / (1.0 + s * s),)
        spike_fn.defvjp(_spike_fwd, _spike_bwd)
        h = jnp.square(jax.nn.relu(jnp.einsum('bsd,fd->bsf', x, W_fc)))
        y = jnp.einsum('bsf,df->bsd', h, W_proj)

        def step(mem, _):
            reset = jax.lax.stop_gradient(spike_fn(mem - THRESHOLD))
            mem_new = BETA * mem + y - reset * THRESHOLD
            spk = spike_fn(mem_new - THRESHOLD)
            return (mem_new, spk)
        mem0 = jnp.zeros_like(y)
        _, spks = jax.lax.scan(step, mem0, None, length=NUM_STEPS)
        return jnp.sum(spks, axis=0) / NUM_STEPS
    x = L0_attn_hidden_states
    x = x + _layernorm(_L0_attn_ref(_layernorm(x, axis=-1), L0_attn_Wq, L0_attn_bq, L0_attn_Wk, L0_attn_bk, L0_attn_Wv, L0_attn_bv, L0_attn_Wo, L0_attn_bo), axis=-1)
    x = x + _layernorm(_L0_ffn_ref(_layernorm(x, axis=-1), L0_ffn_W1, L0_ffn_b1, L0_ffn_W2, L0_ffn_b2), axis=-1)
    x = x + _layernorm(_L1_attn_ref(_layernorm(x, axis=-1), L1_attn_W_in, L1_attn_conv_w, L1_attn_conv_b, L1_attn_A_log, L1_attn_D, L1_attn_dt_bias, L1_attn_W_out), axis=-1)
    x = x + _layernorm(_L1_ffn_ref(_layernorm(x, axis=-1), L1_ffn_W_r, L1_ffn_W_k, L1_ffn_W_v, L1_ffn_mu_r, L1_ffn_mu_k), axis=-1)
    x = x + _layernorm(_L2_attn_ref(_layernorm(x, axis=-1), L2_attn_Wq, L2_attn_Wk, L2_attn_Wv, L2_attn_Wo, L2_attn_gamma), axis=-1)
    x = x + _layernorm(_L2_ffn_ref(_layernorm(x, axis=-1), L2_ffn_W_r, L2_ffn_W_k, L2_ffn_W_v, L2_ffn_mu_r, L2_ffn_mu_k), axis=-1)
    x = x + _layernorm(_L3_attn_ref(_layernorm(x, axis=-1), L3_attn_W_Q, L3_attn_W_K, L3_attn_W_V, L3_attn_W_O), axis=-1)
    x = x + _layernorm(_L3_ffn_ref(_layernorm(x, axis=-1), L3_ffn_W_fc, L3_ffn_W_proj), axis=-1)
    return x

_drawn_inputs = setup_inputs


def setup_inputs(seed=0):
    import zlib

    import numpy as np

    out = dict(_drawn_inputs(seed))
    spreads = {'L0_attn_bq': (0.0, 0.8),
     'L0_attn_bk': (0.0, 0.8),
     'L0_attn_bv': (0.0, 0.1),
     'L0_attn_bo': (0.0, 0.1),
     'L1_attn_conv_b': (0.0, 0.1),
     'L1_attn_D': (1.0, 0.2),
     'L2_attn_gamma': (1.0, 0.2)}
    factors = {'L0_attn_Wq': 4.438, 'L0_attn_Wk': 4.202, 'L0_ffn_b1': 8.0, 'L0_ffn_b2': 8.0}
    for name, (base, spread) in spreads.items():
        noise = np.random.default_rng([zlib.crc32(name.encode()), seed]).standard_normal(out[name].shape)
        drawn = base * np.exp(spread * noise) if base else spread * noise
        out[name] = jnp.asarray(drawn.astype(out[name].dtype))
    for name, factor in factors.items():
        out[name] = (out[name] * factor).astype(out[name].dtype)
    return out
```

```python
from contextlib import ExitStack

import concourse.bass as bass
from concourse import mybir

F32 = mybir.dt.float32
U8 = mybir.dt.uint8
ALU = mybir.AluOpType
ACT = mybir.ActivationFunctionType
AX = mybir.AxisListType

P = 128
NB = 8
T = 512
E = 256
TT = T // P
EC = E // P
EPS = 1e-5


class Common:

    def __init__(self, nc, ctx, sems):
        self.nc, self.ctx, self.sems = nc, ctx, sems

    def sb(self, name, shape, dt=F32):
        return self.ctx.enter_context(self.nc.sbuf_tensor(name, shape, dt))

    def ps(self, name, shape=(P, 512)):
        return self.ctx.enter_context(self.nc.psum_tensor(name, list(shape), F32))

    def sem(self, name):
        return self.sems.new(self.nc, name)


class Semaphores:

    def __init__(self):
        self.stack, self.all = ExitStack(), []

    def new(self, nc, name):
        self.all.append(self.stack.enter_context(nc.semaphore(name)))
        return self.all[-1]


def wait_apart(g, eng, sem, value):
    if not isinstance(value, int):
        eng.compute_val(value)
    eng.wait_ge(g.const_ready, 1)
    eng.wait_ge(sem, value)


def each_batch(eng, body):
    with eng.Fori(0, NB - 1) as i:
        body(i, True)
    body(NB - 1, False)


class NormIn:

    def __init__(self, g, s, tag):
        self.g, self.nc = g, g.nc
        self.st = s.sb(tag + "in_st", [P, TT, 6])
        self.mv = s.sb(tag + "in_mv", [P, TT, 2])
        self.ve = s.sb(tag + "in_ve", [P, TT])
        self.rs = s.sb(tag + "in_rs", [P, TT])
        self.xn = s.sb(tag + "xn", [P, TT, E])
        self.xnT = s.sb(tag + "xnT", [P, EC, T + 1])
        self.psT = [s.ps(tag + f"psT{c}") for c in range(EC)]
        self.stats = s.sem(tag + "in_stats")
        self.moments = s.sem(tag + "in_moments")
        self.var = s.sem(tag + "in_var")
        self.rstd = s.sem(tag + "in_rstd")
        self.xn_ready = s.sem(tag + "xn_ready")
        self.turned = s.sem(tag + "turned")
        self.ready = s.sem(tag + "xnT_ready")

    def x_tile(self, n, t):
        return self.g.x[:, bass.ds(n * TT + t, 1), :]

    def vector(self, eng, n, first=False):
        ve = self.nc.vector
        for t in range(TT):
            ve.bn_stats(self.st[:, t, :], self.x_tile(n, t)).then_inc(self.stats, 1)
        for t in range(TT):
            wait_apart(self.g, eng, self.stats, n * TT + t + 1)
            ve.bn_aggr(self.mv[:, t, :], self.st[:, t, :]).then_inc(self.moments, 1)
        eng.wait_ge(self.moments, n * TT + TT)
        ve.tensor_scalar_add(self.ve[:, :], self.mv[:, :, 1], EPS).then_inc(self.var, 1)
        eng.wait_ge(self.rstd, n + 1)
        if not first:
            eng.wait_ge(self.turned, n)
        for t in range(TT):
            ve.tensor_scalar(self.xn[:, t:t + 1, :], self.x_tile(n, t), self.mv[:, t, 0:1], self.rs[:, t:t + 1],
                             ALU.subtract, ALU.mult).then_inc(self.xn_ready, 1)

    def gpsimd(self, eng, n):
        eng.wait_ge(self.var, n + 1)
        self.nc.gpsimd.tensor_tensor(self.rs[:, :], self.ve[:, :], self.g.minus_half[:, 0:TT],
                                     ALU.pow).then_inc(self.rstd, 1)

    def tensor(self, eng, n):
        for t in range(TT):
            eng.wait_ge(self.xn_ready, n * TT + t + 1)
            for c in range(EC):
                last = self.nc.tensor.transpose(self.psT[c][:, t * P:(t + 1) * P],
                                                self.xn[:, t, c * P:(c + 1) * P], self.g.ident[:, :])
        last.then_inc(self.turned, 1)

    def scalar(self, eng, n):
        eng.wait_ge(self.turned, n + 1)
        for c in range(EC):
            self.nc.scalar.copy(self.xnT[:, c, 1:T + 1], self.psT[c][:, :]).then_inc(self.ready, 1)


class NormOut:

    def __init__(self, g, s, tag):
        self.g, self.nc = g, g.nc
        self.st = s.sb(tag + "out_st", [P, TT, 6])
        self.mv = s.sb(tag + "out_mv", [P, TT, 2])
        self.ve = s.sb(tag + "out_ve", [P, TT])
        self.rs = s.sb(tag + "out_rs", [P, TT])
        self.y = s.sb(tag + "out_y", [P, TT, E])
        self.stats = s.sem(tag + "out_stats")
        self.moments = s.sem(tag + "out_moments")
        self.var = s.sem(tag + "out_var")
        self.rstd = s.sem(tag + "out_rstd")
        self.normed = s.sem(tag + "normed")
        self.added = s.sem(tag + "added")

    def vector(self, eng, i, source, ready, per):
        ve = self.nc.vector
        for t in range(TT):
            if per:
                eng.wait_ge(ready, i * per + t * per // TT + 1)
            ve.bn_stats(self.st[:, t, :], source(t)).then_inc(self.stats, 1)
        for t in range(TT):
            wait_apart(self.g, eng, self.stats, i * TT + t + 1)
            ve.bn_aggr(self.mv[:, t, :], self.st[:, t, :]).then_inc(self.moments, 1)
        eng.wait_ge(self.moments, i * TT + TT)
        ve.tensor_scalar_add(self.ve[:, :], self.mv[:, :, 1], EPS).then_inc(self.var, 1)
        eng.wait_ge(self.rstd, i + 1)
        for t in range(TT):
            ve.tensor_scalar(self.y[:, t, :], source(t), self.mv[:, t, 0:1], self.rs[:, t:t + 1],
                             ALU.subtract, ALU.mult).then_inc(self.normed, 1)

    def gpsimd(self, eng, i):
        eng.wait_ge(self.var, i + 1)
        self.nc.gpsimd.tensor_tensor(self.rs[:, :], self.ve[:, :], self.g.minus_half[:, 0:TT],
                                     ALU.pow).then_inc(self.rstd, 1)
        for t in range(TT):
            eng.wait_ge(self.normed, i * TT + t + 1)
            xt = self.g.x[:, bass.ds(i * TT + t, 1), :]
            self.nc.gpsimd.tensor_tensor(xt, xt, self.y[:, t:t + 1, :], ALU.add).then_inc(self.added, 1)

    def tail(self, eng, i):
        eng.wait_ge(self.added, i * TT + TT)


H0 = 16
D0 = E // H0
WIN = 64
NW = 4
WPAIRS = NW // 2
SCALE0 = float(D0) ** -0.5


def windowed_attention(nc, g, tag, w):
    with ExitStack() as ctx:
        s = Common(nc, ctx, g.sems)
        a, z = NormIn(g, s, tag), NormOut(g, s, tag)
        xnT, psA = a.xnT, a.psT
        qT = s.sb(tag + "qT", [P, EC, NW, WIN + 1])
        kT = s.sb(tag + "kT", [P, EC, T])
        v_win = s.sb(tag + "v_win", [P, NW, E])
        keys = s.sb(tag + "keys", [P, 2, 2, 8 * WIN])
        sc = s.sb(tag + "sc", [P, 2, 8 * WIN])
        mx = s.sb(tag + "mx", [P, 4, 8])
        sums = s.sb(tag + "sums", [P, 4, 8])
        rinv = s.sb(tag + "rinv", [P, 4, 8])
        prT = s.sb(tag + "prT", [P, 2, 4 * P])
        ctxs = s.sb(tag + "ctxs", [P, WPAIRS, E])
        ctxT = s.sb(tag + "ctxT", [P, EC, T])
        o = s.sb(tag + "o", [P, TT, E])
        q0 = s.sb(tag + "q0", [P, EC, H0])
        gmx = s.sb(tag + "gmx", [H0, 1])
        gneg = s.sb(tag + "gneg", [H0, 1])
        gsum = s.sb(tag + "gsum", [H0, 1])
        ginv = s.sb(tag + "ginv", [H0, 1])
        gexp = s.sb(tag + "gexp", [H0, T])
        gpr = s.sb(tag + "gpr", [H0, T])
        gprT = s.sb(tag + "gprT", [P, TT, H0])
        gx = s.sb(tag + "gx", [P, EC, H0])
        gdiag = s.sb(tag + "gdiag", [P, EC, H0])
        gctx = s.sb(tag + "gctx", [P, EC])
        psS = [s.ps(tag + f"psS{j}") for j in range(2)]
        psP = [s.ps(tag + f"psP{j}") for j in range(2)]
        psX = [s.ps(tag + f"psX{j}") for j in range(2)]
        const = s.sem(tag + "const")
        proj_psum = s.sem(tag + "proj_psum")
        proj_ready = s.sem(tag + "proj_ready")
        q0_ready = s.sem(tag + "q0_ready")
        g_psum = s.sem(tag + "g_psum")
        g_max = s.sem(tag + "g_max")
        g_exp = s.sem(tag + "g_exp")
        g_norm = s.sem(tag + "g_norm")
        gT_psum = s.sem(tag + "gT_psum")
        gT_ready = s.sem(tag + "gT_ready")
        gx_psum = s.sem(tag + "gx_psum")
        gx_ready = s.sem(tag + "gx_ready")
        gc_psum = s.sem(tag + "gc_psum")
        gc_steps = s.sem(tag + "gc_steps")
        keys_ready = s.sem(tag + "keys_ready")
        s_psum = s.sem(tag + "s_psum")
        max_ready = s.sem(tag + "max_ready")
        sub_ready = s.sem(tag + "sub_ready")
        exp_ready = s.sem(tag + "exp_ready")
        sum_ready = s.sem(tag + "sum_ready")
        prT_psum = s.sem(tag + "prT_psum")
        prT_ready = s.sem(tag + "prT_ready")
        x_psum = s.sem(tag + "x_psum")
        inv_ready = s.sem(tag + "inv_ready")
        ctx_ready = s.sem(tag + "ctx_ready")
        ctxT_psum = s.sem(tag + "ctxT_psum")
        ctxT_ready = s.sem(tag + "ctxT_ready")
        o_psum = s.sem(tag + "o_psum")
        o_ready = s.sem(tag + "o_ready")
        block = ctx.enter_context(nc.Block())

        def heads(v):
            return v.rearrange("p (h n) -> p h n", h=8)

        def spread(v, n):
            return v.unsqueeze(2).to_broadcast([P, 8, n])

        @block.vector
        def _(eng):
            ve = nc.vector

            def subtract_max(i, n):
                eng.wait_ge(s_psum, i * 4 + n + 1)
                ve.tensor_reduce(mx[:, n, :], heads(psS[n % 2][:, :]), AX.X, ALU.max).then_inc(max_ready, 1)
                eng.wait_ge(max_ready, i * 4 + n + 1)
                if n >= 2:
                    eng.wait_ge(prT_psum, i * 4 + n - 1)
                    eng.wait_ge(sum_ready, i * 4 + n - 1)
                ve.tensor_tensor(heads(sc[:, n % 2, :]), heads(psS[n % 2][:, :]), spread(mx[:, n, :], WIN),
                                 ALU.subtract).then_inc(sub_ready, 1)

            def row_sums(i, n):
                eng.wait_ge(exp_ready, i * 4 + n + 1)
                ve.tensor_reduce(sums[:, n, :], heads(sc[:, n % 2, :]), AX.X, ALU.add).then_inc(sum_ready, 1)

            def body(i, more):
                for c in range(EC):
                    eng.wait_ge(proj_ready, i * 6 + c + 1)
                    ve.tensor_scalar(q0[:, c, :], w["head16"][:, c * H0:(c + 1) * H0], qT[:, c, 0, 0:1], None,
                                     ALU.mult).then_inc(q0_ready, 1)
                eng.wait_ge(g_psum, i + 1)
                ve.tensor_reduce(gmx[:, :], psA[0][0:H0, :], AX.X, ALU.max).then_inc(g_max, 1)
                eng.wait_ge(g_max, i * 2 + 1)
                ve.tensor_scalar(gneg[:, :], gmx[:, :], -SCALE0, None, ALU.mult).then_inc(g_max, 1)
                subtract_max(i, 0)
                subtract_max(i, 1)
                eng.wait_ge(g_exp, i + 1)
                ve.reciprocal(ginv[:, :], gsum[:, :]).then_inc(g_norm, 1)
                eng.wait_ge(g_norm, i * 2 + 1)
                ve.tensor_scalar(gpr[:, :], gexp[:, :], ginv[:, 0:1], None, ALU.mult).then_inc(g_norm, 1)
                row_sums(i, 0)
                subtract_max(i, 2)
                row_sums(i, 1)
                if more:
                    eng.wait_ge(gx_psum, i + 1)
                    a.vector(eng, i + 1)
                subtract_max(i, 3)
                row_sums(i, 2)
                eng.wait_ge(gc_psum, i + 1)
                ve.tensor_tensor(gdiag[:, :, :], psA[1][:, 0:EC * H0].rearrange("p (c h) -> p c h", c=EC),
                                 w["head16"][:, :].rearrange("p (c h) -> p c h", c=EC), ALU.mult).then_inc(gc_steps, 1)
                eng.wait_ge(gc_steps, i * 3 + 1)
                ve.tensor_reduce(gctx[:, :], gdiag[:, :, :], AX.X, ALU.add).then_inc(gc_steps, 1)
                eng.wait_ge(gc_steps, i * 3 + 2)
                ve.tensor_tensor(ctxT[:, :, 0:1], gctx[:, :].unsqueeze(2), w["bv"][:, :].unsqueeze(2),
                                 ALU.add).then_inc(gc_steps, 1)
                row_sums(i, 3)
                eng.wait_ge(sum_ready, i * 4 + 4)
                ve.reciprocal(rinv[:, :, :], sums[:, :, :]).then_inc(inv_ready, 1)
                eng.wait_ge(inv_ready, i + 1)
                eng.wait_ge(x_psum, i + 1)
                for b in range(2):
                    out = ctxs[:, :, :].rearrange("p a (m b d) -> p a m b d", b=2, d=D0)[:, :, :, b, :]
                    inv = rinv[:, :, :].rearrange("p (a c) (m b) -> p a c m b", a=2, b=2)[:, :, :, :, b]
                    for wp in range(WPAIRS):
                        ins = ve.tensor_tensor(
                            out[:, wp, :, :].rearrange("p (c m) d -> p c m d", c=EC),
                            psX[b][:, wp * P:(wp + 1) * P].rearrange("p (c m d) -> p c m d", c=EC, d=D0),
                            inv[:, wp, :, :].unsqueeze(3).to_broadcast([P, EC, 4, D0]), ALU.mult)
                    ins.then_inc(ctx_ready, 1)
                for j in range(2):
                    eng.wait_ge(o_psum, i * 2 + j + 1)
                    ve.tensor_tensor(o[:, 2 * j:2 * j + 2, :], psA[j][:, :], w["bo"][:, :], ALU.add).then_inc(o_ready, 1)
                eng.wait_ge(o_ready, i * 2 + 2)
                z.vector(eng, i, lambda t: o[:, t, :], o_psum, 2)
                z.tail(eng, i)

            ve.memset(ctxT[:, :, :], 0.0).then_inc(const, 1)
            ve.memset(xnT[:, :, 0:1], 0.0).then_inc(const, 1)
            eng.wait_ge(const, 2)
            eng.wait_ge(g.weights[w["sem"]], w["count"])
            a.vector(eng, 0, first=True)
            each_batch(eng, body)

        @block.sync
        def _(eng):
            g.look_ahead(eng)

        @block.gpsimd
        def _(eng):
            def body(i, more):
                for n in range(4):
                    wp, c = divmod(n, 2)
                    eng.wait_ge(proj_ready, i * 6 + 3 + c)
                    if n >= 2:
                        eng.wait_ge(s_psum, i * 4 + n - 1)
                    for k in range(2):
                        at = (2 * wp + k) * P + 1
                        kw = kT[:, c, at:at + WIN].unsqueeze(1).to_broadcast([P, 8, WIN])
                        nc.gpsimd.tensor_tensor(heads(keys[:, n % 2, k, :]), kw, spread(w["head8"][:, :], WIN),
                                                ALU.mult).then_inc(keys_ready, 1)
                if more:
                    a.gpsimd(eng, i + 1)
                z.gpsimd(eng, i)
            eng.wait_ge(g.weights[w["sem"]], w["count"])
            a.gpsimd(eng, 0)
            each_batch(eng, body)

        @block.scalar
        def _(eng):
            sc_e = nc.scalar

            def exponent(i, n):
                eng.wait_ge(sub_ready, i * 4 + n + 1)
                sc_e.activation(sc[:, n % 2, :], sc[:, n % 2, :], ACT.Exp, scale=SCALE0).then_inc(exp_ready, 1)

            def turned(i, n):
                eng.wait_ge(prT_psum, i * 4 + n + 1)
                sc_e.copy(prT[:, n % 2, :], psP[n % 2][:, :]).then_inc(prT_ready, 1)

            def body(i, more):
                for c in range(EC):
                    eng.wait_ge(proj_psum, i * 6 + c + 1)
                    sc_e.activation(qT[:, c, :, :].rearrange("p w n -> p (w n)"), psA[c][:, 0:NW * (WIN + 1)],
                                    ACT.Identity, bias=w["bq"][:, c:c + 1]).then_inc(proj_ready, 1)
                for c in range(EC):
                    eng.wait_ge(proj_psum, i * 6 + c + 3)
                    sc_e.activation(kT[:, c, :], psA[c][:, :], ACT.Identity,
                                    bias=w["bk"][:, c:c + 1]).then_inc(proj_ready, 1)
                for j in range(2):
                    eng.wait_ge(proj_psum, i * 6 + j + 5)
                    sc_e.copy(v_win[:, 2 * j:2 * j + 2, :], psA[j][:, :]).then_inc(proj_ready, 1)
                eng.wait_ge(g_max, i * 2 + 2)
                sc_e.activation(gexp[:, :], psA[0][0:H0, :], ACT.Exp, scale=SCALE0, bias=gneg[:, 0:1],
                                accum_out=gsum[:, 0:1]).then_inc(g_exp, 1)
                exponent(i, 0)
                exponent(i, 1)
                eng.wait_ge(gT_psum, i + 1)
                sc_e.copy(gprT[:, :, :], psA[1][:, 0:TT * H0]).then_inc(gT_ready, 1)
                turned(i, 0)
                exponent(i, 2)
                eng.wait_ge(gx_psum, i + 1)
                sc_e.copy(gx[:, :, :], psA[0][:, 0:EC * H0]).then_inc(gx_ready, 1)
                turned(i, 1)
                exponent(i, 3)
                turned(i, 2)
                turned(i, 3)
                eng.wait_ge(ctxT_psum, i + 1)
                for c in range(EC):
                    sc_e.activation(ctxT[:, c, :].rearrange("p (w n) -> p w n", w=NW)[:, :, 1:1 + WIN],
                                    psA[0][:, c * 256:(c + 1) * 256].rearrange("p (w n) -> p w n", w=NW),
                                    ACT.Identity, bias=w["bv"][:, c:c + 1]).then_inc(ctxT_ready, 1)
                if more:
                    a.scalar(eng, i + 1)
            eng.wait_ge(const, 2)
            eng.wait_ge(g.weights[w["sem"]], w["count"])
            a.scalar(eng, 0)
            each_batch(eng, body)

        @block.tensor
        def _(eng):
            eng.wait_ge(g.weights[w["sem"]], w["count"])
            te = nc.tensor

            def projections(i):
                eng.wait_ge(a.ready, i * EC + EC)
                for f in range(EC):
                    for c in range(EC):
                        mm = te.matmul(psA[f][:, 0:NW * (WIN + 1)], w["Wq"][:, c, f * P:(f + 1) * P],
                                       xnT[:, c, 1:T + 1].rearrange("p (w n) -> p w n", w=NW)[:, :, 0:WIN + 1],
                                       start=c == 0, stop=c == EC - 1)
                    mm.then_inc(proj_psum, 1)
                for f in range(EC):
                    eng.wait_ge(proj_ready, i * 6 + f + 1)
                    for c in range(EC):
                        mm = te.matmul(psA[f][:, :], w["Wk"][:, c, f * P:(f + 1) * P], xnT[:, c, 1:T + 1],
                                       start=c == 0, stop=c == EC - 1)
                    mm.then_inc(proj_psum, 1)
                for j in range(2):
                    eng.wait_ge(proj_ready, i * 6 + j + 3)
                    for k in range(2):
                        at = (2 * j + k) * P + 2
                        for c in range(EC):
                            for b in range(2):
                                mm = te.matmul(psA[j][b * WIN:(b + 1) * WIN, k * E:(k + 1) * E],
                                               xnT[:, c, at:at + WIN], w["Wv"][:, c, :],
                                               start=c == 0, stop=c == EC - 1, skip_group_check=True)
                    mm.then_inc(proj_psum, 1)

            def scores(i, n):
                wp, c = divmod(n, 2)
                eng.wait_ge(keys_ready, i * 8 + 2 * n + 2)
                for k in range(2):
                    mm = te.matmul(psS[n % 2][k * WIN:(k + 1) * WIN, :], qT[:, c, 2 * wp + k, 1:WIN + 1],
                                   keys[:, n % 2, k, :], start=True, stop=True, skip_group_check=True)
                mm.then_inc(s_psum, 1)

            def turn(i, n):
                eng.wait_ge(exp_ready, i * 4 + n + 1)
                for m in range(4):
                    mm = te.transpose(psP[n % 2][:, m * P:(m + 1) * P], sc[:, n % 2, m * P:(m + 1) * P],
                                      g.ident[:, :])
                mm.then_inc(prT_psum, 1)

            def context(i, n):
                wp, c = divmod(n, 2)
                wait_apart(g, eng, prT_ready, i * 4 + n + 1)
                for m in range(4):
                    for b in range(2):
                        for k in range(2):
                            h = 8 * c + 2 * m + b
                            at = wp * P + (4 * c + m) * D0
                            mm = te.matmul(psX[b][k * WIN:(k + 1) * WIN, at:at + D0],
                                           prT[b * WIN:(b + 1) * WIN, n % 2, m * P + k * WIN:m * P + (k + 1) * WIN],
                                           v_win[b * WIN:(b + 1) * WIN, 2 * wp + k, h * D0:(h + 1) * D0],
                                           start=True, stop=True, skip_group_check=True)
                return mm

            def body(i, more):
                projections(i)
                eng.wait_ge(q0_ready, i * 2 + 2)
                eng.wait_ge(proj_ready, i * 6 + 5)
                for c in range(EC):
                    mm = te.matmul(psA[0][0:H0, :], q0[:, c, :], kT[:, c, :], start=c == 0, stop=c == EC - 1)
                mm.then_inc(g_psum, 1)
                scores(i, 0)
                scores(i, 1)
                eng.wait_ge(g_norm, i * 2 + 2)
                eng.wait_ge(proj_ready, i * 6 + 6)
                for t in range(TT):
                    mm = te.matmul(psA[1][:, t * H0:(t + 1) * H0], gpr[:, t * P:(t + 1) * P], g.ident[0:H0, 0:H0],
                                   start=True, stop=True)
                mm.then_inc(gT_psum, 1)
                turn(i, 0)
                scores(i, 2)
                eng.wait_ge(gT_ready, i + 1)
                for c in range(EC):
                    for t in range(TT):
                        mm = te.matmul(psA[0][:, c * H0:(c + 1) * H0], a.xn[:, t, c * P:(c + 1) * P], gprT[:, t, :],
                                       start=t == 0, stop=t == TT - 1)
                mm.then_inc(gx_psum, 1)
                context(i, 0)
                turn(i, 1)
                scores(i, 3)
                eng.wait_ge(gx_ready, i + 1)
                for f in range(EC):
                    for c in range(EC):
                        mm = te.matmul(psA[1][:, f * H0:(f + 1) * H0], w["Wv"][:, c, f * P:(f + 1) * P], gx[:, c, :],
                                       start=c == 0, stop=c == EC - 1)
                mm.then_inc(gc_psum, 1)
                context(i, 1)
                turn(i, 2)
                context(i, 2)
                turn(i, 3)
                context(i, 3).then_inc(x_psum, 1)
                eng.wait_ge(ctx_ready, i * 2 + 2)
                for c in range(EC):
                    for wp in range(WPAIRS):
                        mm = te.transpose(psA[0][:, c * 256 + wp * P:c * 256 + (wp + 1) * P],
                                          ctxs[:, wp, c * P:(c + 1) * P], g.ident[:, :])
                mm.then_inc(ctxT_psum, 1)
                eng.wait_ge(ctxT_ready, i * 2 + 2)
                eng.wait_ge(gc_steps, i * 3 + 3)
                if more:
                    a.tensor(eng, i + 1)
                    eng.wait_ge(a.ready, i * EC + 2 * EC)
                for t in range(TT):
                    for c in range(EC):
                        mm = te.matmul(psA[t // 2][:, (t % 2) * E:(t % 2 + 1) * E], ctxT[:, c, t * P:(t + 1) * P],
                                       w["Wo"][:, c, :], start=c == 0, stop=c == EC - 1)
                    if t % 2:
                        mm.then_inc(o_psum, 1)
                eng.wait_ge(o_ready, i * 2 + 2)
            a.tensor(eng, 0)
            each_batch(eng, body)


FF = 4 * E
FT = FF // P


def mlp(nc, g, tag, w, spiking):
    with ExitStack() as ctx:
        s = Common(nc, ctx, g.sems)
        a, z = NormIn(g, s, tag), NormOut(g, s, tag)
        xnT = a.xnT
        HB = 4
        AHEAD = 2
        h = s.sb(tag + "h", [P, FT, T])
        o = s.sb(tag + "o", [P, TT, E])
        psH = [s.ps(tag + f"psH{j}") for j in range(HB)]
        psO = [s.ps(tag + f"psO{j}") for j in range(TT // 2)]
        h_psum = s.sem(tag + "h_psum")
        h_ready = s.sem(tag + "h_ready")
        relu_ready = s.sem(tag + "relu_ready")
        o_psum = s.sem(tag + "o_psum")
        o_taken = s.sem(tag + "o_taken")
        out_ready = s.sem(tag + "out_ready")
        w_ready = s.sem(tag + "w_ready")
        W1, W2 = w["W1"], w["W2"]
        if spiking:
            mem = s.sb(tag + "mem", [P, TT * E])
            drive = s.sb(tag + "drive", [P, TT * E])
            spikes = s.sb(tag + "spikes", [P, TT * E])
            h_relu = s.sb(tag + "h_relu", [P, 2, T])
            neuron = s.sem(tag + "neuron")
        else:
            absw = s.sb(tag + "absw", [P, EC * FF])
            abs_sum = s.sb(tag + "abs_sum", [P, 2])
            ones = s.sb(tag + "ones", [P, P])
            half = s.sb(tag + "half", [P, 2])
            minus_half = s.sb(tag + "neg_half", [P, 2])
            tern = [s.sb(tag + f"tern{m}", [P, EC * FF]) for m in range(2)]
            below = s.sb(tag + "below", [P, EC * FF])
            raw = [W1[:, :, :].rearrange("p c n -> p (c n)"), W2[:, :, :].rearrange("p c n -> p (c n)")]
            W1 = tern[0][:, :].rearrange("p (c n) -> p c n", c=EC)
            W2 = tern[1][:, :].rearrange("p (c n) -> p c n", c=FT)
            ones_ready = s.sem(tag + "ones_ready")
            abs_ready = s.sem(tag + "abs_ready")
            sum_ready = s.sem(tag + "sum_ready")
            limit = s.sem(tag + "limit")
        NEURON_OPS = 13
        block = ctx.enter_context(nc.Block())

        def half_bank(t):
            return psO[t // 2][:, (t % 2) * E:(t % 2 + 1) * E]

        @block.vector
        def _(eng):
            ve = nc.vector

            def make_ternary():
                ve.memset(ones[:, :], 1.0).then_inc(ones_ready, 1)
                eng.wait_ge(sum_ready, 1)
                ve.tensor_scalar(half[:, :], psH[0][:, 0:2], 1.0 / (E * FF), 1e-8, ALU.mult,
                                 ALU.max).then_inc(limit, 1)
                eng.wait_ge(limit, 1)
                ve.tensor_scalar(minus_half[:, :], half[:, :], -0.5, None, ALU.mult).then_inc(limit, 1)
                eng.wait_ge(limit, 2)
                ve.tensor_scalar(half[:, :], minus_half[:, :], -1.0, None, ALU.mult).then_inc(limit, 1)
                eng.wait_ge(limit, 3)
                for m in range(2):
                    if m:
                        eng.wait_ge(w_ready, 1)
                    ve.tensor_scalar(below[:, :], raw[m], minus_half[:, m:m + 1], None,
                                     ALU.is_lt).then_inc(limit, 1)
                    eng.wait_ge(limit, 4 + m)
                    ve.scalar_tensor_tensor(tern[m][:, :], raw[m], half[:, m:m + 1], below[:, :],
                                            ALU.is_gt, ALU.subtract).then_inc(w_ready, 1)

            def leak_and_fire(i):
                at = [0]

                def chained(ins):
                    at[0] += 1
                    ins.then_inc(neuron, 1)

                def settle():
                    eng.wait_ge(neuron, i * NEURON_OPS + at[0])
                eng.wait_ge(o_taken, i * 2 + 4)
                chained(ve.tensor_scalar(spikes[:, :], drive[:, :], 1.0, None, ALU.is_gt))
                chained(ve.scalar_tensor_tensor(mem[:, :], drive[:, :], 0.9, drive[:, :], ALU.mult, ALU.add))
                settle()
                chained(ve.tensor_tensor(mem[:, :], spikes[:, :], mem[:, :], ALU.subtract))
                settle()
                chained(ve.scalar_tensor_tensor(spikes[:, :], mem[:, :], -1.0, spikes[:, :], ALU.is_lt, ALU.add))
                for _ in range(3):
                    chained(ve.scalar_tensor_tensor(o[:, :, :], mem[:, :], 0.9, drive[:, :], ALU.mult,
                                                    ALU.subtract))
                    settle()
                    chained(ve.scalar_tensor_tensor(mem[:, :], mem[:, :], -1.0, o[:, :, :], ALU.is_lt, ALU.add))
                    settle()
                    chained(ve.scalar_tensor_tensor(spikes[:, :], mem[:, :], -1.0, spikes[:, :], ALU.is_lt,
                                                    ALU.add))
                settle()
                assert at[0] == NEURON_OPS
                ve.tensor_scalar(o[:, :, :], spikes[:, :], 0.2, None, ALU.mult).then_inc(out_ready, 1)

            def body(i, more):
                if more:
                    a.vector(eng, i + 1)
                eng.wait_ge(o_psum, i + 1)
                for j in range(2):
                    if spiking:
                        ve.tensor_copy(drive[:, j * 512:(j + 1) * 512], psO[j][:, :]).then_inc(o_taken, 1)
                    else:
                        ve.tensor_tensor(o[:, 2 * j:2 * j + 2, :], psO[j][:, :],
                                         w["b2"][:, :], ALU.add).then_inc(o_taken, 1)
                if spiking:
                    leak_and_fire(i)
                    z.vector(eng, i, lambda t: o[:, t, :], out_ready, 1)
                else:
                    eng.wait_ge(o_taken, i * 2 + 4)
                    z.vector(eng, i, lambda t: o[:, t, :], o_psum, 1)
                z.tail(eng, i)

            ve.memset(xnT[:, :, 0:1], 0.0).then_inc(o_taken, 2)
            eng.wait_ge(g.weights[w["sem"]], w["count"])
            if not spiking:
                make_ternary()
            a.vector(eng, 0, first=True)
            each_batch(eng, body)

        @block.sync
        def _(eng):
            g.look_ahead(eng)

        @block.gpsimd
        def _(eng):
            def body(i, more):
                if more:
                    a.gpsimd(eng, i + 1)
                z.gpsimd(eng, i)
            a.gpsimd(eng, 0)
            each_batch(eng, body)

        @block.scalar
        def _(eng):
            def body(i, more):
                for f in range(FT):
                    eng.wait_ge(h_psum, i * FT + f + 1)
                    if spiking:
                        nc.scalar.activation(h_relu[:, f % 2, :], psH[f % HB][:, :], ACT.Relu).then_inc(relu_ready, 1)
                        eng.wait_ge(relu_ready, i * FT + f + 1)
                        nc.scalar.activation(h[:, f, :], h_relu[:, f % 2, :], ACT.Square).then_inc(h_ready, 1)
                    else:
                        nc.scalar.activation(h[:, f, :], psH[f % HB][:, :], ACT.Gelu,
                                             bias=w["b1"][:, f:f + 1]).then_inc(h_ready, 1)
                if more:
                    a.scalar(eng, i + 1)
            eng.wait_ge(g.weights[w["sem"]], w["count"])
            if not spiking:
                for m in range(2):
                    if m:
                        eng.wait_ge(abs_ready, 1)
                    nc.scalar.activation(absw[:, :], raw[m], ACT.Abs,
                                         accum_out=abs_sum[:, m:m + 1]).then_inc(abs_ready, 1)
            a.scalar(eng, 0)
            each_batch(eng, body)

        @block.tensor
        def _(eng):
            eng.wait_ge(g.weights[w["sem"]], w["count"])

            def first_product(i, f):
                for c in range(EC):
                    mm = nc.tensor.matmul(psH[f % HB][:, :], W1[:, c, f * P:(f + 1) * P], xnT[:, c, 1:T + 1],
                                          start=c == 0, stop=c == EC - 1)
                mm.then_inc(h_psum, 1)

            def second_product(i, f):
                eng.wait_ge(h_ready, i * FT + f + 1)
                for t in range(TT):
                    mm = nc.tensor.matmul(half_bank(t), h[:, f, t * P:(t + 1) * P], W2[:, f, :],
                                          start=f == 0 and t % 2 == 0, stop=f == FT - 1, skip_group_check=True)
                return mm

            def body(i, more):
                eng.wait_ge(a.ready, i * EC + EC)
                for f in range(FT + AHEAD):
                    if f < FT:
                        first_product(i, f)
                    if f == FT - 1 and more:
                        a.tensor(eng, i + 1)
                    if f == AHEAD:
                        eng.wait_ge(o_taken, i * 2 + 2)
                    if f >= AHEAD:
                        mm = second_product(i, f - AHEAD)
                mm.then_inc(o_psum, 1)

            if not spiking:
                eng.wait_ge(abs_ready, 2)
                eng.wait_ge(ones_ready, 1)
                nc.tensor.matmul(psH[0][:, 0:2], ones[:, :], abs_sum[:, :], start=True, stop=True).then_inc(sum_ready, 1)
                eng.wait_ge(w_ready, 2)
            a.tensor(eng, 0)
            each_batch(eng, body)


def gelu_mlp(nc, g, tag, w):
    mlp(nc, g, tag, w, False)


def spiking_mlp(nc, g, tag, w):
    mlp(nc, g, tag, w, True)


HS = 8
DS = 64
NPAIR = HS // 2
TAPS = 4
LEVELS = 7
MASKED = 5


def state_space(nc, g, tag, w):
    with ExitStack() as ctx:
        s = Common(nc, ctx, g.sems)
        a, z = NormIn(g, s, tag), NormOut(g, s, tag)
        xnT, psA = a.xnT, a.psT
        x_pad = s.sb(tag + "x_pad", [P, NPAIR, T + TAPS - 1])
        skip = x_pad[:, :, TAPS - 1:]
        xs = s.sb(tag + "xs", [P, NPAIR, T])
        gate = s.sb(tag + "gate", [P, NPAIR, T])
        Bt = s.sb(tag + "Bt", [P, NPAIR, T])
        Ct = s.sb(tag + "Ct", [P, NPAIR, T])
        dtb = s.sb(tag + "dtb", [P, 2, T])
        prod = s.sb(tag + "prod", [P, 2, T])
        dA = s.sb(tag + "dA", [P, NPAIR, T])
        BT = dA
        tot = [dA] + [s.sb(tag + f"tot{L}", [P, NPAIR, T >> L]) for L in range(1, LEVELS + 1)]
        Cbd = s.sb(tag + "Cbd", [P, NPAIR, 2, T // 2])
        ST = s.sb(tag + "ST", [P, 2, TT, 4, P])
        xt = s.sb(tag + "xt", [P, TT, HS * DS])
        h = s.sb(tag + "h", [P, TT - 1, NPAIR, P])
        ysum = s.sb(tag + "ysum", [P, 2, T])
        o = s.sb(tag + "o", [P, TT, E])
        negA = s.sb(tag + "negA", [P, NPAIR])
        expA = s.sb(tag + "expA", [P, NPAIR])
        dtT = s.sb(tag + "dtT", [P, T])
        small = {k: s.sb(tag + k, [P, TT * HS]) for k in
                 ("raw", "v", "absv", "u", "w1", "ln", "eq", "d", "d2", "rec", "n", "n2", "r", "dt")}
        psL = [s.ps(tag + f"psL{j}") for j in range(4)]
        psY = [s.ps(tag + f"psY{j}") for j in range(2)]
        const = s.sem(tag + "const")
        moved = s.sem(tag + "moved")
        filled = s.sem(tag + "filled")
        dt_chain = s.sem(tag + "dt_chain")
        dt_act = s.sem(tag + "dt_act")
        conv = s.sem(tag + "conv")
        xs_ready = s.sem(tag + "xs_ready")
        b_scaled = s.sem(tag + "b_scaled")
        dtb_ready = s.sem(tag + "dtb_ready")
        prod_ready = s.sem(tag + "prod_ready")
        skip_ready = s.sem(tag + "skip_ready")
        c_ready = s.sem(tag + "c_ready")
        b_ready = s.sem(tag + "b_ready")
        tot_ready = s.sem(tag + "tot_ready")
        cbd_ready = s.sem(tag + "cbd_ready")
        l_psum = s.sem(tag + "l_psum")
        placed = s.sem(tag + "placed")
        copied = s.sem(tag + "copied")
        bT_psum = s.sem(tag + "bT_psum")
        bT_ready = s.sem(tag + "bT_ready")
        h_psum = s.sem(tag + "h_psum")
        h_ready = s.sem(tag + "h_ready")
        y_psum = s.sem(tag + "y_psum")
        ysum_ready = s.sem(tag + "ysum_ready")
        y_ready = s.sem(tag + "y_ready")
        DT, X, B, DTT, DTB, C, Z, G, XT, OUT, MOVES = 0, 1, 5, 9, 10, 14, 18, 22, 26, 30, 32
        block = ctx.enter_context(nc.Block())

        def blocks(v, m):
            return v.rearrange("p a (k e m) -> p a k e m", e=2, m=m)

        def pairs(tile, k):
            return tile[:, 2 * k:2 * k + 2, :]

        @block.vector
        def _(eng):
            ve = nc.vector

            def step_sizes(i):
                S = small
                n = [0]

                def link(ins):
                    n[0] += 1
                    ins.then_inc(dt_chain, 1)

                def settle():
                    eng.wait_ge(dt_chain, i * 11 + n[0])
                eng.wait_ge(moved, i * MOVES + DT + 1)
                link(ve.tensor_tensor(S["v"][:, :], S["raw"][:, :], w["dt_bias"][:, :], ALU.add))
                settle()
                link(ve.scalar_tensor_tensor(S["absv"][:, :], S["v"][:, :], -1.0, S["v"][:, :], ALU.mult, ALU.max))
                eng.wait_ge(dt_act, i * 2 + 1)
                link(ve.tensor_scalar_add(S["w1"][:, :], S["u"][:, :], 1.0))
                settle()
                link(ve.tensor_scalar(S["eq"][:, :], S["w1"][:, :], 1.0, None, ALU.is_equal))
                link(ve.tensor_scalar_add(S["d"][:, :], S["w1"][:, :], -1.0))
                settle()
                link(ve.tensor_tensor(S["d2"][:, :], S["d"][:, :], S["eq"][:, :], ALU.add))
                settle()
                link(ve.reciprocal(S["rec"][:, :], S["d2"][:, :]))
                eng.wait_ge(dt_act, i * 2 + 2)
                link(ve.tensor_tensor(S["n"][:, :], S["ln"][:, :], S["eq"][:, :], ALU.add))
                settle()
                link(ve.tensor_tensor(S["n2"][:, :], S["n"][:, :], S["u"][:, :], ALU.mult))
                settle()
                link(ve.tensor_tensor(S["r"][:, :], S["n2"][:, :], S["rec"][:, :], ALU.mult))
                settle()
                link(ve.scalar_tensor_tensor(S["dt"][:, :], S["v"][:, :], 0.0, S["r"][:, :], ALU.max, ALU.add))
                assert n[0] == 11

            def convolve(i):
                for k in range(TAPS):
                    for j in range(NPAIR):
                        if k == 0:
                            eng.wait_ge(moved, i * MOVES + X + j + 1)
                            ve.tensor_scalar(xs[:, j, :], x_pad[:, j, 0:T], w["conv_w"][:, j * TAPS:j * TAPS + 1],
                                             None, ALU.mult).then_inc(conv, 1)
                        else:
                            eng.wait_ge(conv, i * 16 + (k - 1) * NPAIR + j + 1)
                            ve.scalar_tensor_tensor(xs[:, j, :], x_pad[:, j, k:k + T],
                                                    w["conv_w"][:, j * TAPS + k:j * TAPS + k + 1], xs[:, j, :],
                                                    ALU.mult, ALU.add).then_inc(conv, 1)

            def update(i, L, k):
                if L == 0:
                    eng.wait_ge(prod_ready, i * NPAIR + 2 * k + 2)
                    ve.tensor_tensor(pairs(Ct, k), pairs(Ct, k), pairs(dA, k), ALU.mult).then_inc(c_ready, 1)
                    return
                m = 1 << (L - 1)
                t = tot[L - 1][:, 2 * k:2 * k + 2, :].rearrange("p a (k e) -> p a k e", e=2)
                eng.wait_ge(cbd_ready, i * 28 + 4 * (L - 1) + 2 * k + 2)
                eng.wait_ge(c_ready, i * 16 + 2 * (L - 1) + k + 1)
                if L > 1:
                    eng.wait_ge(tot_ready, i * 14 + 2 * (L - 2) + k + 1)
                c = blocks(pairs(Ct, k), m)[:, :, :, 1, :]
                ve.tensor_tensor(c, c, t[:, :, :, 0:1].to_broadcast([P, 2, T // (2 * m), m]),
                                 ALU.mult).then_inc(c_ready, 1)
                ve.tensor_tensor(tot[L][:, 2 * k:2 * k + 2, :], t[:, :, :, 0], t[:, :, :, 1],
                                 ALU.mult).then_inc(tot_ready, 1)

            def place(i, L, k):
                m = 1 << L
                for half in range(2):
                    wait_apart(g, eng, l_psum, i * 28 + 4 * L + 2 * k + half + 1)
                    out = ST[:, k, 2 * half:2 * half + 2, :, :].rearrange("p q h (b e m) -> p (q h) b e m", e=2, m=m)
                    mask = w["masks"][:, L * 64:(L + 1) * 64].bitcast(mybir.dt.uint32)
                    mask = mask.rearrange("p (b m) -> p b m", m=m).unsqueeze(1).to_broadcast([P, 8, 64 // m, m])
                    data = psL[2 * k + half][:, :].rearrange("p (h b m) -> p h b m", h=8, m=m)
                    ve.copy_predicated(out[:, :, :, 1, :], mask, data).then_inc(placed, 1)

            def states(i):
                eng.wait_ge(tot_ready, i * 14 + 14)
                for q in range(TT - 1):
                    eng.wait_ge(h_psum, i * 3 + q + 1)
                    if q:
                        eng.wait_ge(h_ready, i * 3 + q)
                    for p in range(NPAIR):
                        for b in range(2):
                            r = slice(b * DS, (b + 1) * DS)
                            new = psL[q][r, p * P + b * DS:p * P + (b + 1) * DS]
                            out = h[r, q, p, b * DS:(b + 1) * DS]
                            if q:
                                ins = ve.scalar_tensor_tensor(out, h[r, q - 1, p, b * DS:(b + 1) * DS],
                                                              tot[LEVELS][r, p, q:q + 1], new, ALU.mult, ALU.add)
                            else:
                                ins = ve.tensor_copy(out, new)
                    ins.then_inc(h_ready, 1)

            def body(i, more):
                step_sizes(i)
                convolve(i)
                for k in range(2):
                    update(i, 0, k)
                if more:
                    a.vector(eng, i + 1)
                for L in range(1, LEVELS + 1):
                    for k in range(2):
                        update(i, L, k)
                        if L - 1 < MASKED:
                            place(i, L - 1, k)
                states(i)
                for p in range(NPAIR):
                    eng.wait_ge(y_psum, i * NPAIR + p + 1)
                    eng.wait_ge(skip_ready, i * NPAIR + p + 1)
                    if p >= 2:
                        eng.wait_ge(y_ready, i * NPAIR + p - 1)
                    ve.tensor_tensor(ysum[:, p % 2, :], psY[p % 2][:, :], skip[:, p, :], ALU.add).then_inc(ysum_ready, 1)
                eng.wait_ge(moved, (i + 1) * MOVES)
                z.vector(eng, i, lambda t: o[:, t, :], moved, 0)
                z.tail(eng, i)

            eng.wait_ge(g.weights[w["sem"]], w["count"])
            ve.memset(x_pad[:, :, 0:TAPS - 1], 0.0).then_inc(const, 1)
            ve.memset(Cbd[:, :, :, :], 0.0).then_inc(const, 1)
            ve.memset(ST[:, :, :, :, :], 0.0).then_inc(const, 1)
            ve.memset(h[:, :, :, :], 0.0).then_inc(const, 1)
            ve.memset(dtT[:, :], 0.0).then_inc(const, 1)
            ve.memset(xnT[:, :, 0:1], 0.0).then_inc(const, 1)
            eng.wait_ge(const, 7)
            ve.tensor_scalar(negA[:, :], expA[:, :], -1.0, None, ALU.mult).then_inc(const, 1)
            a.vector(eng, 0, first=True)
            each_batch(eng, body)

        @block.sync
        def _(eng):
            g.look_ahead(eng)

        @block.gpsimd
        def _(eng):
            gp = nc.gpsimd

            def body(i, more):
                for p in range(NPAIR):
                    eng.wait_ge(dtb_ready, i * NPAIR + p + 1)
                    eng.wait_ge(moved, i * MOVES + B + p + 1)
                    gp.tensor_tensor(Bt[:, p, :], Bt[:, p, :], dtb[:, p % 2, :], ALU.mult).then_inc(b_scaled, 1)
                for p in range(NPAIR):
                    eng.wait_ge(b_scaled, i * NPAIR + p + 1)
                    eng.wait_ge(moved, i * MOVES + C + p + 1)
                    if p >= 2:
                        eng.wait_ge(filled, i * MOVES + G + p - 1)
                    gp.tensor_tensor(prod[:, p % 2, :], Bt[:, p, :], Ct[:, p, :], ALU.mult).then_inc(prod_ready, 1)
                if more:
                    a.gpsimd(eng, i + 1)
                for L in range(1, LEVELS + 1):
                    m = 1 << (L - 1)
                    for k in range(2):
                        eng.wait_ge(l_psum, i * 28 + 4 * (L - 1) + 2 * k + 2)
                        if L > 1:
                            eng.wait_ge(tot_ready, i * 14 + 2 * (L - 2) + k + 1)
                            eng.wait_ge(b_ready, i * 14 + 2 * (L - 2) + k + 1)
                        t = tot[L - 1][:, 2 * k:2 * k + 2, :].rearrange("p a (k e) -> p a k e", e=2)
                        b = blocks(pairs(Bt, k), m)[:, :, :, 0, :]
                        gp.tensor_tensor(b, b, t[:, :, :, 1:2].to_broadcast([P, 2, T // (2 * m), m]),
                                         ALU.mult).then_inc(b_ready, 1)
                    if L == 2:
                        for p in range(NPAIR):
                            eng.wait_ge(moved, i * MOVES + G + p + 1)
                            eng.wait_ge(xs_ready, i * NPAIR + p + 1)
                            gp.tensor_tensor(skip[:, p, :], skip[:, p, :], xs[:, p, :], ALU.mult).then_inc(skip_ready, 1)
                for p in range(NPAIR):
                    eng.wait_ge(ysum_ready, i * NPAIR + p + 1)
                    gp.tensor_tensor(gate[:, p, :], gate[:, p, :], ysum[:, p % 2, :], ALU.mult).then_inc(y_ready, 1)
                z.gpsimd(eng, i)
            eng.wait_ge(const, 8)
            a.gpsimd(eng, 0)
            each_batch(eng, body)

        @block.scalar
        def _(eng):
            sc = nc.scalar

            def take(i, use):
                eng.wait_ge(filled, i * MOVES + use + 1)
                return psA[use % 2]

            def block_diagonal(i, L, k):
                m = 1 << L
                if L:
                    eng.wait_ge(l_psum, i * 28 + 4 * (L - 1) + 2 * k + 2)
                eng.wait_ge(c_ready, i * 16 + 2 * L + k + 1)
                for b in range(2):
                    r = slice(b * DS, (b + 1) * DS)
                    sc.copy(Cbd[r, 2 * k:2 * k + 2, b, :].rearrange("p a (k m) -> p a k m", m=m),
                            blocks(Ct[r, 2 * k:2 * k + 2, :], m)[:, :, :, 1, :]).then_inc(cbd_ready, 1)

            def copy_scores(i, L, k):
                for half in range(2):
                    eng.wait_ge(l_psum, i * 28 + 4 * L + 2 * k + half + 1)
                    ps = psL[2 * k + half][:, :].rearrange("p (h n) -> p h n", h=8)
                    out = ST[:, k, 2 * half:2 * half + 2, :, :].rearrange("p q h n -> p (q h) n")
                    m = 1 << L
                    for j in range(64 // m):
                        r = slice(2 * m * j, 2 * m * j + m)
                        sc.copy(out[r, :, (2 * j + 1) * m:(2 * j + 2) * m],
                                ps[r, :, j * m:(j + 1) * m]).then_inc(copied, 1)

            def body(i, more):
                S = small
                sc.copy(S["raw"][:, :], take(i, DT)[:, 0:TT * HS]).then_inc(moved, 1)
                sc.copy(x_pad[:, 0, TAPS - 1:], take(i, X)[:, :]).then_inc(moved, 1)
                eng.wait_ge(dt_chain, i * 11 + 2)
                sc.activation(S["u"][:, :], S["absv"][:, :], ACT.Exp, scale=-1.0).then_inc(dt_act, 1)
                for j in range(1, NPAIR):
                    sc.copy(x_pad[:, j, TAPS - 1:], take(i, X + j)[:, :]).then_inc(moved, 1)
                eng.wait_ge(dt_chain, i * 11 + 3)
                sc.activation(S["ln"][:, :], S["w1"][:, :], ACT.Ln).then_inc(dt_act, 1)
                for p in range(NPAIR):
                    sc.copy(Bt[:, p, :], take(i, B + p)[:, :]).then_inc(moved, 1)
                sc.copy(dtT[0:HS, :], take(i, DTT)[0:HS, :]).then_inc(moved, 1)
                for p in range(NPAIR):
                    ps = take(i, DTB + p)
                    if p >= 2:
                        eng.wait_ge(b_scaled, i * NPAIR + p - 1)
                    sc.copy(dtb[:, p % 2, :], ps[:, :]).then_inc(dtb_ready, 1)
                    sc.activation(dA[:, p, :], ps[:, :], ACT.Exp, scale=negA[:, p:p + 1]).then_inc(moved, 1)
                for p in range(NPAIR):
                    sc.copy(Ct[:, p, :], take(i, C + p)[:, :]).then_inc(moved, 1)
                for p in range(NPAIR):
                    sc.activation(gate[:, p, :], take(i, Z + p)[:, :], ACT.Silu).then_inc(moved, 1)
                for j in range(NPAIR):
                    eng.wait_ge(conv, i * 16 + 3 * NPAIR + j + 1)
                    sc.activation(xs[:, j, :], xs[:, j, :], ACT.Silu, bias=w["conv_b"][:, j:j + 1]).then_inc(xs_ready, 1)
                for k in range(2):
                    block_diagonal(i, 0, k)
                for p in range(NPAIR):
                    sc.activation(skip[:, p, :], take(i, G + p)[:, :], ACT.Identity,
                                  bias=w["D"][:, p:p + 1]).then_inc(moved, 1)
                for t in range(TT):
                    sc.copy(xt[:, t, :], take(i, XT + t)[:, :]).then_inc(moved, 1)
                for L in range(1, LEVELS):
                    for k in range(2):
                        block_diagonal(i, L, k)
                        if L - 1 >= MASKED:
                            copy_scores(i, L - 1, k)
                for k in range(2):
                    copy_scores(i, LEVELS - 1, k)
                for q in range(TT):
                    eng.wait_ge(bT_psum, i * TT + q + 1)
                    sc.copy(BT[:, q, :], psL[q][:, :]).then_inc(bT_ready, 1)
                if more:
                    a.scalar(eng, i + 1)
                for j in range(2):
                    sc.copy(o[:, 2 * j:2 * j + 2, :], take(i, OUT + j)[:, :]).then_inc(moved, 1)
            eng.wait_ge(g.weights[w["sem"]], w["count"])
            sc.activation(expA[:, :], w["A_log"][:, :], ACT.Exp).then_inc(const, 1)
            eng.wait_ge(const, 8)
            a.scalar(eng, 0)
            each_batch(eng, body)

        @block.tensor
        def _(eng):
            te = nc.tensor
            eng.wait_ge(const, 8)

            def bank(i, use):
                if use >= 2:
                    eng.wait_ge(moved, i * MOVES + use - 1)
                return psA[use % 2]

            def rows(i, use, cols):
                ps = bank(i, use)
                for c in range(EC):
                    mm = te.matmul(ps[:, :], w["W_in"][:, c, cols:cols + P], xnT[:, c, 1:T + 1],
                                   start=c == 0, stop=c == EC - 1)
                mm.then_inc(filled, 1)

            def level(i, L, k):
                eng.wait_ge(cbd_ready, i * 28 + 4 * L + 2 * k + 2)
                if L:
                    eng.wait_ge(b_ready, i * 14 + 2 * (L - 1) + k + 1)
                    if L - 1 < MASKED:
                        eng.wait_ge(placed, i * 20 + 4 * (L - 1) + 2 * k + 2)
                    else:
                        eng.wait_ge(copied, i * 12 + 4 * k + 4)
                for half in range(2):
                    for q in range(2 * half, 2 * half + 2):
                        for p in range(2 * k, 2 * k + 2):
                            at = (q % 2) * 256 + (p % 2) * P
                            mm = te.matmul(psL[2 * k + half][:, at:at + P], Bt[:, p, q * P:(q + 1) * P],
                                           Cbd[:, p, :, q * 64:(q + 1) * 64], start=True, stop=True,
                                           skip_group_check=True)
                    mm.then_inc(l_psum, 1)

            def body(i, more):
                eng.wait_ge(a.ready, i * EC + EC)
                ps = bank(i, DT)
                for t in range(TT):
                    for c in range(EC):
                        mm = te.matmul(ps[:, t * HS:(t + 1) * HS], xnT[:, c, 1 + t * P:1 + (t + 1) * P],
                                       w["W_in"][:, c, 2048:2048 + HS], start=c == 0, stop=c == EC - 1)
                mm.then_inc(filled, 1)
                for j in range(NPAIR):
                    rows(i, X + j, j * P)
                for p in range(NPAIR):
                    rows(i, B + p, 1024 + p * P)
                eng.wait_ge(dt_chain, i * 11 + 11)
                ps = bank(i, DTT)
                for t in range(TT):
                    mm = te.transpose(ps[0:HS, t * P:(t + 1) * P], small["dt"][:, t * HS:(t + 1) * HS], g.ident[:, :])
                mm.then_inc(filled, 1)
                eng.wait_ge(moved, i * MOVES + DTT + 1)
                for p in range(NPAIR):
                    te.matmul(bank(i, DTB + p)[:, :], w["onehot"][:, p * P:(p + 1) * P], dtT[:, :],
                              start=True, stop=True).then_inc(filled, 1)
                for p in range(NPAIR):
                    rows(i, C + p, 1536 + p * P)
                for p in range(NPAIR):
                    rows(i, Z + p, 512 + p * P)
                for k in range(2):
                    for p in range(2 * k, 2 * k + 2):
                        eng.wait_ge(prod_ready, i * NPAIR + p + 1)
                        te.matmul(bank(i, G + p)[:, :], w["same_head"][:, :], prod[:, p % 2, :],
                                  start=True, stop=True).then_inc(filled, 1)
                for k in range(2):
                    level(i, 0, k)
                for t in range(TT):
                    ps = bank(i, XT + t)
                    if t == 0:
                        eng.wait_ge(xs_ready, i * NPAIR + NPAIR)
                    for j in range(NPAIR):
                        mm = te.transpose(ps[:, j * P:(j + 1) * P], xs[:, j, t * P:(t + 1) * P], g.ident[:, :])
                    mm.then_inc(filled, 1)
                for L in range(1, LEVELS):
                    for k in range(2):
                        level(i, L, k)
                eng.wait_ge(b_ready, i * 14 + 14)
                eng.wait_ge(copied, i * 12 + 12)
                for q in range(TT):
                    for p in range(NPAIR):
                        mm = te.transpose(psL[q][:, p * P:(p + 1) * P], Bt[:, p, q * P:(q + 1) * P], g.ident[:, :])
                    mm.then_inc(bT_psum, 1)
                eng.wait_ge(moved, i * MOVES + XT + TT)
                for q in range(TT - 1):
                    eng.wait_ge(bT_ready, i * TT + q + 1)
                    for p in range(NPAIR):
                        mm = te.matmul(psL[q][:, p * P:(p + 1) * P], BT[:, q, p * P:(p + 1) * P],
                                       xt[:, q, p * P:(p + 1) * P], start=True, stop=True, skip_group_check=True)
                    mm.then_inc(h_psum, 1)
                eng.wait_ge(c_ready, i * 16 + 16)
                for p in range(NPAIR):
                    if p >= 2:
                        eng.wait_ge(ysum_ready, i * NPAIR + p - 1)
                    for q in range(TT):
                        ps = psY[p % 2][:, q * P:(q + 1) * P]
                        for b in range(2):
                            hd = 2 * p + b
                            mm = te.matmul(ps[b * DS:(b + 1) * DS, :], xt[:, q, hd * DS:(hd + 1) * DS],
                                           ST[:, hd // 4, q, hd % 4, :], start=True, stop=q == 0,
                                           skip_group_check=True)
                        if q:
                            eng.wait_ge(h_ready, i * 3 + q)
                            mm = te.matmul(ps, h[:, q - 1, p, :], Ct[:, p, q * P:(q + 1) * P],
                                           start=False, stop=True, skip_group_check=True)
                    mm.then_inc(y_psum, 1)
                if more:
                    a.tensor(eng, i + 1)
                    eng.wait_ge(a.ready, i * EC + 2 * EC)
                for t in range(TT):
                    if t % 2 == 0:
                        ps = bank(i, OUT + t // 2)
                    for p in range(NPAIR):
                        eng.wait_ge(y_ready, i * NPAIR + p + 1)
                        mm = te.matmul(ps[:, (t % 2) * E:(t % 2 + 1) * E], gate[:, p, t * P:(t + 1) * P],
                                       w["W_out"][:, p, :], start=p == 0, stop=p == NPAIR - 1)
                    if t % 2:
                        mm.then_inc(filled, 1)
                eng.wait_ge(moved, (i + 1) * MOVES)
            a.tensor(eng, 0)
            each_batch(eng, body)


def rwkv_mix(nc, g, tag, w):
    with ExitStack() as ctx:
        s = Common(nc, ctx, g.sems)
        a, z = NormIn(g, s, tag), NormOut(g, s, tag)
        xnT = a.xnT
        diff = s.sb(tag + "diff", [P, EC, T])
        xr = s.sb(tag + "xr", [P, EC, T])
        xk = s.sb(tag + "xk", [P, EC, T])
        r = s.sb(tag + "r", [P, TT, E])
        k_relu = s.sb(tag + "k_relu", [P, EC, T])
        k_act = s.sb(tag + "k_act", [P, EC, T])
        gated = s.sb(tag + "gated", [P, TT, E])
        psR = [s.ps(tag + f"psR{j}") for j in range(TT // 2)]
        psK = [s.ps(tag + f"psK{f}") for f in range(EC)]
        psO = [s.ps(tag + f"psO{j}") for j in range(TT // 2)]
        zeroed = s.sem(tag + "zeroed")
        diff_ready = s.sem(tag + "diff_ready")
        xr_ready = s.sem(tag + "xr_ready")
        xk_ready = s.sem(tag + "xk_ready")
        r_psum = s.sem(tag + "r_psum")
        r_ready = s.sem(tag + "r_ready")
        k_psum = s.sem(tag + "k_psum")
        relu_ready = s.sem(tag + "relu_ready")
        k_ready = s.sem(tag + "k_ready")
        o_psum = s.sem(tag + "o_psum")
        gated_ready = s.sem(tag + "gated_ready")
        block = ctx.enter_context(nc.Block())

        def half(ps, t):
            return ps[t // 2][:, (t % 2) * E:(t % 2 + 1) * E]

        @block.vector
        def _(eng):
            ve = nc.vector

            def mix(n):
                for c in range(EC):
                    eng.wait_ge(a.ready, n * EC + c + 1)
                    ve.tensor_tensor(diff[:, c, :], xnT[:, c, 1:T + 1], xnT[:, c, 0:T],
                                     ALU.subtract).then_inc(diff_ready, 1)
                for c in range(EC):
                    eng.wait_ge(diff_ready, n * EC + c + 1)
                    ve.scalar_tensor_tensor(xr[:, c, :], diff[:, c, :], w["mu_r"][:, c:c + 1], xnT[:, c, 0:T],
                                            ALU.mult, ALU.add).then_inc(xr_ready, 1)
                for c in range(EC):
                    ve.scalar_tensor_tensor(xk[:, c, :], diff[:, c, :], w["mu_k"][:, c:c + 1], xnT[:, c, 0:T],
                                            ALU.mult, ALU.add).then_inc(xk_ready, 1)

            def body(i, more):
                if more:
                    a.vector(eng, i + 1)
                for f in range(EC):
                    eng.wait_ge(relu_ready, i * EC + f + 1)
                    ve.tensor_tensor(k_act[:, f, :], k_relu[:, f, :], k_relu[:, f, :],
                                     ALU.mult).then_inc(k_ready, 1)
                if more:
                    mix(i + 1)
                eng.wait_ge(r_ready, i * 2 + 2)
                for j in range(2):
                    eng.wait_ge(o_psum, i * 2 + j + 1)
                    ve.tensor_tensor(gated[:, 2 * j:2 * j + 2, :], psO[j][:, :], r[:, 2 * j:2 * j + 2, :],
                                     ALU.mult).then_inc(gated_ready, 1)
                z.vector(eng, i, lambda t: gated[:, t, :], gated_ready, 2)
                z.tail(eng, i)

            ve.memset(xnT[:, :, 0:1], 0.0).then_inc(zeroed, 1)
            eng.wait_ge(g.weights[w["sem"]], w["count"])
            eng.wait_ge(zeroed, 1)
            a.vector(eng, 0, first=True)
            mix(0)
            each_batch(eng, body)

        @block.sync
        def _(eng):
            g.look_ahead(eng)

        @block.gpsimd
        def _(eng):
            def body(i, more):
                if more:
                    a.gpsimd(eng, i + 1)
                z.gpsimd(eng, i)
            a.gpsimd(eng, 0)
            each_batch(eng, body)

        @block.scalar
        def _(eng):
            def body(i, more):
                for j in range(2):
                    eng.wait_ge(r_psum, i * 2 + j + 1)
                    nc.scalar.activation(r[:, 2 * j:2 * j + 2, :], psR[j][:, :], ACT.Sigmoid).then_inc(r_ready, 1)
                for f in range(EC):
                    eng.wait_ge(k_psum, i * EC + f + 1)
                    nc.scalar.activation(k_relu[:, f, :], psK[f][:, :], ACT.Relu).then_inc(relu_ready, 1)
                if more:
                    a.scalar(eng, i + 1)
                eng.wait_ge(gated_ready, i * 2 + 2)
            a.scalar(eng, 0)
            each_batch(eng, body)

        @block.tensor
        def _(eng):
            eng.wait_ge(g.weights[w["sem"]], w["count"])

            def body(i, more):
                eng.wait_ge(xr_ready, i * EC + EC)
                for t in range(TT):
                    for c in range(EC):
                        mm = nc.tensor.matmul(half(psR, t), xr[:, c, t * P:(t + 1) * P], w["W_r"][:, c, :],
                                              start=c == 0, stop=c == EC - 1)
                    if t % 2:
                        mm.then_inc(r_psum, 1)
                eng.wait_ge(xk_ready, i * EC + EC)
                for f in range(EC):
                    for c in range(EC):
                        mm = nc.tensor.matmul(psK[f][:, :], w["W_k"][:, c, f * P:(f + 1) * P], xk[:, c, :],
                                              start=c == 0, stop=c == EC - 1)
                    mm.then_inc(k_psum, 1)
                if more:
                    a.tensor(eng, i + 1)
                eng.wait_ge(k_ready, i * EC + EC)
                eng.wait_ge(r_ready, i * 2 + 2)
                for t in range(TT):
                    for f in range(EC):
                        mm = nc.tensor.matmul(half(psO, t), k_act[:, f, t * P:(t + 1) * P], w["W_v"][:, f, :],
                                              start=f == 0, stop=f == EC - 1)
                    if t % 2:
                        mm.then_inc(o_psum, 1)
            a.tensor(eng, 0)
            each_batch(eng, body)


H2 = 16
D2 = E // H2
G2 = 4
NG2 = H2 // G2
SLOT = 64
T_COL = {3: (0, 512), 2: (512, 384), 0: (896, 128), 1: (1024, 256)}
WCOLS = 1280
F32R = mybir.dt.float32r


def distance_attention(nc, g, tag, w):
    with ExitStack() as ctx:
        s = Common(nc, ctx, g.sems)
        a, z = NormIn(g, s, tag), NormOut(g, s, tag)
        xnT = a.xnT
        hi = s.sb(tag + "hi", [P, EC, T], F32R)
        lo = s.sb(tag + "lo", [P, EC, T], F32R)
        sq_hi = s.sb(tag + "sq_hi", [P, EC, T], F32R)
        sq_lo = s.sb(tag + "sq_lo", [P, EC, T], F32R)
        round_hi = s.sb(tag + "round_hi", [P, 2, T], F32R)
        aug = [s.sb(tag + f"aug{j}", [P, H2 // 2, T], F32R) for j in range(2)]
        v_pad = s.sb(tag + "v_pad", [P, TT, H2, 2 * D2])
        wts = s.sb(tag + "wts", [P, 2, G2, WCOLS])
        sq = wts[:, 0, 0, 0:EC * T].rearrange("p (c n) -> p c n", c=EC)
        ctxT = s.sb(tag + "ctxT", [P, NG2, T])
        o = s.sb(tag + "o", [P, TT, E])
        select = s.sb(tag + "select", [P, 12 * P], F32R)
        decay = s.sb(tag + "decay", [P, H2])
        psA = a.psT
        psS = [s.ps(tag + f"psS{j}") for j in range(4)]
        psC = [s.ps(tag + f"psC{j}") for j in range(2)]
        const = s.sem(tag + "const")
        qk_psum = s.sem(tag + "qk_psum")
        hi_ready = s.sem(tag + "hi_ready")
        lo_ready = s.sem(tag + "lo_ready")
        sq_ready = s.sem(tag + "sq_ready")
        sq_hi_ready = s.sem(tag + "sq_hi_ready")
        sq_lo_ready = s.sem(tag + "sq_lo_ready")
        rep_psum = s.sem(tag + "rep_psum")
        round_ready = s.sem(tag + "round_ready")
        aug_ready = s.sem(tag + "aug_ready")
        v_psum = s.sem(tag + "v_psum")
        v_ready = s.sem(tag + "v_ready")
        s_psum = s.sem(tag + "s_psum")
        dist_ready = s.sem(tag + "dist_ready")
        exp_ready = s.sem(tag + "exp_ready")
        masked = s.sem(tag + "masked")
        ctx_psum = s.sem(tag + "ctx_psum")
        ctx_ready = s.sem(tag + "ctx_ready")
        o_psum = s.sem(tag + "o_psum")
        o_ready = s.sem(tag + "o_ready")
        block = ctx.enter_context(nc.Block())
        NP2 = H2 // 2
        REGIONS = [(3,), (2, 0), (1,)]

        def cols(t):
            return slice(T_COL[t][0], T_COL[t][0] + T_COL[t][1])

        def region(j):
            return slice(T_COL[REGIONS[j][0]][0], T_COL[REGIONS[j][-1]][0] + T_COL[REGIONS[j][-1]][1])

        @block.vector
        def _(eng):
            ve = nc.vector

            def parts(i, side):
                for c in range(EC):
                    n = i * 4 + 2 * side + c
                    eng.wait_ge(sq_ready, n + 1)
                    ve.scalar_tensor_tensor(lo[:, c, :], psA[c][:, :], 1.0 - 3.0 * side, hi[:, c, :].bitcast(F32),
                                            ALU.mult, ALU.subtract).then_inc(lo_ready, 1)
                for c in range(EC):
                    n = i * 4 + 2 * side + c
                    eng.wait_ge(sq_hi_ready, n + 1)
                    ve.tensor_tensor(sq_lo[:, c, :], sq[:, c, :], sq_hi[:, c, :].bitcast(F32),
                                     ALU.subtract).then_inc(sq_lo_ready, 1)

            def augment(i, side):
                for p in range(NP2):
                    n = i * 16 + side * NP2 + p
                    eng.wait_ge(round_ready, n + 1)
                    ve.scalar_tensor_tensor(aug[side][:, p, :], round_hi[:, p % 2, :].bitcast(F32),
                                            w["rows"][:, side:side + 1], psA[p % 2][:, :],
                                            ALU.mult, ALU.add).then_inc(aug_ready, 1)

            def distances(i, h):
                for j in range(3):
                    r = 3 * h + j
                    eng.wait_ge(s_psum, i * 48 + r + 1)
                    width = region(j).stop - region(j).start
                    ve.tensor_scalar(wts[:, (h // G2) % 2, h % G2, region(j)], psS[r % 4][:, 0:width], 0.0, None,
                                     ALU.max).then_inc(dist_ready, 1)

            def body(i, more):
                for side in range(2):
                    parts(i, side)
                    augment(i, side)
                for h in range(H2):
                    if h % G2 == 0 and h // G2 >= 2:
                        eng.wait_ge(ctx_psum, i * 4 + h // G2 - 1)
                    distances(i, h)
                    if h == 6 and more:
                        a.vector(eng, i + 1)
                z.vector(eng, i, lambda t: o[:, t, :], o_ready, 2)
                z.tail(eng, i)

            eng.wait_ge(g.weights[w["sem"]], w["count"])
            ve.tensor_copy(select[:, :], w["select"][:, :]).then_inc(const, 1)
            ve.tensor_scalar(decay[:, :], w["gamma"][:, :], -float(D2) ** -0.5, None, ALU.mult).then_inc(const, 1)
            ve.memset(v_pad[:, :, :, :], 0.0).then_inc(const, 1)
            ve.memset(xnT[:, :, 0:1], 0.0).then_inc(const, 1)
            a.vector(eng, 0, first=True)
            each_batch(eng, body)

        @block.sync
        def _(eng):
            g.look_ahead(eng)

        @block.gpsimd
        def _(eng):
            def body(i, more):
                for k in range(NG2):
                    if k == 1 and more:
                        a.gpsimd(eng, i + 1)
                    wait_apart(g, eng, exp_ready, i * H2 + G2 * k + G2)
                    for t, n in ((3, 1), (2, 2), (1, 1)):
                        first = T_COL[t][0] + T_COL[t][1] - P
                        v = wts[:, k % 2, :, first:first + n * P]
                        if n == 2:
                            v = v.rearrange("p h (b s) -> p h b s", b=2)
                            pattern = [[0, G2], [0, 2], [-1, P]]
                        else:
                            pattern = [[0, G2], [-1, P]]
                        nc.gpsimd.affine_select(out=v, in_=v, compare_op=ALU.is_gt, fill=0.0, base=0,
                                                pattern=pattern, channel_multiplier=1).then_inc(masked, 1)
                z.gpsimd(eng, i)
            a.gpsimd(eng, 0)
            each_batch(eng, body)

        @block.scalar
        def _(eng):
            def parts(i, side):
                for c in range(EC):
                    n = i * 4 + 2 * side + c
                    eng.wait_ge(qk_psum, n + 1)
                    nc.scalar.activation(hi[:, c, :], psA[c][:, :], ACT.Copy, scale=1.0 - 3.0 * side).then_inc(hi_ready, 1)
                    nc.scalar.activation(sq[:, c, :], psA[c][:, :], ACT.Square).then_inc(sq_ready, 1)
                for c in range(EC):
                    n = i * 4 + 2 * side + c
                    eng.wait_ge(sq_ready, n + 1)
                    nc.scalar.copy(sq_hi[:, c, :], sq[:, c, :]).then_inc(sq_hi_ready, 1)

            def rounded(i, side):
                for p in range(NP2):
                    n = i * 16 + side * NP2 + p
                    eng.wait_ge(rep_psum, n + 1)
                    nc.scalar.activation(round_hi[:, p % 2, :], psA[p % 2][:, :], ACT.Identity,
                                         bias=w["rows"][:, 2 + side:3 + side]).then_inc(round_ready, 1)

            def body(i, more):
                for side in range(2):
                    parts(i, side)
                    rounded(i, side)
                for j in range(2):
                    eng.wait_ge(v_psum, i * 2 + j + 1)
                    for t in range(2):
                        ins = nc.scalar.copy(v_pad[:, 2 * j + t, :, 0:D2],
                                             psA[j][:, t * E:(t + 1) * E].rearrange("p (h d) -> p h d", d=D2))
                    ins.then_inc(v_ready, 1)
                for h in range(H2):
                    eng.wait_ge(dist_ready, i * 48 + 3 * h + 3)
                    v = wts[:, (h // G2) % 2, h % G2, :]
                    nc.scalar.activation(v, v, ACT.Exp, scale=decay[:, h:h + 1]).then_inc(exp_ready, 1)
                    if h % G2 == G2 - 1 and h > G2:
                        context(i, h // G2 - 1)
                context(i, NG2 - 1)
                for j in range(2):
                    eng.wait_ge(o_psum, i * 2 + j + 1)
                    nc.scalar.copy(o[:, 2 * j:2 * j + 2, :], psA[j][:, :]).then_inc(o_ready, 1)
                if more:
                    a.scalar(eng, i + 1)

            def context(i, k):
                eng.wait_ge(ctx_psum, i * NG2 + k + 1)
                nc.scalar.copy(ctxT[:, k, :], psC[k % 2][:, :]).then_inc(ctx_ready, 1)

            eng.wait_ge(g.weights[w["sem"]], w["count"])
            eng.wait_ge(const, 4)
            a.scalar(eng, 0)
            each_batch(eng, body)

        @block.tensor
        def _(eng):
            eng.wait_ge(g.weights[w["sem"]], w["count"])
            eng.wait_ge(const, 4)
            te = nc.tensor

            def project(i, side):
                W = w["Wk"] if side else w["Wq"]
                for f in range(EC):
                    for c in range(EC):
                        mm = te.matmul(psA[f][:, :], W[:, c, f * P:(f + 1) * P], xnT[:, c, 1:T + 1],
                                       start=c == 0, stop=c == EC - 1)
                    mm.then_inc(qk_psum, 1)

            def replicate(i, side):
                n = i * 4 + 2 * side + 2
                eng.wait_ge(lo_ready, n)
                eng.wait_ge(sq_lo_ready, n)
                for p in range(NP2):
                    c, k = divmod(p, 4)
                    if p >= 2:
                        eng.wait_ge(aug_ready, i * 16 + side * NP2 + p - 1)
                    place = select[:, k * P:(k + 1) * P]
                    norm = select[:, (4 + 4 * side + k) * P:(5 + 4 * side + k) * P]
                    te.matmul(psA[p % 2][:, :], place, hi[:, c, :], start=True, stop=False)
                    te.matmul(psA[p % 2][:, :], place, lo[:, c, :], start=False, stop=False)
                    te.matmul(psA[p % 2][:, :], norm, sq_hi[:, c, :], start=False, stop=False)
                    te.matmul(psA[p % 2][:, :], norm, sq_lo[:, c, :], start=False, stop=True).then_inc(rep_psum, 1)
                eng.wait_ge(aug_ready, i * 16 + side * NP2 + NP2)

            def values(i):
                for t in range(TT):
                    for c in range(EC):
                        mm = te.matmul(psA[t // 2][:, (t % 2) * E:(t % 2 + 1) * E], xnT[:, c, 1 + t * P:1 + (t + 1) * P],
                                       w["Wv"][:, c, :], start=c == 0, stop=c == EC - 1)
                    if t % 2:
                        mm.then_inc(v_psum, 1)

            def scores(i, k):
                for h in range(G2 * k, G2 * k + G2):
                    base, p = SLOT * (h % 2), h // 2
                    for j in range(3):
                        r = 3 * h + j
                        if r >= 4:
                            eng.wait_ge(dist_ready, i * 48 + r - 3)
                        for t in REGIONS[j]:
                            at = T_COL[t][0] - region(j).start
                            mm = te.matmul(psS[r % 4][:, at:at + T_COL[t][1]],
                                           aug[1][base:base + SLOT, p, t * P:(t + 1) * P],
                                           aug[0][base:base + SLOT, p, 0:T_COL[t][1]], start=True, stop=True)
                        mm.then_inc(s_psum, 1)

            def contexts(i, k):
                eng.wait_ge(masked, i * 12 + 3 * k + 3)
                if k >= 2:
                    eng.wait_ge(ctx_ready, i * NG2 + k - 1)
                for t in (3, 2, 1, 0):
                    for j in range(G2):
                        mm = te.matmul(psC[k % 2][32 * j:32 * j + 32, 0:T_COL[t][1]], v_pad[:, t, G2 * k + j, :],
                                       wts[:, k % 2, j, cols(t)], start=t == 3, stop=t == 0, skip_group_check=True)
                mm.then_inc(ctx_psum, 1)

            def body(i, more):
                eng.wait_ge(a.ready, i * EC + EC)
                for side in range(2):
                    project(i, side)
                    replicate(i, side)
                values(i)
                scores(i, 0)
                eng.wait_ge(v_ready, i * 2 + 2)
                for k in range(NG2):
                    if k + 1 < NG2:
                        scores(i, k + 1)
                    contexts(i, k)
                eng.wait_ge(ctx_ready, i * NG2 + NG2)
                for t in range(TT):
                    for k in range(NG2):
                        mm = te.matmul(psA[t // 2][:, (t % 2) * E:(t % 2 + 1) * E], ctxT[:, k, t * P:(t + 1) * P],
                                       w["Wo"][:, k, :], start=k == 0, stop=k == NG2 - 1)
                    if t % 2:
                        mm.then_inc(o_psum, 1)
                if more:
                    eng.wait_ge(o_ready, i * 2 + 2)
                    a.tensor(eng, i + 1)
            a.tensor(eng, 0)
            each_batch(eng, body)


H3 = 16
D3 = 64
HALF = H3 * D3 // 2
PI_4 = 0.7853981633974483


def angular_attention(nc, g, tag, w):
    with ExitStack() as ctx:
        s = Common(nc, ctx, g.sems)
        a, z = NormIn(g, s, tag), NormOut(g, s, tag)
        xnT = a.xnT
        th = s.sb(tag + "th", [P, TT, 2 * H3])
        cos = s.sb(tag + "cos", [P, TT, 2 * H3])
        sin = s.sb(tag + "sin", [P, TT, 2 * H3])
        d1 = s.sb(tag + "d1", [P, TT, H3])
        d2 = s.sb(tag + "d2", [P, TT, H3])
        d3 = s.sb(tag + "d3", [P, TT, H3])
        d4 = s.sb(tag + "d4", [P, TT, H3])
        cos_q = s.sb(tag + "cos_q", [P, TT, H3])
        sin_q = s.sb(tag + "sin_q", [P, TT, H3])
        half_pi = s.sb(tag + "half_pi", [P, 1])
        kv = [s.sb(tag + f"kv{j}", [P, 2, 2, HALF]) for j in range(2)]
        wsum = s.sb(tag + "wsum", [P, 2, 2, HALF])
        heads = s.sb(tag + "heads", [P, TT, 2 * HALF])
        headsT = s.sb(tag + "headsT", [P, 2, 8, P])
        o = s.sb(tag + "o", [P, TT, E])
        psC = [s.ps(tag + f"psC{j}") for j in range(4)]
        psV = s.ps(tag + "psV")
        psQ = s.ps(tag + "psQ")
        const = s.sem(tag + "const")
        qk_psum = s.sem(tag + "qk_psum")
        tanh_ready = s.sem(tag + "tanh_ready")
        trig_ready = s.sem(tag + "trig_ready")
        den_psum = s.sem(tag + "den_psum")
        den = s.sem(tag + "den")
        v_psum = s.sem(tag + "v_psum")
        kv_ready = s.sem(tag + "kv_ready")
        cum_ready = s.sem(tag + "cum_ready")
        weighted = s.sem(tag + "weighted")
        heads_ready = s.sem(tag + "heads_ready")
        headsT_psum = s.sem(tag + "headsT_psum")
        headsT_ready = s.sem(tag + "headsT_ready")
        o_psum = s.sem(tag + "o_psum")
        o_ready = s.sem(tag + "o_ready")
        W_V, W_O = w["W_V"], w["W_O"]
        block = ctx.enter_context(nc.Block())
        N = 2 * TT

        def per_head(tile, t, half, first):
            v = tile[:, t, first + half * 8:first + half * 8 + 8]
            return v.unsqueeze(2).to_broadcast([P, 8, D3])

        def by_head(v):
            return v.rearrange("p (h d) -> p h d", d=D3)

        @block.vector
        def _(eng):
            ve = nc.vector

            def key_values(i, n):
                t, half = divmod(n, 2)
                eng.wait_ge(v_psum, i * N + n + 1)
                for j, trig in enumerate((cos, sin)):
                    ve.tensor_tensor(by_head(kv[t % 2][:, half, j, :]), by_head(psV[:, :]),
                                     per_head(trig, t, half, H3), ALU.mult).then_inc(kv_ready, 1)

            def weigh(i, n):
                t, half = divmod(n, 2)
                eng.wait_ge(cum_ready, i * N + n + 1)
                if n >= 2:
                    eng.wait_ge(heads_ready, i * N + n - 1)
                for j, trig in enumerate((cos_q, sin_q)):
                    ve.tensor_tensor(by_head(wsum[:, n % 2, j, :]), by_head(psC[2 * half + j][:, :]),
                                     per_head(trig, t, half, 0), ALU.mult).then_inc(weighted, 1)

            def denominators(i):
                eng.wait_ge(den_psum, i + 1)
                sums = psQ[:, 128:256].rearrange("p (t j) -> p t j", t=TT)
                steps = [
                    lambda: ve.tensor_tensor(d1[:, :, :], sums[:, :, 0:H3], cos[:, :, 0:H3], ALU.mult),
                    lambda: ve.tensor_tensor(d2[:, :, :], sums[:, :, H3:2 * H3], sin[:, :, 0:H3], ALU.mult),
                    lambda: ve.tensor_tensor(d3[:, :, :], d1[:, :, :], d2[:, :, :], ALU.add),
                    lambda: ve.tensor_scalar_add(d4[:, :, :], d3[:, :, :], 1e-6),
                    lambda: ve.reciprocal(d1[:, :, :], d4[:, :, :]),
                    lambda: ve.tensor_tensor(cos_q[:, :, :], cos[:, :, 0:H3], d1[:, :, :], ALU.mult),
                    lambda: ve.tensor_tensor(sin_q[:, :, :], sin[:, :, 0:H3], d1[:, :, :], ALU.mult),
                ]
                for k, step in enumerate(steps):
                    if k:
                        eng.wait_ge(den, i * 7 + k)
                    step().then_inc(den, 1)
                eng.wait_ge(den, i * 7 + 7)

            def body(i, more):
                eng.wait_ge(trig_ready, i * 2 + 2)
                for n in range(N):
                    key_values(i, n)
                    if n == 0:
                        denominators(i)
                    if n == 2 and more:
                        a.vector(eng, i + 1)
                    if n >= 1:
                        weigh(i, n - 1)
                weigh(i, N - 1)
                z.vector(eng, i, lambda t: o[:, t, :], o_ready, TT)
                z.tail(eng, i)
                eng.wait_ge(heads_ready, i * N + N)

            ve.memset(half_pi[:, :], 2 * PI_4).then_inc(const, 1)
            ve.memset(xnT[:, :, 0:1], 0.0).then_inc(const, 1)
            a.vector(eng, 0, first=True)
            each_batch(eng, body)

        @block.sync
        def _(eng):
            g.look_ahead(eng)

        @block.gpsimd
        def _(eng):
            def body(i, more):
                for n in range(N):
                    if n == 1 and more:
                        a.gpsimd(eng, i + 1)
                    t, half = divmod(n, 2)
                    eng.wait_ge(weighted, i * 2 * N + 2 * n + 2)
                    nc.gpsimd.tensor_tensor(heads[:, t, half * HALF:(half + 1) * HALF], wsum[:, n % 2, 0, :],
                                            wsum[:, n % 2, 1, :], ALU.add).then_inc(heads_ready, 1)
                z.gpsimd(eng, i)
            a.gpsimd(eng, 0)
            each_batch(eng, body)

        @block.scalar
        def _(eng):
            def trigonometry(n):
                eng.wait_ge(qk_psum, n + 1)
                flat = "p t j -> p (t j)"
                nc.scalar.activation(th[:, :, :].rearrange(flat), psQ[:, 0:128], ACT.Tanh).then_inc(tanh_ready, 1)
                eng.wait_ge(tanh_ready, n + 1)
                nc.scalar.activation(cos[:, :, :], th[:, :, :], ACT.Sin, scale=PI_4,
                                     bias=half_pi[:, 0:1]).then_inc(trig_ready, 1)
                nc.scalar.activation(sin[:, :, :], th[:, :, :], ACT.Sin, scale=PI_4).then_inc(trig_ready, 1)

            def body(i, more):
                if more:
                    a.scalar(eng, i + 1)
                    trigonometry(i + 1)
                for t in range(TT):
                    for k in range(2):
                        eng.wait_ge(headsT_psum, i * N + 2 * t + k + 1)
                        nc.scalar.copy(headsT[:, t % 2, 4 * k:4 * k + 4, :], a.psT[k][:, :]).then_inc(headsT_ready, 1)
                    eng.wait_ge(o_psum, i * TT + t + 1)
                    nc.scalar.copy(o[:, t, :], psC[t][:, 0:E]).then_inc(o_ready, 1)
            eng.wait_ge(const, 1)
            a.scalar(eng, 0)
            trigonometry(0)
            each_batch(eng, body)

        @block.tensor
        def _(eng):
            eng.wait_ge(g.weights[w["sem"]], w["count"])

            def queries_keys(n):
                eng.wait_ge(a.ready, n * EC + EC)
                for t in range(TT):
                    for c in range(EC):
                        mm = nc.tensor.matmul(psQ[:, t * 32:t * 32 + 32], xnT[:, c, 1 + t * P:1 + (t + 1) * P],
                                              w["W_QK"][:, c, :], start=c == 0, stop=c == EC - 1)
                mm.then_inc(qk_psum, 1)

            def values(i, n):
                t, half = divmod(n, 2)
                if n >= 1:
                    eng.wait_ge(kv_ready, i * 2 * N + 2 * n)
                for c in range(EC):
                    mm = nc.tensor.matmul(psV[:, :], xnT[:, c, 1 + t * P:1 + (t + 1) * P],
                                          W_V[:, c, half * HALF:(half + 1) * HALF], start=c == 0, stop=c == EC - 1)
                mm.then_inc(v_psum, 1)

            def denominators(i):
                eng.wait_ge(trig_ready, i * 2 + 2)
                for t in range(TT):
                    for j, trig in enumerate((cos, sin)):
                        for u in range(t + 1):
                            mm = nc.tensor.matmul(psQ[:, 128 + t * 32 + j * H3:128 + t * 32 + (j + 1) * H3],
                                                  w["tri"][:, :] if u == t else w["ones"][:, :],
                                                  trig[:, u, H3:2 * H3], start=u == 0, stop=u == t)
                mm.then_inc(den_psum, 1)

            def running_sum(i, n):
                t, half = divmod(n, 2)
                eng.wait_ge(kv_ready, i * 2 * N + 2 * n + 2)
                if t:
                    eng.wait_ge(weighted, i * 2 * N + 2 * n - 2)
                for j in range(2):
                    if t:
                        nc.tensor.matmul(psC[2 * half + j][:, :], w["rest"][:, :], kv[(t - 1) % 2][:, half, j, :],
                                         start=False, stop=True, skip_group_check=True)
                    mm = nc.tensor.matmul(psC[2 * half + j][:, :], w["tri"][:, :], kv[t % 2][:, half, j, :],
                                          start=t == 0, stop=True, skip_group_check=True)
                mm.then_inc(cum_ready, 1)

            def project(i, t):
                eng.wait_ge(heads_ready, i * N + 2 * t + 2)
                if t:
                    eng.wait_ge(headsT_ready, i * N + 2 * t)
                for k in range(8):
                    mm = nc.tensor.transpose(a.psT[k // 4][:, (k % 4) * P:(k % 4 + 1) * P],
                                             heads[:, t, k * P:(k + 1) * P], g.ident[:, :])
                    if k % 4 == 3:
                        mm.then_inc(headsT_psum, 1)
                eng.wait_ge(headsT_ready, i * N + 2 * t + 2)
                if t == 0:
                    eng.wait_ge(weighted, (i + 1) * 2 * N)
                for k in range(8):
                    mm = nc.tensor.matmul(psC[t][:, 0:E], headsT[:, t % 2, k, :], W_O[:, k, :],
                                          start=k == 0, stop=k == 7)
                mm.then_inc(o_psum, 1)

            def body(i, more):
                values(i, 0)
                denominators(i)
                for n in range(1, N):
                    values(i, n)
                    running_sum(i, n - 1)
                running_sum(i, N - 1)
                if more:
                    a.tensor(eng, i + 1)
                    queries_keys(i + 1)
                for t in range(TT):
                    project(i, t)
                eng.wait_ge(o_ready, i * TT + TT)
            a.tensor(eng, 0)
            queries_keys(0)
            each_batch(eng, body)


WEIGHTS = [
    [("Wq", "mat", (E, E)), ("Wk", "mat", (E, E)), ("Wv", "mat", (E, E)), ("Wo", "mat", (E, E)),
     ("bq", "flat", (P, EC)), ("bk", "flat", (P, EC)), ("bv", "flat", (P, EC)), ("bo", "flat", (P, 2 * E)),
     ("head8", "flat", (P, 8)), ("head16", "flat", (P, EC * H0))],
    [("W1", "mat", (E, FF)), ("W2", "mat", (FF, E)), ("b1", "flat", (P, FT)), ("b2", "flat", (P, 2 * E))],
    [("W_in", "mat", (E, 2048 + HS)), ("W_out", "mat", (HS * DS, E)), ("conv_w", "flat", (P, NPAIR * TAPS)),
     ("conv_b", "flat", (P, NPAIR)), ("A_log", "flat", (P, NPAIR)), ("D", "flat", (P, NPAIR)),
     ("dt_bias", "flat", (P, TT * HS)), ("onehot", "flat", (P, NPAIR * P)), ("same_head", "flat", (P, P)),
     ("masks", "flat", (P, MASKED * 64))],
    [("W_r", "mat", (E, E)), ("W_k", "mat", (E, E)), ("W_v", "mat", (E, E)), ("mu_r", "flat", (P, EC)), ("mu_k", "flat", (P, EC))],
    [("Wq", "mat", (E, E)), ("Wk", "mat", (E, E)), ("Wv", "mat", (E, E)), ("Wo", "mat", (2 * E, E)),
     ("gamma", "flat", (P, H2)), ("rows", "flat", (P, 4)), ("select", "flat", (P, 12 * P))],
    [("W_r", "mat", (E, E)), ("W_k", "mat", (E, E)), ("W_v", "mat", (E, E)), ("mu_r", "flat", (P, EC)), ("mu_k", "flat", (P, EC))],
    [("W_QK", "mat", (E, 2 * H3)), ("W_V", "mat", (E, H3 * D3)), ("W_O", "mat", (H3 * D3, E)),
     ("tri", "flat", (P, P)), ("rest", "flat", (P, P)), ("ones", "flat", (P, P))],
    [("W1", "mat", (E, FF)), ("W2", "mat", (FF, E))],
]
ARENA = (6200, 4640)
SUBLAYERS = [windowed_attention, gelu_mlp, state_space, rwkv_mix, distance_attention, rwkv_mix, angular_attention, spiking_mlp]


def build(nc, d, out, subs=tuple(range(8))):
    with ExitStack() as ctx:
        lasting = Semaphores()
        ctx.enter_context(lasting.stack)
        g = Common(nc, ctx, lasting)
        g.x = g.sb("x", [P, NB * TT, E])
        g.ident = g.sb("ident", [P, P])
        g.minus_half = g.sb("minus_half", [P, TT])
        g.x_loaded = g.sem("x_loaded")
        g.const_ready = g.sem("const_ready")
        out_stored = g.sem("out_stored")
        g.weights = [g.sem(f"weights{k}") for k in range(8)]
        arena = [g.sb(f"arena{j}", [P, ARENA[j]]) for j in range(2)]
        loads, tiles = [[] for _ in range(8)], [{} for _ in range(8)]
        for k in subs:
            at = 0
            for name, kind, size in WEIGHTS[k]:
                src = d[f"l{k}_{name}"]
                width = size[0] // P * size[1] if kind == "mat" else size[1]
                tile = arena[k % 2][0:P if kind == "mat" else size[0], at:at + width]
                at += width + width % 2
                if kind == "mat":
                    tile = tile.rearrange("p (c n) -> p c n", n=size[1])
                    src = src.rearrange("(c p) n -> p c n", p=P)
                loads[k].append((tile, src))
                tiles[k][name] = tile
            assert at <= ARENA[k % 2], (k, at)
            tiles[k]["sem"], tiles[k]["count"] = k, 16 * len(loads[k])

        def load_weights(eng, k):
            for tile, src in loads[k]:
                eng.dma_start(tile, src).then_inc(g.weights[k], 16)

        with nc.Block() as block:
            @block.sync
            def _(eng):
                eng.dma_start(g.ident[:, :], d["ident"]).then_inc(g.x_loaded, 16)
                for b in range(NB):
                    eng.dma_start(g.x[:, b * TT:(b + 1) * TT, :],
                                  d["x"][b].rearrange("(t p) e -> p t e", p=P)).then_inc(g.x_loaded, 16)
                load_weights(eng, subs[0])

            @block.vector
            def _(eng):
                nc.vector.memset(g.minus_half[:, :], -0.5).then_inc(g.const_ready, 1)
                eng.wait_ge(g.const_ready, 1)
                eng.wait_ge(g.x_loaded, 16 * (NB + 1))

        before = Semaphores()
        for k, after in zip(subs, list(subs[1:]) + [None]):
            def look_ahead(eng, cleared=before.all, after=after):
                if after is not None:
                    load_weights(eng, after)
                for sem in cleared:
                    eng.sem_clear(sem)
            g.sems, g.look_ahead = Semaphores(), look_ahead
            SUBLAYERS[k](nc, g, f"l{k}_", tiles[k])
            before.stack.close()
            before = g.sems
        before.stack.close()

        with nc.Block() as block:
            @block.sync
            def _(eng):
                for b in range(NB):
                    eng.dma_start(out[b].rearrange("(t p) e -> p t e", p=P),
                                  g.x[:, b * TT:(b + 1) * TT, :]).then_inc(out_stored, 16)
                eng.wait_ge(out_stored, 16 * NB)


def state_space_layout(np, v, col):
    W = v["L1_attn_W_in"]
    inner = HS * DS
    heads = W[2 * inner:].reshape(HS, 2 * DS + 1, E)
    parts = [W[:2 * inner], heads[:, :DS].reshape(inner, E), heads[:, DS:2 * DS].reshape(inner, E), heads[:, 2 * DS]]
    same = np.kron(np.eye(2), np.ones((DS, DS))).astype(np.float32)
    onehot = np.zeros((P, NPAIR, 2, DS), np.float32)
    for hd in range(HS):
        onehot[hd, hd // 2, hd % 2] = 1.0
    masks = np.zeros((P, MASKED, 64), np.float32)
    for L in range(MASKED):
        m = 1 << L
        for n in range(64):
            k = n // m
            masks[2 * m * k:2 * m * k + m, L, n] = 1.0
    return {
        "W_in": np.concatenate(parts).T, "W_out": v["L1_attn_W_out"].T,
        "conv_w": v["L1_attn_conv_w"][:, 0].reshape(NPAIR, P, TAPS).transpose(1, 0, 2).reshape(P, NPAIR * TAPS),
        "conv_b": col(v["L1_attn_conv_b"]), "A_log": col(v["L1_attn_A_log"].reshape(-1)),
        "D": col(np.repeat(v["L1_attn_D"], DS)),
        "dt_bias": np.broadcast_to(np.tile(v["L1_attn_dt_bias"], TT), (P, TT * HS)),
        "onehot": onehot.reshape(P, NPAIR * P), "same_head": same, "masks": masks.reshape(P, MASKED * 64),
    }


def split_rows(np):
    rows = np.zeros((P, 4), np.float32)
    select = np.zeros((P, 12, P), np.float32)
    for side, low, ones, norm in ((0, slice(32, 48), 50, 48), (1, slice(16, 32), 48, 50)):
        for slot in (0, SLOT):
            r = rows[slot:slot + SLOT]
            r[low, side] = -1.0
            r[norm + 1, side] = -1.0
            r[ones:ones + 2, side] = 1.0
            r[ones:ones + 2, 2 + side] = 1.0
    for k in range(4):
        for b in range(2):
            for j in range(D2):
                src = (2 * k + b) * D2 + j
                for copy in range(3):
                    select[src, k, b * SLOT + copy * D2 + j] = 1.0
                for side, norm in ((0, 48), (1, 50)):
                    select[src, 4 + 4 * side + k, b * SLOT + norm:b * SLOT + norm + 2] = 1.0
    return rows, select.reshape(P, 12 * P)


def layouts(v):
    import numpy as np

    def col(a):
        return a.reshape(-1, P).T

    def row(a):
        return np.broadcast_to(np.concatenate([a, a]), (P, 2 * E))

    d = {"x": v["L0_attn_hidden_states"], "ident": np.eye(P, dtype=np.float32)}
    for key, a in state_space_layout(np, v, col).items():
        d["l2_" + key] = a
    for k, layer in ((3, "L1_ffn_"), (5, "L2_ffn_")):
        for name in ("W_r", "W_k", "W_v"):
            d[f"l{k}_{name}"] = v[layer + name].T
        for name in ("mu_r", "mu_k"):
            d[f"l{k}_{name}"] = col(v[layer + name])
    for name in ("Wq", "Wk", "Wv", "Wo"):
        d["l0_" + name] = v["L0_attn_" + name]
    for name in ("bq", "bk", "bv"):
        d["l0_" + name] = col(v["L0_attn_" + name])
    d["l0_bo"] = row(v["L0_attn_bo"])
    head8 = np.repeat(np.eye(8, dtype=np.float32), D0, axis=0)
    d["l0_head8"] = head8
    head16 = np.zeros((P, EC, H0), np.float32)
    for c in range(EC):
        head16[:, c, 8 * c:8 * c + 8] = head8
    d["l0_head16"] = head16.reshape(P, EC * H0)
    d["l1_W1"], d["l1_W2"] = v["L0_ffn_W1"].T, v["L0_ffn_W2"].T
    d["l1_b1"] = col(v["L0_ffn_b1"])
    d["l1_b2"] = row(v["L0_ffn_b2"])
    for name in ("Wq", "Wk", "Wv"):
        d["l4_" + name] = v["L2_attn_" + name]
    wo = np.zeros((H2, 2 * D2, E), np.float32)
    wo[:, :D2] = v["L2_attn_Wo"].reshape(H2, D2, E)
    d["l4_Wo"] = wo.reshape(2 * E, E)
    d["l4_gamma"] = np.broadcast_to(v["L2_attn_gamma"], (P, H2))
    d["l4_rows"], d["l4_select"] = split_rows(np)
    tri = np.triu(np.ones((P, P), np.float32))
    d["l6_W_QK"] = np.concatenate([v["L3_attn_W_Q"][:, :, 0], v["L3_attn_W_K"][:, :, 0]]).T
    d["l6_W_V"] = v["L3_attn_W_V"].transpose(1, 0, 2).reshape(E, -1)
    d["l6_W_O"] = v["L3_attn_W_O"].transpose(2, 1, 0).reshape(-1, E)
    d["l6_tri"], d["l6_rest"], d["l6_ones"] = tri, np.tril(np.ones((P, P), np.float32), -1), np.ones((P, P), np.float32)
    d["l7_W1"], d["l7_W2"] = v["L3_ffn_W_fc"].T, v["L3_ffn_W_proj"].T
    return {k: np.ascontiguousarray(a) for k, a in d.items()}


def kernel(**inputs):
    import numpy as np
    import concourse.bacc as bacc
    from concourse.bass_utils import run_bass_kernel_spmd

    arrays = layouts({k: np.asarray(a) for k, a in inputs.items()})
    nc = bacc.Bacc("TRN2", target_bir_lowering=False, num_devices=1)
    dram = {k: nc.dram_tensor(k + "_dram", a.shape, mybir.dt.from_np(a.dtype), kind="ExternalInput").ap()
            for k, a in arrays.items()}
    out = nc.dram_tensor("out_dram", (NB, T, E), F32, kind="ExternalOutput").ap()
    build(nc, dram, out)
    r = run_bass_kernel_spmd(nc, [{k + "_dram": a for k, a in arrays.items()}], core_ids=[0])
    return r.results[0]["out_dram"]
```

```python
from contextlib import ExitStack

import concourse.bass as bass
from concourse import mybir

F32 = mybir.dt.float32
F32R = mybir.dt.float32r
ALU = mybir.AluOpType
ACT = mybir.ActivationFunctionType
AX = mybir.AxisListType

P = 128
NB = 8
T = 512
E = 256
TT = T // P
EC = E // P
EPS = 1e-5


class Common:

    def __init__(self, nc, ctx, sems):
        self.nc, self.ctx, self.sems = nc, ctx, sems

    def sb(self, name, shape, dt=F32):
        return self.ctx.enter_context(self.nc.sbuf_tensor(name, shape, dt))

    def ps(self, name, shape=(P, 512)):
        return self.ctx.enter_context(self.nc.psum_tensor(name, list(shape), F32))

    def sem(self, name):
        return self.sems.new(self.nc, name)


class Semaphores:

    def __init__(self):
        self.stack, self.all = ExitStack(), []

    def new(self, nc, name):
        self.all.append(self.stack.enter_context(nc.semaphore(name)))
        return self.all[-1]


def wait_apart(g, eng, sem, value):
    if not isinstance(value, int):
        eng.compute_val(value)
    eng.wait_ge(g.const_ready, 1)
    eng.wait_ge(sem, value)


def each_batch(eng, body, ahead=1):
    with eng.Fori(0, NB - ahead) as i:
        body(i, True)
    for i in range(NB - ahead, NB):
        body(i, False)


class NormIn:

    def __init__(self, g, s, tag):
        self.g, self.nc = g, g.nc
        self.loading = g.loading
        self.st = s.sb(tag + "in_st", [P, TT, 6])
        self.mv = s.sb(tag + "in_mv", [P, TT, 2])
        self.ve = s.sb(tag + "in_ve", [P, TT])
        self.rs = s.sb(tag + "in_rs", [P, TT])
        self.xn = s.sb(tag + "xn", [P, TT, E])
        self.xnT = s.sb(tag + "xnT", [P, EC, T + 1])
        self.psT = [s.ps(tag + f"psT{c}") for c in range(EC)]
        self.stats = s.sem(tag + "in_stats")
        self.moments = s.sem(tag + "in_moments")
        self.var = s.sem(tag + "in_var")
        self.rstd = s.sem(tag + "in_rstd")
        self.xn_ready = s.sem(tag + "xn_ready")
        self.turned = s.sem(tag + "turned")
        self.ready = s.sem(tag + "xnT_ready")

    def x_tile(self, n, t):
        return self.g.x[:, bass.ds(n * TT + t, 1), :]

    def vector(self, eng, n, first=False):
        self.statistics(eng, n)
        self.normalise(eng, n, first)

    def statistics(self, eng, n):
        ve = self.nc.vector
        if self.loading and not (isinstance(n, int) and n == 0):
            eng.wait_ge(self.g.x_loaded, 16 * (NB - 1))
        for t in range(TT):
            ve.bn_stats(self.st[:, t, :], self.x_tile(n, t)).then_inc(self.stats, 1)
        for t in range(TT):
            wait_apart(self.g, eng, self.stats, n * TT + t + 1)
            ve.bn_aggr(self.mv[:, t, :], self.st[:, t, :]).then_inc(self.moments, 1)
        eng.wait_ge(self.moments, n * TT + TT)
        ve.tensor_scalar_add(self.ve[:, :], self.mv[:, :, 1], EPS).then_inc(self.var, 1)

    def normalise(self, eng, n, first=False):
        ve = self.nc.vector
        eng.wait_ge(self.rstd, n + 1)
        if not first:
            eng.wait_ge(self.turned, n)
        for t in range(TT):
            ve.tensor_scalar(self.xn[:, t:t + 1, :], self.x_tile(n, t), self.mv[:, t, 0:1], self.rs[:, t:t + 1],
                             ALU.subtract, ALU.mult).then_inc(self.xn_ready, 1)

    def gpsimd(self, eng, n):
        eng.wait_ge(self.var, n + 1)
        self.nc.gpsimd.tensor_tensor(self.rs[:, :], self.ve[:, :], self.g.minus_half[:, 0:TT],
                                     ALU.pow).then_inc(self.rstd, 1)

    def tensor(self, eng, n):
        for t in range(TT):
            eng.wait_ge(self.xn_ready, n * TT + t + 1)
            for c in range(EC):
                last = self.nc.tensor.transpose(self.psT[c][:, t * P:(t + 1) * P],
                                                self.xn[:, t, c * P:(c + 1) * P], self.g.ident[:, :])
        last.then_inc(self.turned, 1)

    def scalar(self, eng, n):
        eng.wait_ge(self.turned, n + 1)
        for c in range(EC):
            self.nc.scalar.copy(self.xnT[:, c, 1:T + 1], self.psT[c][:, :]).then_inc(self.ready, 1)


class NormOut:

    def __init__(self, g, s, tag, y=None):
        self.g, self.nc = g, g.nc
        self.st = s.sb(tag + "out_st", [P, TT, 6])
        self.mv = s.sb(tag + "out_mv", [P, TT, 2])
        self.ve = s.sb(tag + "out_ve", [P, TT])
        self.rs = s.sb(tag + "out_rs", [P, TT])
        self.y = s.sb(tag + "out_y", [P, TT, E]) if y is None else y
        self.stats = s.sem(tag + "out_stats")
        self.moments = s.sem(tag + "out_moments")
        self.var = s.sem(tag + "out_var")
        self.rstd = s.sem(tag + "out_rstd")
        self.normed = s.sem(tag + "normed")
        self.added = s.sem(tag + "added")

    def vector(self, eng, i, source, ready, per):
        self.statistics(eng, i, source, ready, per)
        self.normalise(eng, i, source)

    def statistics(self, eng, i, source, ready, per):
        ve = self.nc.vector
        self.free(eng, i)
        for t in range(TT):
            if per:
                eng.wait_ge(ready, i * per + t * per // TT + 1)
            ve.bn_stats(self.st[:, t, :], source(t)).then_inc(self.stats, 1)
        for t in range(TT):
            wait_apart(self.g, eng, self.stats, i * TT + t + 1)
            ve.bn_aggr(self.mv[:, t, :], self.st[:, t, :]).then_inc(self.moments, 1)
        eng.wait_ge(self.moments, i * TT + TT)
        ve.tensor_scalar_add(self.ve[:, :], self.mv[:, :, 1], EPS).then_inc(self.var, 1)

    def normalise(self, eng, i, source):
        ve = self.nc.vector
        eng.wait_ge(self.rstd, i + 1)
        for t in range(TT):
            ve.tensor_scalar(self.y[:, t, :], source(t), self.mv[:, t, 0:1], self.rs[:, t:t + 1],
                             ALU.subtract, ALU.mult).then_inc(self.normed, 1)

    def gpsimd(self, eng, i):
        eng.wait_ge(self.var, i + 1)
        self.nc.gpsimd.tensor_tensor(self.rs[:, :], self.ve[:, :], self.g.minus_half[:, 0:TT],
                                     ALU.pow).then_inc(self.rstd, 1)
        for t in range(TT):
            eng.wait_ge(self.normed, i * TT + t + 1)
            xt = self.g.x[:, bass.ds(i * TT + t, 1), :]
            self.nc.gpsimd.tensor_tensor(xt, xt, self.y[:, t:t + 1, :], ALU.add).then_inc(self.added, 1)

    def free(self, eng, i):
        eng.wait_ge(self.added, i * TT + TT)

    def gpsimd_start(self, eng):
        self.nc.gpsimd.memset(self.y[:, 0, 0:1], 0.0).then_inc(self.added, TT)


H0 = 16
D0 = E // H0
WIN = 64
NW = 4
WPAIRS = NW // 2
SCALE0 = float(D0) ** -0.5


def windowed_attention(nc, g, tag, w):
    with ExitStack() as ctx:
        s = Common(nc, ctx, g.sems)
        a, z = NormIn(g, s, tag), NormOut(g, s, tag)
        xnT, psA = a.xnT, a.psT
        qT = s.sb(tag + "qT", [P, EC, NW, WIN + 1])
        kT = s.sb(tag + "kT", [P, EC, T])
        v_win = s.sb(tag + "v_win", [P, NW, E])
        keys = s.sb(tag + "keys", [P, 2, 2, 8 * WIN])
        sc = s.sb(tag + "sc", [P, 2, 8 * WIN])
        mx = s.sb(tag + "mx", [P, 4, 8])
        sums = s.sb(tag + "sums", [P, 4, 8])
        rinv = s.sb(tag + "rinv", [P, 4, 8])
        prT = s.sb(tag + "prT", [P, 2, 4 * P])
        ctxs = s.sb(tag + "ctxs", [P, WPAIRS, E])
        ctxT = s.sb(tag + "ctxT", [P, EC, T])
        o = s.sb(tag + "o", [P, TT, E])
        q0 = s.sb(tag + "q0", [P, EC, H0])
        gmx = s.sb(tag + "gmx", [H0, 1])
        gneg = s.sb(tag + "gneg", [H0, 1])
        gsum = s.sb(tag + "gsum", [H0, 1])
        ginv = s.sb(tag + "ginv", [H0, 1])
        gexp = s.sb(tag + "gexp", [H0, T])
        gpr = s.sb(tag + "gpr", [H0, T])
        gprT = s.sb(tag + "gprT", [P, TT, H0])
        gx = s.sb(tag + "gx", [P, EC, H0])
        gdiag = s.sb(tag + "gdiag", [P, EC, H0])
        gctx = s.sb(tag + "gctx", [P, EC])
        psS = [s.ps(tag + f"psS{j}") for j in range(2)]
        psP = [s.ps(tag + f"psP{j}") for j in range(2)]
        psX = [s.ps(tag + f"psX{j}") for j in range(2)]
        const = s.sem(tag + "const")
        proj_psum = s.sem(tag + "proj_psum")
        proj_ready = s.sem(tag + "proj_ready")
        q0_ready = s.sem(tag + "q0_ready")
        g_psum = s.sem(tag + "g_psum")
        g_max = s.sem(tag + "g_max")
        g_exp = s.sem(tag + "g_exp")
        g_norm = s.sem(tag + "g_norm")
        gT_psum = s.sem(tag + "gT_psum")
        gT_ready = s.sem(tag + "gT_ready")
        gx_psum = s.sem(tag + "gx_psum")
        gx_ready = s.sem(tag + "gx_ready")
        gc_psum = s.sem(tag + "gc_psum")
        gc_steps = s.sem(tag + "gc_steps")
        keys_ready = s.sem(tag + "keys_ready")
        s_psum = s.sem(tag + "s_psum")
        max_ready = s.sem(tag + "max_ready")
        sub_ready = s.sem(tag + "sub_ready")
        exp_ready = s.sem(tag + "exp_ready")
        sum_ready = s.sem(tag + "sum_ready")
        prT_psum = s.sem(tag + "prT_psum")
        prT_ready = s.sem(tag + "prT_ready")
        x_psum = s.sem(tag + "x_psum")
        inv_ready = s.sem(tag + "inv_ready")
        ctx_ready = s.sem(tag + "ctx_ready")
        ctxT_psum = s.sem(tag + "ctxT_psum")
        ctxT_ready = s.sem(tag + "ctxT_ready")
        o_psum = s.sem(tag + "o_psum")
        o_ready = s.sem(tag + "o_ready")
        block = ctx.enter_context(nc.Block())

        def heads(v):
            return v.rearrange("p (h n) -> p h n", h=8)

        def spread(v, n):
            return v.unsqueeze(2).to_broadcast([P, 8, n])

        @block.vector
        def _(eng):
            ve = nc.vector

            def subtract_max(i, n):
                eng.wait_ge(s_psum, i * 4 + n + 1)
                ve.tensor_reduce(mx[:, n, :], heads(psS[n % 2][:, :]), AX.X, ALU.max).then_inc(max_ready, 1)
                eng.wait_ge(max_ready, i * 4 + n + 1)
                if n >= 2:
                    eng.wait_ge(prT_psum, i * 4 + n - 1)
                    eng.wait_ge(sum_ready, i * 4 + n - 1)
                ve.tensor_tensor(heads(sc[:, n % 2, :]), heads(psS[n % 2][:, :]), spread(mx[:, n, :], WIN),
                                 ALU.subtract).then_inc(sub_ready, 1)

            def row_sums(i, n):
                eng.wait_ge(exp_ready, i * 4 + n + 1)
                ve.tensor_reduce(sums[:, n, :], heads(sc[:, n % 2, :]), AX.X, ALU.add).then_inc(sum_ready, 1)

            def first_query(n):
                for c in range(EC):
                    eng.wait_ge(proj_ready, n * 6 + c + 1)
                    ve.tensor_scalar(q0[:, c, :], w["head16"][:, c * H0:(c + 1) * H0], qT[:, c, 0, 0:1], None,
                                     ALU.mult).then_inc(q0_ready, 1)

            def body(i, more):
                eng.wait_ge(g_psum, i + 1)
                ve.tensor_reduce(gmx[:, :], psA[0][0:H0, :], AX.X, ALU.max).then_inc(g_max, 1)
                eng.wait_ge(g_max, i * 2 + 1)
                ve.tensor_scalar(gneg[:, :], gmx[:, :], -SCALE0, None, ALU.mult).then_inc(g_max, 1)
                subtract_max(i, 0)
                subtract_max(i, 1)
                eng.wait_ge(g_exp, i + 1)
                ve.reciprocal(ginv[:, :], gsum[:, :]).then_inc(g_norm, 1)
                eng.wait_ge(g_norm, i * 2 + 1)
                ve.tensor_scalar(gpr[:, :], gexp[:, :], ginv[:, 0:1], None, ALU.mult).then_inc(g_norm, 1)
                row_sums(i, 0)
                subtract_max(i, 2)
                row_sums(i, 1)
                if more:
                    eng.wait_ge(gx_psum, i + 1)
                    a.statistics(eng, i + 1)
                subtract_max(i, 3)
                if more:
                    a.normalise(eng, i + 1)
                row_sums(i, 2)
                eng.wait_ge(gc_psum, i + 1)
                ve.tensor_tensor(gdiag[:, :, :], psA[1][:, 0:EC * H0].rearrange("p (c h) -> p c h", c=EC),
                                 w["head16"][:, :].rearrange("p (c h) -> p c h", c=EC), ALU.mult).then_inc(gc_steps, 1)
                eng.wait_ge(gc_steps, i * 3 + 1)
                ve.tensor_reduce(gctx[:, :], gdiag[:, :, :], AX.X, ALU.add).then_inc(gc_steps, 1)
                eng.wait_ge(gc_steps, i * 3 + 2)
                ve.tensor_tensor(ctxT[:, :, 0:1], gctx[:, :].unsqueeze(2), w["bv"][:, :].unsqueeze(2),
                                 ALU.add).then_inc(gc_steps, 1)
                row_sums(i, 3)
                eng.wait_ge(sum_ready, i * 4 + 4)
                ve.reciprocal(rinv[:, :, :], sums[:, :, :]).then_inc(inv_ready, 1)
                eng.wait_ge(inv_ready, i + 1)
                eng.wait_ge(x_psum, i + 1)
                for b in range(2):
                    out = ctxs[:, :, :].rearrange("p a (m b d) -> p a m b d", b=2, d=D0)[:, :, :, b, :]
                    inv = rinv[:, :, :].rearrange("p (a c) (m b) -> p a c m b", a=2, b=2)[:, :, :, :, b]
                    for wp in range(WPAIRS):
                        ins = ve.tensor_tensor(
                            out[:, wp, :, :].rearrange("p (c m) d -> p c m d", c=EC),
                            psX[b][:, wp * P:(wp + 1) * P].rearrange("p (c m d) -> p c m d", c=EC, d=D0),
                            inv[:, wp, :, :].unsqueeze(3).to_broadcast([P, EC, 4, D0]), ALU.mult)
                    ins.then_inc(ctx_ready, 1)
                if more:
                    first_query(i + 1)
                for j in range(2):
                    eng.wait_ge(o_psum, i * 2 + j + 1)
                    ve.tensor_tensor(o[:, 2 * j:2 * j + 2, :], psA[j][:, :], w["bo"][:, :], ALU.add).then_inc(o_ready, 1)
                eng.wait_ge(o_ready, i * 2 + 2)
                z.vector(eng, i, lambda t: o[:, t, :], o_psum, 2)

            ve.memset(ctxT[:, :, :], 0.0).then_inc(const, 1)
            ve.memset(xnT[:, :, 0:1], 0.0).then_inc(const, 1)
            eng.wait_ge(const, 2)
            a.vector(eng, 0, first=True)
            eng.wait_ge(g.weights[w["sem"]], w["count"])
            first_query(0)
            each_batch(eng, body)

        @block.sync
        def _(eng):
            g.look_ahead(eng, z)

        @block.gpsimd
        def _(eng):
            def spread_keys(i, n):
                wp, c = divmod(n, 2)
                eng.wait_ge(proj_ready, i * 6 + 3 + c)
                if n >= 2:
                    eng.wait_ge(s_psum, i * 4 + n - 1)
                for k in range(2):
                    at = (2 * wp + k) * P + 1
                    kw = kT[:, c, at:at + WIN].unsqueeze(1).to_broadcast([P, 8, WIN])
                    nc.gpsimd.tensor_tensor(heads(keys[:, n % 2, k, :]), kw, spread(w["head8"][:, :], WIN),
                                            ALU.mult).then_inc(keys_ready, 1)

            def body(i, more):
                spread_keys(i, 2)
                spread_keys(i, 3)
                if more:
                    a.gpsimd(eng, i + 1)
                    eng.wait_ge(s_psum, i * 4 + 4)
                    spread_keys(i + 1, 0)
                    spread_keys(i + 1, 1)
                z.gpsimd(eng, i)
            eng.wait_ge(g.weights[w["sem"]], w["count"])
            z.gpsimd_start(eng)
            a.gpsimd(eng, 0)
            spread_keys(0, 0)
            spread_keys(0, 1)
            each_batch(eng, body)

        @block.scalar
        def _(eng):
            sc_e = nc.scalar

            def exponent(i, n):
                eng.wait_ge(sub_ready, i * 4 + n + 1)
                sc_e.activation(sc[:, n % 2, :], sc[:, n % 2, :], ACT.Exp, scale=SCALE0).then_inc(exp_ready, 1)

            def turned(i, n):
                eng.wait_ge(prT_psum, i * 4 + n + 1)
                sc_e.copy(prT[:, n % 2, :], psP[n % 2][:, :]).then_inc(prT_ready, 1)

            def queries(n):
                for c in range(EC):
                    eng.wait_ge(proj_psum, n * 6 + c + 1)
                    sc_e.activation(qT[:, c, :, :].rearrange("p w n -> p (w n)"), psA[c][:, 0:NW * (WIN + 1)],
                                    ACT.Identity, bias=w["bq"][:, c:c + 1]).then_inc(proj_ready, 1)

            def all_keys(n):
                for c in range(EC):
                    eng.wait_ge(proj_psum, n * 6 + c + 3)
                    sc_e.activation(kT[:, c, :], psA[c][:, :], ACT.Identity,
                                    bias=w["bk"][:, c:c + 1]).then_inc(proj_ready, 1)

            def values(n):
                for j in range(2):
                    eng.wait_ge(proj_psum, n * 6 + j + 5)
                    sc_e.copy(v_win[:, 2 * j:2 * j + 2, :], psA[j][:, :]).then_inc(proj_ready, 1)

            def body(i, more):
                eng.wait_ge(g_max, i * 2 + 2)
                sc_e.activation(gexp[:, :], psA[0][0:H0, :], ACT.Exp, scale=SCALE0, bias=gneg[:, 0:1],
                                accum_out=gsum[:, 0:1]).then_inc(g_exp, 1)
                exponent(i, 0)
                exponent(i, 1)
                turned(i, 0)
                eng.wait_ge(gT_psum, i + 1)
                sc_e.copy(gprT[:, :, :], psA[1][:, 0:TT * H0]).then_inc(gT_ready, 1)
                exponent(i, 2)
                eng.wait_ge(gx_psum, i + 1)
                sc_e.copy(gx[:, :, :], psA[0][:, 0:EC * H0]).then_inc(gx_ready, 1)
                turned(i, 1)
                exponent(i, 3)
                if more:
                    a.scalar(eng, i + 1)
                turned(i, 2)
                if more:
                    queries(i + 1)
                turned(i, 3)
                if more:
                    all_keys(i + 1)
                    values(i + 1)
                eng.wait_ge(ctxT_psum, i + 1)
                for c in range(EC):
                    sc_e.activation(ctxT[:, c, :].rearrange("p (w n) -> p w n", w=NW)[:, :, 1:1 + WIN],
                                    psA[0][:, c * 256:(c + 1) * 256].rearrange("p (w n) -> p w n", w=NW),
                                    ACT.Identity, bias=w["bv"][:, c:c + 1]).then_inc(ctxT_ready, 1)
            eng.wait_ge(const, 2)
            eng.wait_ge(g.weights[w["sem"]], w["count"])
            a.scalar(eng, 0)
            queries(0)
            all_keys(0)
            values(0)
            each_batch(eng, body)

        @block.tensor
        def _(eng):
            eng.wait_ge(g.weights[w["sem"]], w["count"])
            te = nc.tensor

            def queries(i):
                eng.wait_ge(a.ready, i * EC + EC)
                for f in range(EC):
                    for c in range(EC):
                        mm = te.matmul(psA[f][:, 0:NW * (WIN + 1)], w["Wq"][:, c, f * P:(f + 1) * P],
                                       xnT[:, c, 1:T + 1].rearrange("p (w n) -> p w n", w=NW)[:, :, 0:WIN + 1],
                                       start=c == 0, stop=c == EC - 1)
                    mm.then_inc(proj_psum, 1)

            def all_keys(i):
                for f in range(EC):
                    eng.wait_ge(proj_ready, i * 6 + f + 1)
                    for c in range(EC):
                        mm = te.matmul(psA[f][:, :], w["Wk"][:, c, f * P:(f + 1) * P], xnT[:, c, 1:T + 1],
                                       start=c == 0, stop=c == EC - 1)
                    mm.then_inc(proj_psum, 1)

            def values(i):
                for j in range(2):
                    eng.wait_ge(proj_ready, i * 6 + j + 3)
                    for k in range(2):
                        at = (2 * j + k) * P + 2
                        for c in range(EC):
                            for b in range(2):
                                mm = te.matmul(psA[j][b * WIN:(b + 1) * WIN, k * E:(k + 1) * E],
                                               xnT[:, c, at:at + WIN], w["Wv"][:, c, :],
                                               start=c == 0, stop=c == EC - 1, skip_group_check=True)
                    mm.then_inc(proj_psum, 1)

            def scores(i, n):
                wp, c = divmod(n, 2)
                eng.wait_ge(keys_ready, i * 8 + 2 * n + 2)
                for k in range(2):
                    mm = te.matmul(psS[n % 2][k * WIN:(k + 1) * WIN, :], qT[:, c, 2 * wp + k, 1:WIN + 1],
                                   keys[:, n % 2, k, :], start=True, stop=True, skip_group_check=True)
                mm.then_inc(s_psum, 1)

            def turn(i, n):
                eng.wait_ge(exp_ready, i * 4 + n + 1)
                for m in range(4):
                    mm = te.transpose(psP[n % 2][:, m * P:(m + 1) * P], sc[:, n % 2, m * P:(m + 1) * P],
                                      g.ident[:, :])
                mm.then_inc(prT_psum, 1)

            def context(i, n):
                wp, c = divmod(n, 2)
                wait_apart(g, eng, prT_ready, i * 4 + n + 1)
                for m in range(4):
                    for b in range(2):
                        for k in range(2):
                            h = 8 * c + 2 * m + b
                            at = wp * P + (4 * c + m) * D0
                            mm = te.matmul(psX[b][k * WIN:(k + 1) * WIN, at:at + D0],
                                           prT[b * WIN:(b + 1) * WIN, n % 2, m * P + k * WIN:m * P + (k + 1) * WIN],
                                           v_win[b * WIN:(b + 1) * WIN, 2 * wp + k, h * D0:(h + 1) * D0],
                                           start=True, stop=True, skip_group_check=True)
                return mm

            def body(i, more):
                eng.wait_ge(q0_ready, i * 2 + 2)
                for c in range(EC):
                    mm = te.matmul(psA[0][0:H0, :], q0[:, c, :], kT[:, c, :], start=c == 0, stop=c == EC - 1)
                mm.then_inc(g_psum, 1)
                scores(i, 0)
                scores(i, 1)
                turn(i, 0)
                scores(i, 2)
                eng.wait_ge(g_norm, i * 2 + 2)
                for t in range(TT):
                    mm = te.matmul(psA[1][:, t * H0:(t + 1) * H0], gpr[:, t * P:(t + 1) * P], g.ident[0:H0, 0:H0],
                                   start=True, stop=True)
                mm.then_inc(gT_psum, 1)
                eng.wait_ge(gT_ready, i + 1)
                for c in range(EC):
                    for t in range(TT):
                        mm = te.matmul(psA[0][:, c * H0:(c + 1) * H0], a.xn[:, t, c * P:(c + 1) * P], gprT[:, t, :],
                                       start=t == 0, stop=t == TT - 1)
                mm.then_inc(gx_psum, 1)
                context(i, 0)
                turn(i, 1)
                scores(i, 3)
                eng.wait_ge(gx_ready, i + 1)
                for f in range(EC):
                    for c in range(EC):
                        mm = te.matmul(psA[1][:, f * H0:(f + 1) * H0], w["Wv"][:, c, f * P:(f + 1) * P], gx[:, c, :],
                                       start=c == 0, stop=c == EC - 1)
                mm.then_inc(gc_psum, 1)
                context(i, 1)
                if more:
                    eng.wait_ge(gc_steps, i * 3 + 1)
                    a.tensor(eng, i + 1)
                turn(i, 2)
                if more:
                    queries(i + 1)
                context(i, 2)
                turn(i, 3)
                if more:
                    all_keys(i + 1)
                context(i, 3).then_inc(x_psum, 1)
                if more:
                    values(i + 1)
                    eng.wait_ge(proj_ready, i * 6 + 6 + 6)
                else:
                    eng.wait_ge(gc_steps, i * 3 + 1)
                eng.wait_ge(ctx_ready, i * 2 + 2)
                for c in range(EC):
                    for wp in range(WPAIRS):
                        mm = te.transpose(psA[0][:, c * 256 + wp * P:c * 256 + (wp + 1) * P],
                                          ctxs[:, wp, c * P:(c + 1) * P], g.ident[:, :])
                mm.then_inc(ctxT_psum, 1)
                eng.wait_ge(ctxT_ready, i * 2 + 2)
                eng.wait_ge(gc_steps, i * 3 + 3)
                for t in range(TT):
                    for c in range(EC):
                        mm = te.matmul(psA[t // 2][:, (t % 2) * E:(t % 2 + 1) * E], ctxT[:, c, t * P:(t + 1) * P],
                                       w["Wo"][:, c, :], start=c == 0, stop=c == EC - 1)
                    if t % 2:
                        mm.then_inc(o_psum, 1)
                eng.wait_ge(o_ready, i * 2 + 2)
            a.tensor(eng, 0)
            queries(0)
            all_keys(0)
            values(0)
            eng.wait_ge(proj_ready, 6)
            each_batch(eng, body)


FF = 4 * E
FT = FF // P


def gelu_mlp(nc, g, tag, w):
    with ExitStack() as ctx:
        s = Common(nc, ctx, g.sems)
        a, z = NormIn(g, s, tag), NormOut(g, s, tag)
        HB = 4
        AHEAD = 3
        x_hi = s.sb(tag + "x_hi", [P, EC, T], F32R)
        x_lo = s.sb(tag + "x_lo", [P, EC, T], F32R)
        RING = 4
        h_act = s.sb(tag + "h_act", [P, RING, T])
        h_hi = s.sb(tag + "h_hi", [P, FT, T], F32R)
        h_lo = s.sb(tag + "h_lo", [P, FT, T], F32R)
        o = s.sb(tag + "o", [P, TT, E])
        absw = s.sb(tag + "absw", [P, EC * FF])
        abs_sum = s.sb(tag + "abs_sum", [P, 2])
        ones = s.sb(tag + "ones", [P, P])
        half = s.sb(tag + "half", [P, 2])
        minus_half = s.sb(tag + "neg_half", [P, 2])
        below = s.sb(tag + "below", [P, EC * FF])
        tern = [s.sb(tag + f"tern{m}", [P, EC * FF], F32R) for m in range(2)]
        raw = [w["W1"].rearrange("p c n -> p (c n)"), w["W2"].rearrange("p c n -> p (c n)")]
        W1 = tern[0][:, :].rearrange("p (c n) -> p c n", c=EC)
        W2 = tern[1][:, :].rearrange("p (c n) -> p c n", c=FT)
        psH = [s.ps(tag + f"psH{j}") for j in range(HB)]
        psO = [s.ps(tag + f"psO{j}") for j in range(TT // 2)]
        ones_ready = s.sem(tag + "ones_ready")
        abs_ready = s.sem(tag + "abs_ready")
        sum_ready = s.sem(tag + "sum_ready")
        limit = s.sem(tag + "limit")
        w_ready = s.sem(tag + "w_ready")
        x_hi_ready = s.sem(tag + "x_hi_ready")
        x_ready = s.sem(tag + "x_ready")
        h_psum = s.sem(tag + "h_psum")
        act_ready = s.sem(tag + "act_ready")
        h_hi_ready = s.sem(tag + "h_hi_ready")
        h_ready = s.sem(tag + "h_ready")
        o_psum = s.sem(tag + "o_psum")
        o_taken = s.sem(tag + "o_taken")
        block = ctx.enter_context(nc.Block())

        @block.vector
        def _(eng):
            ve = nc.vector

            def limits():
                eng.wait_ge(sum_ready, 1)
                ve.tensor_scalar(half[:, :], psH[0][:, 0:2], 1.0 / (E * FF), 1e-8, ALU.mult,
                                 ALU.max).then_inc(limit, 1)
                eng.wait_ge(limit, 1)
                ve.tensor_scalar(minus_half[:, :], half[:, :], -0.5, None, ALU.mult).then_inc(limit, 1)
                eng.wait_ge(limit, 2)
                ve.tensor_scalar(half[:, :], minus_half[:, :], -1.0, None, ALU.mult).then_inc(limit, 1)
                eng.wait_ge(limit, 3)

            def make_ternary(m):
                if m:
                    eng.wait_ge(w_ready, 1)
                ve.tensor_scalar(below[:, :], raw[m], minus_half[:, m:m + 1], None, ALU.is_lt).then_inc(limit, 1)
                eng.wait_ge(limit, 4 + m)
                ve.scalar_tensor_tensor(tern[m][:, :], raw[m], half[:, m:m + 1], below[:, :],
                                        ALU.is_gt, ALU.subtract).then_inc(w_ready, 1)

            def rest_of_x(n):
                for c in range(EC):
                    eng.wait_ge(x_hi_ready, n * EC + c + 1)
                    ve.tensor_tensor(x_lo[:, c, :], a.psT[c][:, :], x_hi[:, c, :].bitcast(F32),
                                     ALU.subtract).then_inc(x_ready, 1)

            def rest_of_h(i, f):
                eng.wait_ge(h_hi_ready, i * FT + f + 1)
                ve.tensor_tensor(h_lo[:, f, :], h_act[:, f % RING, :], h_hi[:, f, :].bitcast(F32),
                                 ALU.subtract).then_inc(h_ready, 1)

            def take_output(i):
                eng.wait_ge(o_psum, i + 1)
                z.free(eng, i)
                for j in range(2):
                    ve.tensor_tensor(o[:, 2 * j:2 * j + 2, :], psO[j][:, :], w["b2"], ALU.add).then_inc(o_taken, 1)
                eng.wait_ge(o_taken, i * 2 + 4)

            def source(t):
                return o[:, t, :]

            def body(i, before, more):
                if before:
                    take_output(i - 1)
                rest_of_h(i, 0)
                rest_of_h(i, 1)
                if more:
                    a.statistics(eng, i + 1)
                rest_of_h(i, 2)
                if more:
                    a.normalise(eng, i + 1)
                rest_of_h(i, 3)
                if before:
                    z.statistics(eng, i - 1, source, o_psum, 0)
                rest_of_h(i, 4)
                if before:
                    z.normalise(eng, i - 1, source)
                for f in range(5, FT):
                    rest_of_h(i, f)
                if more:
                    rest_of_x(i + 1)

            ve.memset(ones[:, :], 1.0).then_inc(ones_ready, 1)
            ve.memset(h_act[:, :, 0:1], 0.0).then_inc(h_ready, RING)
            ve.memset(o[:, 0, 0:1], 0.0).then_inc(o_taken, 2)
            a.vector(eng, 0, first=True)
            eng.wait_ge(g.weights[w["sem"]], w["count"])
            limits()
            make_ternary(0)
            rest_of_x(0)
            make_ternary(1)
            body(0, False, True)
            with eng.Fori(1, NB - 1) as i:
                body(i, True, True)
            body(NB - 1, True, False)
            take_output(NB - 1)
            z.vector(eng, NB - 1, source, o_psum, 0)

        @block.sync
        def _(eng):
            g.look_ahead(eng, z)

        @block.gpsimd
        def _(eng):
            z.gpsimd_start(eng)
            a.gpsimd(eng, 0)
            a.gpsimd(eng, 1)
            with eng.Fori(1, NB - 1) as i:
                a.gpsimd(eng, i + 1)
                z.gpsimd(eng, i - 1)
            z.gpsimd(eng, NB - 2)
            z.gpsimd(eng, NB - 1)

        @block.scalar
        def _(eng):
            def round_x(n):
                eng.wait_ge(a.turned, n + 1)
                for c in range(EC):
                    nc.scalar.copy(x_hi[:, c, :], a.psT[c][:, :]).then_inc(x_hi_ready, 1)

            def body(i, more):
                for f in range(FT):
                    eng.wait_ge(h_psum, i * FT + f + 1)
                    if f == FT - 1 and more:
                        round_x(i + 1)
                    eng.wait_ge(h_ready, i * FT + f + 1)
                    nc.scalar.activation(h_act[:, f % RING, :], psH[f % HB][:, :], ACT.Gelu,
                                         bias=w["b1"][:, f:f + 1]).then_inc(act_ready, 1)
                    eng.wait_ge(act_ready, i * FT + f + 1)
                    nc.scalar.copy(h_hi[:, f, :], h_act[:, f % RING, :]).then_inc(h_hi_ready, 1)
            eng.wait_ge(g.weights[w["sem"]], w["count"])
            for m in range(2):
                if m:
                    eng.wait_ge(abs_ready, 1)
                nc.scalar.activation(absw[:, :], raw[m], ACT.Abs, accum_out=abs_sum[:, m:m + 1]).then_inc(abs_ready, 1)
            round_x(0)
            each_batch(eng, body)

        @block.tensor
        def _(eng):
            def first_product(i, f):
                for c in range(EC):
                    for k, part in enumerate((x_hi, x_lo)):
                        mm = nc.tensor.matmul(psH[f % HB][:, :], W1[:, c, f * P:(f + 1) * P], part[:, c, :],
                                              start=c == 0 and k == 0, stop=c == EC - 1 and k == 1)
                mm.then_inc(h_psum, 1)

            def second_product(i, f):
                eng.wait_ge(h_ready, i * FT + f + 1 + RING)
                for t in range(TT):
                    for part in (h_hi, h_lo):
                        mm = nc.tensor.matmul(psO[t // 2][:, (t % 2) * E:(t % 2 + 1) * E],
                                              part[:, f, t * P:(t + 1) * P], W2[:, f, :],
                                              start=f == 0 and t % 2 == 0 and part is h_hi, stop=f == FT - 1,
                                              skip_group_check=True)
                return mm

            def body(i, more):
                eng.wait_ge(x_ready, i * EC + EC)
                for f in range(FT + AHEAD):
                    if f < FT:
                        first_product(i, f)
                    if f == FT - 2 and more:
                        a.tensor(eng, i + 1)
                    if f == AHEAD:
                        eng.wait_ge(o_taken, i * 2 + 2)
                    if f >= AHEAD:
                        mm = second_product(i, f - AHEAD)
                mm.then_inc(o_psum, 1)

            a.tensor(eng, 0)
            eng.wait_ge(abs_ready, 2)
            eng.wait_ge(ones_ready, 1)
            nc.tensor.matmul(psH[0][:, 0:2], ones[:, :], abs_sum[:, :], start=True, stop=True).then_inc(sum_ready, 1)
            eng.wait_ge(w_ready, 2)
            each_batch(eng, body)


def spiking_mlp(nc, g, tag, w):
    with ExitStack() as ctx:
        s = Common(nc, ctx, g.sems)
        a, z = NormIn(g, s, tag), NormOut(g, s, tag)
        xnT = a.xnT
        HB = 4
        AHEAD = 2
        h = s.sb(tag + "h", [P, FT, T])
        o = s.sb(tag + "o", [P, TT, E])
        psH = [s.ps(tag + f"psH{j}") for j in range(HB)]
        psO = [s.ps(tag + f"psO{j}") for j in range(TT // 2)]
        h_psum = s.sem(tag + "h_psum")
        h_ready = s.sem(tag + "h_ready")
        relu_ready = s.sem(tag + "relu_ready")
        o_psum = s.sem(tag + "o_psum")
        o_taken = s.sem(tag + "o_taken")
        out_ready = s.sem(tag + "out_ready")
        W1, W2 = w["W1"], w["W2"]
        mem = s.sb(tag + "mem", [P, TT * E])
        drive = s.sb(tag + "drive", [P, TT * E])
        spikes = s.sb(tag + "spikes", [P, TT * E])
        h_relu = s.sb(tag + "h_relu", [P, 2, T])
        neuron = s.sem(tag + "neuron")
        NEURON_OPS = 13
        block = ctx.enter_context(nc.Block())

        def half_bank(t):
            return psO[t // 2][:, (t % 2) * E:(t % 2 + 1) * E]

        @block.vector
        def _(eng):
            ve = nc.vector

            def leak_and_fire(i):
                at = [0]

                def chained(ins):
                    at[0] += 1
                    ins.then_inc(neuron, 1)

                def settle():
                    eng.wait_ge(neuron, i * NEURON_OPS + at[0])
                eng.wait_ge(o_taken, i * 2 + 4)
                chained(ve.tensor_scalar(spikes[:, :], drive[:, :], 1.0, None, ALU.is_gt))
                chained(ve.scalar_tensor_tensor(mem[:, :], drive[:, :], 0.9, drive[:, :], ALU.mult, ALU.add))
                settle()
                chained(ve.tensor_tensor(mem[:, :], spikes[:, :], mem[:, :], ALU.subtract))
                settle()
                chained(ve.scalar_tensor_tensor(spikes[:, :], mem[:, :], -1.0, spikes[:, :], ALU.is_lt, ALU.add))
                for _ in range(3):
                    chained(ve.scalar_tensor_tensor(o[:, :, :], mem[:, :], 0.9, drive[:, :], ALU.mult,
                                                    ALU.subtract))
                    settle()
                    chained(ve.scalar_tensor_tensor(mem[:, :], mem[:, :], -1.0, o[:, :, :], ALU.is_lt, ALU.add))
                    settle()
                    chained(ve.scalar_tensor_tensor(spikes[:, :], mem[:, :], -1.0, spikes[:, :], ALU.is_lt,
                                                    ALU.add))
                settle()
                assert at[0] == NEURON_OPS
                ve.tensor_scalar(o[:, :, :], spikes[:, :], 0.2, None, ALU.mult).then_inc(out_ready, 1)

            def body(i, more):
                eng.wait_ge(o_psum, i + 1)
                for j in range(2):
                    ve.tensor_copy(drive[:, j * 512:(j + 1) * 512], psO[j][:, :]).then_inc(o_taken, 1)
                if more:
                    a.vector(eng, i + 2)
                leak_and_fire(i)
                z.vector(eng, i, lambda t: o[:, t, :], out_ready, 1)

            ve.memset(xnT[:, :, 0:1], 0.0).then_inc(o_taken, 2)
            a.vector(eng, 0, first=True)
            a.vector(eng, 1)
            each_batch(eng, body, 2)

        @block.sync
        def _(eng):
            g.look_ahead(eng, z)

        @block.gpsimd
        def _(eng):
            def body(i, more):
                if more:
                    a.gpsimd(eng, i + 2)
                z.gpsimd(eng, i)
            z.gpsimd_start(eng)
            a.gpsimd(eng, 0)
            a.gpsimd(eng, 1)
            each_batch(eng, body, 2)

        @block.scalar
        def _(eng):
            def body(i, more):
                for f in range(FT):
                    eng.wait_ge(h_psum, i * FT + f + 1)
                    nc.scalar.activation(h_relu[:, f % 2, :], psH[f % HB][:, :], ACT.Relu).then_inc(relu_ready, 1)
                    eng.wait_ge(relu_ready, i * FT + f + 1)
                    nc.scalar.activation(h[:, f, :], h_relu[:, f % 2, :], ACT.Square).then_inc(h_ready, 1)
                if more:
                    a.scalar(eng, i + 1)
            a.scalar(eng, 0)
            each_batch(eng, body)

        @block.tensor
        def _(eng):
            eng.wait_ge(g.weights[w["sem"]], w["count"])

            def first_product(i, f):
                for c in range(EC):
                    mm = nc.tensor.matmul(psH[f % HB][:, :], W1[:, c, f * P:(f + 1) * P], xnT[:, c, 1:T + 1],
                                          start=c == 0, stop=c == EC - 1)
                mm.then_inc(h_psum, 1)

            def second_product(i, f):
                eng.wait_ge(h_ready, i * FT + f + 1)
                for t in range(TT):
                    mm = nc.tensor.matmul(half_bank(t), h[:, f, t * P:(t + 1) * P], W2[:, f, :],
                                          start=f == 0 and t % 2 == 0, stop=f == FT - 1, skip_group_check=True)
                return mm

            def body(i, more):
                eng.wait_ge(a.ready, i * EC + EC)
                for f in range(FT + AHEAD):
                    if f < FT:
                        first_product(i, f)
                    if f == FT - 1 and more:
                        a.tensor(eng, i + 1)
                    if f == AHEAD:
                        eng.wait_ge(o_taken, i * 2 + 2)
                    if f >= AHEAD:
                        mm = second_product(i, f - AHEAD)
                mm.then_inc(o_psum, 1)

            a.tensor(eng, 0)
            each_batch(eng, body)


HS = 8
DS = 64
NPAIR = HS // 2
TAPS = 4
LEVELS = 7
MASKED = 5


def state_space(nc, g, tag, w):
    with ExitStack() as ctx:
        s = Common(nc, ctx, g.sems)
        o = s.sb(tag + "o", [P, TT, E])
        a, z = NormIn(g, s, tag), NormOut(g, s, tag, y=o)
        xnT, psA = a.xnT, a.psT
        x_pad = s.sb(tag + "x_pad", [P, NPAIR, T + TAPS - 1])
        skip = x_pad[:, :, TAPS - 1:]
        xs = s.sb(tag + "xs", [P, NPAIR, T])
        gate = s.sb(tag + "gate", [P, NPAIR, T])
        Bt = s.sb(tag + "Bt", [P, NPAIR, T])
        Ct = s.sb(tag + "Ct", [P, NPAIR, T])
        dtb = s.sb(tag + "dtb", [P, 2, T])
        prod = s.sb(tag + "prod", [P, 2, T])
        dA = s.sb(tag + "dA", [P, NPAIR, T])
        BT = dA
        tot = [dA] + [s.sb(tag + f"tot{L}", [P, NPAIR, T >> L]) for L in range(1, LEVELS + 1)]
        Cbd = [s.sb(tag + f"Cbd{j}", [P, NPAIR, 2, T // 2]) for j in range(2)]
        ST = s.sb(tag + "ST", [P, 2, TT, 4, P])
        xt = s.sb(tag + "xt", [P, TT, HS * DS])
        h = s.sb(tag + "h", [P, TT - 1, NPAIR, P])
        ysum = s.sb(tag + "ysum", [P, 2, T])
        negA = s.sb(tag + "negA", [P, NPAIR])
        expA = s.sb(tag + "expA", [P, NPAIR])
        dtT = s.sb(tag + "dtT", [P, T])
        small = {k: s.sb(tag + k, [P, TT * HS]) for k in
                 ("raw", "v", "absv", "u", "w1", "ln", "eq", "d", "d2", "rec", "n", "n2", "r", "dt")}
        psL = [s.ps(tag + f"psL{j}") for j in range(4)]
        psY = [s.ps(tag + f"psY{j}") for j in range(2)]
        const = s.sem(tag + "const")
        moved = s.sem(tag + "moved")
        filled = s.sem(tag + "filled")
        dt_chain = s.sem(tag + "dt_chain")
        dt_act = s.sem(tag + "dt_act")
        conv = s.sem(tag + "conv")
        xs_ready = s.sem(tag + "xs_ready")
        b_scaled = s.sem(tag + "b_scaled")
        dtb_ready = s.sem(tag + "dtb_ready")
        prod_ready = s.sem(tag + "prod_ready")
        skip_ready = s.sem(tag + "skip_ready")
        c_ready = s.sem(tag + "c_ready")
        b_ready = s.sem(tag + "b_ready")
        tot_ready = s.sem(tag + "tot_ready")
        cbd_ready = s.sem(tag + "cbd_ready")
        l_psum = s.sem(tag + "l_psum")
        placed = s.sem(tag + "placed")
        copied = s.sem(tag + "copied")
        bT_psum = s.sem(tag + "bT_psum")
        bT_ready = s.sem(tag + "bT_ready")
        h_psum = s.sem(tag + "h_psum")
        h_ready = s.sem(tag + "h_ready")
        y_psum = s.sem(tag + "y_psum")
        ysum_ready = s.sem(tag + "ysum_ready")
        y_ready = s.sem(tag + "y_ready")
        DT, X, B, DTT, DTB, C, Z, G, XT, OUT, MOVES = 0, 1, 5, 9, 10, 11, 18, 19, 26, 30, 32
        block = ctx.enter_context(nc.Block())

        def blocks(v, m):
            return v.rearrange("p a (k e m) -> p a k e m", e=2, m=m)

        def pairs(tile, k):
            return tile[:, 2 * k:2 * k + 2, :]

        @block.vector
        def _(eng):
            ve = nc.vector

            def step_sizes(i):
                S = small
                n = [0]

                def link(ins):
                    n[0] += 1
                    ins.then_inc(dt_chain, 1)

                def settle():
                    eng.wait_ge(dt_chain, i * 11 + n[0])
                eng.wait_ge(moved, i * MOVES + DT + 1)
                link(ve.tensor_tensor(S["v"][:, :], S["raw"][:, :], w["dt_bias"][:, :], ALU.add))
                settle()
                link(ve.scalar_tensor_tensor(S["absv"][:, :], S["v"][:, :], -1.0, S["v"][:, :], ALU.mult, ALU.max))
                eng.wait_ge(dt_act, i * 2 + 1)
                link(ve.tensor_scalar_add(S["w1"][:, :], S["u"][:, :], 1.0))
                settle()
                link(ve.tensor_scalar(S["eq"][:, :], S["w1"][:, :], 1.0, None, ALU.is_equal))
                link(ve.tensor_scalar_add(S["d"][:, :], S["w1"][:, :], -1.0))
                settle()
                link(ve.tensor_tensor(S["d2"][:, :], S["d"][:, :], S["eq"][:, :], ALU.add))
                settle()
                link(ve.reciprocal(S["rec"][:, :], S["d2"][:, :]))
                eng.wait_ge(dt_act, i * 2 + 2)
                link(ve.tensor_tensor(S["n"][:, :], S["ln"][:, :], S["eq"][:, :], ALU.add))
                settle()
                link(ve.tensor_tensor(S["n2"][:, :], S["n"][:, :], S["u"][:, :], ALU.mult))
                settle()
                link(ve.tensor_tensor(S["r"][:, :], S["n2"][:, :], S["rec"][:, :], ALU.mult))
                settle()
                link(ve.scalar_tensor_tensor(S["dt"][:, :], S["v"][:, :], 0.0, S["r"][:, :], ALU.max, ALU.add))
                assert n[0] == 11

            def convolve(i):
                for k in range(TAPS):
                    for j in range(NPAIR):
                        if k == 0:
                            eng.wait_ge(moved, i * MOVES + X + j + 1)
                            ve.tensor_scalar(xs[:, j, :], x_pad[:, j, 0:T], w["conv_w"][:, j * TAPS:j * TAPS + 1],
                                             None, ALU.mult).then_inc(conv, 1)
                        else:
                            eng.wait_ge(conv, i * 16 + (k - 1) * NPAIR + j + 1)
                            ve.scalar_tensor_tensor(xs[:, j, :], x_pad[:, j, k:k + T],
                                                    w["conv_w"][:, j * TAPS + k:j * TAPS + k + 1], xs[:, j, :],
                                                    ALU.mult, ALU.add).then_inc(conv, 1)

            def update(i, L, k):
                if L == 0:
                    eng.wait_ge(prod_ready, i * NPAIR + 2 * k + 2)
                    ve.tensor_tensor(pairs(Ct, k), pairs(Ct, k), pairs(dA, k), ALU.mult).then_inc(c_ready, 1)
                    return
                m = 1 << (L - 1)
                t = tot[L - 1][:, 2 * k:2 * k + 2, :].rearrange("p a (k e) -> p a k e", e=2)
                eng.wait_ge(cbd_ready, i * 28 + 4 * (L - 1) + 2 * k + 2)
                eng.wait_ge(c_ready, i * 16 + 2 * (L - 1) + k + 1)
                if L > 1:
                    eng.wait_ge(tot_ready, i * 14 + 2 * (L - 2) + k + 1)
                c = blocks(pairs(Ct, k), m)[:, :, :, 1, :]
                ve.tensor_tensor(c, c, t[:, :, :, 0:1].to_broadcast([P, 2, T // (2 * m), m]),
                                 ALU.mult).then_inc(c_ready, 1)
                ve.tensor_tensor(tot[L][:, 2 * k:2 * k + 2, :], t[:, :, :, 0], t[:, :, :, 1],
                                 ALU.mult).then_inc(tot_ready, 1)

            def place(i, L, k):
                m = 1 << L
                for half in range(2):
                    wait_apart(g, eng, l_psum, i * 28 + 4 * L + 2 * k + half + 1)
                    out = ST[:, k, 2 * half:2 * half + 2, :, :].rearrange("p q h (b e m) -> p (q h) b e m", e=2, m=m)
                    mask = w["masks"][:, L * 64:(L + 1) * 64].bitcast(mybir.dt.uint32)
                    mask = mask.rearrange("p (b m) -> p b m", m=m).unsqueeze(1).to_broadcast([P, 8, 64 // m, m])
                    data = psL[2 * k + half][:, :].rearrange("p (h b m) -> p h b m", h=8, m=m)
                    ve.copy_predicated(out[:, :, :, 1, :], mask, data).then_inc(placed, 1)

            def states(i):
                eng.wait_ge(tot_ready, i * 14 + 14)
                for q in range(TT - 1):
                    eng.wait_ge(h_psum, i * 3 + q + 1)
                    if q:
                        eng.wait_ge(h_ready, i * 3 + q)
                    for p in range(NPAIR):
                        for b in range(2):
                            r = slice(b * DS, (b + 1) * DS)
                            new = psL[q][r, p * P + b * DS:p * P + (b + 1) * DS]
                            out = h[r, q, p, b * DS:(b + 1) * DS]
                            if q:
                                ins = ve.scalar_tensor_tensor(out, h[r, q - 1, p, b * DS:(b + 1) * DS],
                                                              tot[LEVELS][r, p, q:q + 1], new, ALU.mult, ALU.add)
                            else:
                                ins = ve.tensor_copy(out, new)
                    ins.then_inc(h_ready, 1)

            def body(i, more):
                step_sizes(i)
                convolve(i)
                for k in range(2):
                    update(i, 0, k)
                for L in range(1, LEVELS + 1):
                    for k in range(2):
                        update(i, L, k)
                        if L - 1 < MASKED:
                            place(i, L - 1, k)
                if more:
                    a.vector(eng, i + 1)
                states(i)
                for p in range(NPAIR):
                    eng.wait_ge(y_psum, i * NPAIR + p + 1)
                    eng.wait_ge(skip_ready, i * NPAIR + p + 1)
                    if p >= 2:
                        eng.wait_ge(y_ready, i * NPAIR + p - 1)
                    ve.tensor_tensor(ysum[:, p % 2, :], psY[p % 2][:, :], skip[:, p, :], ALU.add).then_inc(ysum_ready, 1)
                eng.wait_ge(moved, (i + 1) * MOVES)
                z.vector(eng, i, lambda t: o[:, t, :], moved, 0)

            eng.wait_ge(g.weights[w["sem"]], w["count"])
            ve.memset(x_pad[:, :, 0:TAPS - 1], 0.0).then_inc(const, 1)
            for j in range(2):
                ve.memset(Cbd[j][:, :, :, :], 0.0).then_inc(const, 1)
            ve.memset(ST[:, :, :, :, :], 0.0).then_inc(const, 1)
            ve.memset(h[:, :, :, :], 0.0).then_inc(const, 1)
            ve.memset(dtT[:, :], 0.0).then_inc(const, 1)
            ve.memset(xnT[:, :, 0:1], 0.0).then_inc(const, 1)
            eng.wait_ge(const, 8)
            ve.tensor_scalar(negA[:, :], expA[:, :], -1.0, None, ALU.mult).then_inc(const, 1)
            a.vector(eng, 0, first=True)
            each_batch(eng, body)

        @block.sync
        def _(eng):
            g.look_ahead(eng, z)

        @block.gpsimd
        def _(eng):
            gp = nc.gpsimd

            def body(i, more):
                for p in range(NPAIR):
                    eng.wait_ge(dtb_ready, i * NPAIR + p + 1)
                    eng.wait_ge(moved, i * MOVES + B + p + 1)
                    gp.tensor_tensor(Bt[:, p, :], Bt[:, p, :], dtb[:, p % 2, :], ALU.mult).then_inc(b_scaled, 1)
                    eng.wait_ge(b_scaled, i * NPAIR + p + 1)
                    eng.wait_ge(moved, i * MOVES + C + 2 * p + 1)
                    if p >= 2:
                        eng.wait_ge(filled, i * MOVES + G + 2 * (p - 2) + 1)
                    gp.tensor_tensor(prod[:, p % 2, :], Bt[:, p, :], Ct[:, p, :], ALU.mult).then_inc(prod_ready, 1)
                for L in range(1, LEVELS + 1):
                    m = 1 << (L - 1)
                    for k in range(2):
                        eng.wait_ge(l_psum, i * 28 + 4 * (L - 1) + 2 * k + 2)
                        if L > 1:
                            eng.wait_ge(tot_ready, i * 14 + 2 * (L - 2) + k + 1)
                            eng.wait_ge(b_ready, i * 14 + 2 * (L - 2) + k + 1)
                        t = tot[L - 1][:, 2 * k:2 * k + 2, :].rearrange("p a (k e) -> p a k e", e=2)
                        b = blocks(pairs(Bt, k), m)[:, :, :, 0, :]
                        gp.tensor_tensor(b, b, t[:, :, :, 1:2].to_broadcast([P, 2, T // (2 * m), m]),
                                         ALU.mult).then_inc(b_ready, 1)
                    if 0 <= L - 2 < NPAIR:
                        p = L - 2
                        eng.wait_ge(moved, i * MOVES + G + 2 * p + 1)
                        eng.wait_ge(xs_ready, i * NPAIR + p + 1)
                        gp.tensor_tensor(skip[:, p, :], skip[:, p, :], xs[:, p, :], ALU.mult).then_inc(skip_ready, 1)
                if more:
                    a.gpsimd(eng, i + 1)
                for p in range(NPAIR):
                    eng.wait_ge(ysum_ready, i * NPAIR + p + 1)
                    gp.tensor_tensor(gate[:, p, :], gate[:, p, :], ysum[:, p % 2, :], ALU.mult).then_inc(y_ready, 1)
                z.gpsimd(eng, i)
            eng.wait_ge(const, 9)
            z.gpsimd_start(eng)
            a.gpsimd(eng, 0)
            each_batch(eng, body)

        @block.scalar
        def _(eng):
            sc = nc.scalar

            def take(i, use):
                eng.wait_ge(filled, i * MOVES + use + 1)
                return psA[use % 2]

            def block_diagonal(i, L, k):
                m = 1 << L
                if L >= 2:
                    eng.wait_ge(l_psum, i * 28 + 4 * (L - 2) + 2 * k + 2)
                eng.wait_ge(c_ready, i * 16 + 2 * L + k + 1)
                for b in range(2):
                    r = slice(b * DS, (b + 1) * DS)
                    sc.copy(Cbd[L % 2][r, 2 * k:2 * k + 2, b, :].rearrange("p a (k m) -> p a k m", m=m),
                            blocks(Ct[r, 2 * k:2 * k + 2, :], m)[:, :, :, 1, :]).then_inc(cbd_ready, 1)

            def copy_scores(i, L, k):
                for half in range(2):
                    eng.wait_ge(l_psum, i * 28 + 4 * L + 2 * k + half + 1)
                    ps = psL[2 * k + half][:, :].rearrange("p (h n) -> p h n", h=8)
                    out = ST[:, k, 2 * half:2 * half + 2, :, :].rearrange("p q h n -> p (q h) n")
                    m = 1 << L
                    for j in range(64 // m):
                        r = slice(2 * m * j, 2 * m * j + m)
                        sc.copy(out[r, :, (2 * j + 1) * m:(2 * j + 2) * m],
                                ps[r, :, j * m:(j + 1) * m]).then_inc(copied, 1)

            def body(i, more):
                S = small
                sc.copy(S["raw"][:, :], take(i, DT)[:, 0:TT * HS]).then_inc(moved, 1)
                sc.copy(x_pad[:, 0, TAPS - 1:], take(i, X)[:, :]).then_inc(moved, 1)
                eng.wait_ge(dt_chain, i * 11 + 2)
                sc.activation(S["u"][:, :], S["absv"][:, :], ACT.Exp, scale=-1.0).then_inc(dt_act, 1)
                for j in range(1, NPAIR):
                    sc.copy(x_pad[:, j, TAPS - 1:], take(i, X + j)[:, :]).then_inc(moved, 1)
                eng.wait_ge(dt_chain, i * 11 + 3)
                sc.activation(S["ln"][:, :], S["w1"][:, :], ACT.Ln).then_inc(dt_act, 1)
                for p in range(NPAIR):
                    sc.copy(Bt[:, p, :], take(i, B + p)[:, :]).then_inc(moved, 1)
                sc.copy(dtT[0:HS, :], take(i, DTT)[0:HS, :]).then_inc(moved, 1)
                for p in range(NPAIR):
                    ps = take(i, DTB + 2 * p)
                    if p >= 2:
                        eng.wait_ge(b_scaled, i * NPAIR + p - 1)
                    sc.copy(dtb[:, p % 2, :], ps[:, :]).then_inc(dtb_ready, 1)
                    sc.activation(dA[:, p, :], ps[:, :], ACT.Exp, scale=negA[:, p:p + 1]).then_inc(moved, 1)
                    sc.copy(Ct[:, p, :], take(i, C + 2 * p)[:, :]).then_inc(moved, 1)
                for p in range(NPAIR):
                    sc.activation(gate[:, p, :], take(i, Z + 2 * p)[:, :], ACT.Silu).then_inc(moved, 1)
                    ps = take(i, G + 2 * p)
                    eng.wait_ge(conv, i * 16 + 3 * NPAIR + p + 1)
                    sc.activation(skip[:, p, :], ps[:, :], ACT.Identity, bias=w["D"][:, p:p + 1]).then_inc(moved, 1)
                for k in range(2):
                    block_diagonal(i, 0, k)
                for k in range(2):
                    block_diagonal(i, 1, k)
                for j in range(NPAIR):
                    eng.wait_ge(conv, i * 16 + 3 * NPAIR + j + 1)
                    sc.activation(xs[:, j, :], xs[:, j, :], ACT.Silu, bias=w["conv_b"][:, j:j + 1]).then_inc(xs_ready, 1)
                for L in range(2, LEVELS):
                    for k in range(2):
                        block_diagonal(i, L, k)
                        if L - 1 >= MASKED:
                            copy_scores(i, L - 1, k)
                    if L - 2 < TT:
                        sc.copy(xt[:, L - 2, :], take(i, XT + L - 2)[:, :]).then_inc(moved, 1)
                for k in range(2):
                    copy_scores(i, LEVELS - 1, k)
                for q in range(TT):
                    eng.wait_ge(bT_psum, i * TT + q + 1)
                    sc.copy(BT[:, q, :], psL[q][:, :]).then_inc(bT_ready, 1)
                if more:
                    a.scalar(eng, i + 1)
                z.free(eng, i)
                for j in range(2):
                    sc.copy(o[:, 2 * j:2 * j + 2, :], take(i, OUT + j)[:, :]).then_inc(moved, 1)
            eng.wait_ge(g.weights[w["sem"]], w["count"])
            sc.activation(expA[:, :], w["A_log"][:, :], ACT.Exp).then_inc(const, 1)
            eng.wait_ge(const, 9)
            a.scalar(eng, 0)
            each_batch(eng, body)

        @block.tensor
        def _(eng):
            te = nc.tensor
            eng.wait_ge(const, 9)

            def bank(i, use):
                if use >= 2:
                    eng.wait_ge(moved, i * MOVES + use - 1)
                return psA[use % 2]

            def rows(i, use, cols):
                ps = bank(i, use)
                for c in range(EC):
                    mm = te.matmul(ps[:, :], w["W_in"][:, c, cols:cols + P], xnT[:, c, 1:T + 1],
                                   start=c == 0, stop=c == EC - 1)
                mm.then_inc(filled, 1)

            def level(i, L, k):
                eng.wait_ge(cbd_ready, i * 28 + 4 * L + 2 * k + 2)
                if L:
                    eng.wait_ge(b_ready, i * 14 + 2 * (L - 1) + k + 1)
                    if L - 1 < MASKED:
                        eng.wait_ge(placed, i * 20 + 4 * (L - 1) + 2 * k + 2)
                    else:
                        eng.wait_ge(copied, i * 12 + 4 * k + 4)
                for half in range(2):
                    for q in range(2 * half, 2 * half + 2):
                        for p in range(2 * k, 2 * k + 2):
                            at = (q % 2) * 256 + (p % 2) * P
                            mm = te.matmul(psL[2 * k + half][:, at:at + P], Bt[:, p, q * P:(q + 1) * P],
                                           Cbd[L % 2][:, p, :, q * 64:(q + 1) * 64], start=True, stop=True,
                                           skip_group_check=True)
                    mm.then_inc(l_psum, 1)

            def body(i, more):
                eng.wait_ge(a.ready, i * EC + EC)
                ps = bank(i, DT)
                for t in range(TT):
                    for c in range(EC):
                        mm = te.matmul(ps[:, t * HS:(t + 1) * HS], xnT[:, c, 1 + t * P:1 + (t + 1) * P],
                                       w["W_in"][:, c, 2048:2048 + HS], start=c == 0, stop=c == EC - 1)
                mm.then_inc(filled, 1)
                for j in range(NPAIR):
                    rows(i, X + j, j * P)
                for p in range(NPAIR):
                    rows(i, B + p, 1024 + p * P)
                eng.wait_ge(dt_chain, i * 11 + 11)
                ps = bank(i, DTT)
                for t in range(TT):
                    mm = te.transpose(ps[0:HS, t * P:(t + 1) * P], small["dt"][:, t * HS:(t + 1) * HS], g.ident[:, :])
                mm.then_inc(filled, 1)
                eng.wait_ge(moved, i * MOVES + DTT + 1)
                for p in range(NPAIR):
                    te.matmul(bank(i, DTB + 2 * p)[:, :], w["onehot"][:, p * P:(p + 1) * P], dtT[:, :],
                              start=True, stop=True).then_inc(filled, 1)
                    rows(i, C + 2 * p, 1536 + p * P)
                for p in range(NPAIR):
                    rows(i, Z + 2 * p, 512 + p * P)
                    eng.wait_ge(prod_ready, i * NPAIR + p + 1)
                    te.matmul(bank(i, G + 2 * p)[:, :], w["same_head"][:, :], prod[:, p % 2, :],
                              start=True, stop=True).then_inc(filled, 1)
                for k in range(2):
                    level(i, 0, k)
                for L in range(1, LEVELS):
                    for k in range(2):
                        level(i, L, k)
                    if L <= TT:
                        t = L - 1
                        ps = bank(i, XT + t)
                        if t == 0:
                            eng.wait_ge(xs_ready, i * NPAIR + NPAIR)
                        for j in range(NPAIR):
                            mm = te.transpose(ps[:, j * P:(j + 1) * P], xs[:, j, t * P:(t + 1) * P], g.ident[:, :])
                        mm.then_inc(filled, 1)
                eng.wait_ge(b_ready, i * 14 + 14)
                eng.wait_ge(copied, i * 12 + 12)
                for q in range(TT):
                    for p in range(NPAIR):
                        mm = te.transpose(psL[q][:, p * P:(p + 1) * P], Bt[:, p, q * P:(q + 1) * P], g.ident[:, :])
                    mm.then_inc(bT_psum, 1)
                eng.wait_ge(moved, i * MOVES + XT + TT)
                for q in range(TT - 1):
                    eng.wait_ge(bT_ready, i * TT + q + 1)
                    for p in range(NPAIR):
                        mm = te.matmul(psL[q][:, p * P:(p + 1) * P], BT[:, q, p * P:(p + 1) * P],
                                       xt[:, q, p * P:(p + 1) * P], start=True, stop=True, skip_group_check=True)
                    mm.then_inc(h_psum, 1)
                if more:
                    a.tensor(eng, i + 1)
                eng.wait_ge(c_ready, i * 16 + 16)
                for p in range(NPAIR):
                    if p >= 2:
                        eng.wait_ge(ysum_ready, i * NPAIR + p - 1)
                    for q in range(TT):
                        ps = psY[p % 2][:, q * P:(q + 1) * P]
                        for b in range(2):
                            hd = 2 * p + b
                            mm = te.matmul(ps[b * DS:(b + 1) * DS, :], xt[:, q, hd * DS:(hd + 1) * DS],
                                           ST[:, hd // 4, q, hd % 4, :], start=True, stop=q == 0,
                                           skip_group_check=True)
                        if q:
                            eng.wait_ge(h_ready, i * 3 + q)
                            mm = te.matmul(ps, h[:, q - 1, p, :], Ct[:, p, q * P:(q + 1) * P],
                                           start=False, stop=True, skip_group_check=True)
                    mm.then_inc(y_psum, 1)
                if more:
                    eng.wait_ge(a.ready, i * EC + 2 * EC)
                for t in range(TT):
                    if t % 2 == 0:
                        ps = bank(i, OUT + t // 2)
                    for p in range(NPAIR):
                        eng.wait_ge(y_ready, i * NPAIR + p + 1)
                        mm = te.matmul(ps[:, (t % 2) * E:(t % 2 + 1) * E], gate[:, p, t * P:(t + 1) * P],
                                       w["W_out"][:, p, :], start=p == 0, stop=p == NPAIR - 1)
                    if t % 2:
                        mm.then_inc(filled, 1)
                eng.wait_ge(moved, (i + 1) * MOVES)
            a.tensor(eng, 0)
            each_batch(eng, body)


def rwkv_mix(nc, g, tag, w):
    with ExitStack() as ctx:
        s = Common(nc, ctx, g.sems)
        a, z = NormIn(g, s, tag), NormOut(g, s, tag)
        xnT = a.xnT
        diff = s.sb(tag + "diff", [P, EC, T])
        xr = s.sb(tag + "xr", [P, EC, T])
        xk = s.sb(tag + "xk", [P, EC, T])
        r = s.sb(tag + "r", [P, TT, E])
        k_relu = s.sb(tag + "k_relu", [P, EC, T])
        k_act = s.sb(tag + "k_act", [P, EC, T])
        gated = s.sb(tag + "gated", [P, TT, E])
        psR = [s.ps(tag + f"psR{j}") for j in range(TT // 2)]
        psK = [s.ps(tag + f"psK{f}") for f in range(EC)]
        psO = [s.ps(tag + f"psO{j}") for j in range(TT // 2)]
        zeroed = s.sem(tag + "zeroed")
        diff_ready = s.sem(tag + "diff_ready")
        xr_ready = s.sem(tag + "xr_ready")
        xk_ready = s.sem(tag + "xk_ready")
        r_psum = s.sem(tag + "r_psum")
        r_ready = s.sem(tag + "r_ready")
        k_psum = s.sem(tag + "k_psum")
        relu_ready = s.sem(tag + "relu_ready")
        k_ready = s.sem(tag + "k_ready")
        o_psum = s.sem(tag + "o_psum")
        gated_ready = s.sem(tag + "gated_ready")
        block = ctx.enter_context(nc.Block())

        def half(ps, t):
            return ps[t // 2][:, (t % 2) * E:(t % 2 + 1) * E]

        @block.vector
        def _(eng):
            ve = nc.vector

            def difference(n):
                for c in range(EC):
                    eng.wait_ge(a.ready, n * EC + c + 1)
                    ve.tensor_tensor(diff[:, c, :], xnT[:, c, 1:T + 1], xnT[:, c, 0:T],
                                     ALU.subtract).then_inc(diff_ready, 1)

            def mix(n, out, mu, ready):
                for c in range(EC):
                    eng.wait_ge(diff_ready, n * EC + c + 1)
                    ve.scalar_tensor_tensor(out[:, c, :], diff[:, c, :], mu[:, c:c + 1], xnT[:, c, 0:T],
                                            ALU.mult, ALU.add).then_inc(ready, 1)

            def body(i, more, two_more=False):
                if more:
                    difference(i + 1)
                    if two_more:
                        a.statistics(eng, i + 2)
                    eng.wait_ge(r_psum, i * 2 + 2)
                    mix(i + 1, xr, w["mu_r"], xr_ready)
                if two_more:
                    a.normalise(eng, i + 2)
                if more:
                    eng.wait_ge(k_psum, i * EC + EC)
                    mix(i + 1, xk, w["mu_k"], xk_ready)
                eng.wait_ge(r_ready, i * 2 + 2)
                z.free(eng, i)
                for j in range(2):
                    eng.wait_ge(o_psum, i * 2 + j + 1)
                    ve.tensor_tensor(gated[:, 2 * j:2 * j + 2, :], psO[j][:, :], r[:, 2 * j:2 * j + 2, :],
                                     ALU.mult).then_inc(gated_ready, 1)
                z.vector(eng, i, lambda t: gated[:, t, :], gated_ready, 2)

            ve.memset(xnT[:, :, 0:1], 0.0).then_inc(zeroed, 1)
            eng.wait_ge(g.weights[w["sem"]], w["count"])
            eng.wait_ge(zeroed, 1)
            a.vector(eng, 0, first=True)
            difference(0)
            mix(0, xr, w["mu_r"], xr_ready)
            mix(0, xk, w["mu_k"], xk_ready)
            a.vector(eng, 1)
            with eng.Fori(0, NB - 2) as i:
                body(i, True, True)
            body(NB - 2, True)
            body(NB - 1, False)

        @block.sync
        def _(eng):
            g.look_ahead(eng, z)

        @block.gpsimd
        def _(eng):
            def body(i, more):
                if more:
                    a.gpsimd(eng, i + 2)
                z.gpsimd(eng, i)
            z.gpsimd_start(eng)
            a.gpsimd(eng, 0)
            a.gpsimd(eng, 1)
            each_batch(eng, body, 2)

        @block.scalar
        def _(eng):
            def body(i, more):
                if more:
                    a.scalar(eng, i + 1)
                for j in range(2):
                    eng.wait_ge(r_psum, i * 2 + j + 1)
                    nc.scalar.activation(r[:, 2 * j:2 * j + 2, :], psR[j][:, :], ACT.Sigmoid).then_inc(r_ready, 1)
                for f in range(EC):
                    eng.wait_ge(k_psum, i * EC + f + 1)
                    nc.scalar.activation(k_relu[:, f, :], psK[f][:, :], ACT.Relu).then_inc(relu_ready, 1)
                    eng.wait_ge(relu_ready, i * EC + f + 1)
                    nc.scalar.activation(k_act[:, f, :], k_relu[:, f, :], ACT.Square).then_inc(k_ready, 1)
                eng.wait_ge(gated_ready, i * 2 + 2)
                if more:
                    eng.wait_ge(xk_ready, i * EC + 2 * EC)
            a.scalar(eng, 0)
            each_batch(eng, body)

        @block.tensor
        def _(eng):
            eng.wait_ge(g.weights[w["sem"]], w["count"])

            def body(i, more):
                if more:
                    a.tensor(eng, i + 1)
                eng.wait_ge(xr_ready, i * EC + EC)
                for t in range(TT):
                    for c in range(EC):
                        mm = nc.tensor.matmul(half(psR, t), xr[:, c, t * P:(t + 1) * P], w["W_r"][:, c, :],
                                              start=c == 0, stop=c == EC - 1)
                    if t % 2:
                        mm.then_inc(r_psum, 1)
                eng.wait_ge(xk_ready, i * EC + EC)
                for f in range(EC):
                    for c in range(EC):
                        mm = nc.tensor.matmul(psK[f][:, :], w["W_k"][:, c, f * P:(f + 1) * P], xk[:, c, :],
                                              start=c == 0, stop=c == EC - 1)
                    mm.then_inc(k_psum, 1)
                eng.wait_ge(k_ready, i * EC + EC)
                eng.wait_ge(r_ready, i * 2 + 2)
                for t in range(TT):
                    for f in range(EC):
                        mm = nc.tensor.matmul(half(psO, t), k_act[:, f, t * P:(t + 1) * P], w["W_v"][:, f, :],
                                              start=f == 0, stop=f == EC - 1)
                    if t % 2:
                        mm.then_inc(o_psum, 1)
            a.tensor(eng, 0)
            each_batch(eng, body)


H2 = 16
D2 = E // H2
G2 = 4
NG2 = H2 // G2
SLOT = 64
T_COL = {3: (0, 512), 2: (512, 384), 0: (896, 128), 1: (1024, 256)}
WCOLS = 1280


def distance_attention(nc, g, tag, w):
    with ExitStack() as ctx:
        s = Common(nc, ctx, g.sems)
        o = s.sb(tag + "o", [P, TT, E])
        a, z = NormIn(g, s, tag), NormOut(g, s, tag, y=o)
        xnT = a.xnT
        hi = [s.sb(tag + f"hi{j}", [P, EC, T], F32R) for j in range(2)]
        lo = [s.sb(tag + f"lo{j}", [P, EC, T], F32R) for j in range(2)]
        sq_hi = [s.sb(tag + f"sq_hi{j}", [P, EC, T], F32R) for j in range(2)]
        sq_lo = [s.sb(tag + f"sq_lo{j}", [P, EC, T], F32R) for j in range(2)]
        round_hi = s.sb(tag + "round_hi", [P, 2, T], F32R)
        aug = [s.sb(tag + f"aug{j}", [P, 4, T], F32R) for j in range(2)]
        v_pad = s.sb(tag + "v_pad", [P, TT, H2, 2 * D2])
        wts = s.sb(tag + "wts", [P, 2, G2, WCOLS])
        sq = s.sb(tag + "sq", [P, EC, T])
        ctxT = s.sb(tag + "ctxT", [P, NG2, T])
        select = s.sb(tag + "select", [P, 12 * P], F32R)
        decay = s.sb(tag + "decay", [P, H2])
        psA = a.psT
        psS = [s.ps(tag + f"psS{j}") for j in range(4)]
        psC = [s.ps(tag + f"psC{j}") for j in range(2)]
        const = s.sem(tag + "const")
        qk_psum = s.sem(tag + "qk_psum")
        hi_ready = s.sem(tag + "hi_ready")
        lo_ready = s.sem(tag + "lo_ready")
        sq_ready = s.sem(tag + "sq_ready")
        sq_hi_ready = s.sem(tag + "sq_hi_ready")
        sq_lo_ready = s.sem(tag + "sq_lo_ready")
        rep_psum = s.sem(tag + "rep_psum")
        round_ready = s.sem(tag + "round_ready")
        aug_ready = s.sem(tag + "aug_ready")
        v_psum = s.sem(tag + "v_psum")
        v_ready = s.sem(tag + "v_ready")
        s_psum = s.sem(tag + "s_psum")
        dist_ready = s.sem(tag + "dist_ready")
        exp_ready = s.sem(tag + "exp_ready")
        masked = s.sem(tag + "masked")
        ctx_psum = s.sem(tag + "ctx_psum")
        ctx_ready = s.sem(tag + "ctx_ready")
        o_psum = s.sem(tag + "o_psum")
        o_ready = s.sem(tag + "o_ready")
        block = ctx.enter_context(nc.Block())
        REGIONS = [(3,), (2, 0), (1,)]
        SPLIT_X, SPLIT_Q, SPLIT_K = H2 - 4, H2 - 3, H2 - 2

        def cols(t):
            return slice(T_COL[t][0], T_COL[t][0] + T_COL[t][1])

        def region(j):
            return slice(T_COL[REGIONS[j][0]][0], T_COL[REGIONS[j][-1]][0] + T_COL[REGIONS[j][-1]][1])

        @block.vector
        def _(eng):
            ve = nc.vector

            def parts(i, side):
                for c in range(EC):
                    n = i * 4 + 2 * side + c
                    eng.wait_ge(sq_ready, n + 1)
                    ve.scalar_tensor_tensor(lo[side][:, c, :], psA[c][:, :], 1.0 - 3.0 * side,
                                            hi[side][:, c, :].bitcast(F32), ALU.mult, ALU.subtract).then_inc(lo_ready, 1)
                for c in range(EC):
                    n = i * 4 + 2 * side + c
                    eng.wait_ge(sq_hi_ready, n + 1)
                    ve.tensor_tensor(sq_lo[side][:, c, :], sq[:, c, :], sq_hi[side][:, c, :].bitcast(F32),
                                     ALU.subtract).then_inc(sq_lo_ready, 1)

            def augment(i, r):
                side, at = (r // 2) % 2, 2 * ((r // 4) % 2) + r % 2
                eng.wait_ge(round_ready, i * 16 + r + 1)
                ve.scalar_tensor_tensor(aug[side][:, at, :], round_hi[:, r % 2, :].bitcast(F32),
                                        w["rows"][:, side:side + 1], psA[r % 2][:, :],
                                        ALU.mult, ALU.add).then_inc(aug_ready, 1)

            def distances(i, h):
                for j in range(3):
                    r = 3 * h + j
                    eng.wait_ge(s_psum, i * 48 + r + 1)
                    width = region(j).stop - region(j).start
                    ve.tensor_scalar(wts[:, (h // G2) % 2, h % G2, region(j)], psS[r % 4][:, 0:width], 0.0, None,
                                     ALU.max).then_inc(dist_ready, 1)

            def body(i, more, two_more=False):
                for h in range(H2):
                    if h % G2 == 0 and h // G2 >= 2:
                        eng.wait_ge(ctx_psum, i * 4 + h // G2 - 1)
                    distances(i, h)
                    if h < H2 - G2:
                        augment(i, G2 + h)
                    elif more and h in (SPLIT_Q, SPLIT_K):
                        parts(i + 1, h - SPLIT_Q)
                if more:
                    for r in range(G2):
                        augment(i + 1, r)
                if two_more:
                    a.vector(eng, i + 2)
                z.vector(eng, i, lambda t: o[:, t, :], o_ready, 2)

            eng.wait_ge(g.weights[w["sem"]], w["count"])
            ve.tensor_copy(select[:, :], w["select"]).then_inc(const, 1)
            ve.tensor_scalar(decay[:, :], w["gamma"][:, :], -float(D2) ** -0.5, None, ALU.mult).then_inc(const, 1)
            ve.memset(v_pad[:, :, :, :], 0.0).then_inc(const, 1)
            ve.memset(xnT[:, :, 0:1], 0.0).then_inc(const, 1)
            a.vector(eng, 0, first=True)
            for side in range(2):
                parts(0, side)
            for r in range(G2):
                augment(0, r)
            a.vector(eng, 1)
            with eng.Fori(0, NB - 2) as i:
                body(i, True, True)
            body(NB - 2, True)
            body(NB - 1, False)

        @block.sync
        def _(eng):
            g.look_ahead(eng, z)

        @block.gpsimd
        def _(eng):
            def body(i, more):
                for k in range(NG2):
                    wait_apart(g, eng, exp_ready, i * H2 + G2 * k + G2)
                    for t, n in ((3, 1), (2, 2), (1, 1)):
                        first = T_COL[t][0] + T_COL[t][1] - P
                        v = wts[:, k % 2, :, first:first + n * P]
                        if n == 2:
                            v = v.rearrange("p h (b s) -> p h b s", b=2)
                            pattern = [[0, G2], [0, 2], [-1, P]]
                        else:
                            pattern = [[0, G2], [-1, P]]
                        nc.gpsimd.affine_select(out=v, in_=v, compare_op=ALU.is_gt, fill=0.0, base=0,
                                                pattern=pattern, channel_multiplier=1).then_inc(masked, 1)
                if more:
                    a.gpsimd(eng, i + 2)
                z.gpsimd(eng, i)
            z.gpsimd_start(eng)
            a.gpsimd(eng, 0)
            a.gpsimd(eng, 1)
            each_batch(eng, body, 2)

        @block.scalar
        def _(eng):
            def parts(i, side):
                for c in range(EC):
                    n = i * 4 + 2 * side + c
                    eng.wait_ge(qk_psum, n + 1)
                    nc.scalar.activation(hi[side][:, c, :], psA[c][:, :], ACT.Copy,
                                         scale=1.0 - 3.0 * side).then_inc(hi_ready, 1)
                    if side:
                        eng.wait_ge(sq_lo_ready, i * 4 + c + 1)
                    nc.scalar.activation(sq[:, c, :], psA[c][:, :], ACT.Square).then_inc(sq_ready, 1)
                for c in range(EC):
                    n = i * 4 + 2 * side + c
                    eng.wait_ge(sq_ready, n + 1)
                    nc.scalar.copy(sq_hi[side][:, c, :], sq[:, c, :]).then_inc(sq_hi_ready, 1)

            def rounded(i, r):
                side = (r // 2) % 2
                eng.wait_ge(rep_psum, i * 16 + r + 1)
                nc.scalar.activation(round_hi[:, r % 2, :], psA[r % 2][:, :], ACT.Identity,
                                     bias=w["rows"][:, 2 + side:3 + side]).then_inc(round_ready, 1)

            def body(i, more):
                for j in range(2):
                    eng.wait_ge(v_psum, i * 2 + j + 1)
                    for t in range(2):
                        ins = nc.scalar.copy(v_pad[:, 2 * j + t, :, 0:D2],
                                             psA[j][:, t * E:(t + 1) * E].rearrange("p (h d) -> p h d", d=D2))
                    ins.then_inc(v_ready, 1)
                for h in range(H2):
                    if h < H2 - G2:
                        rounded(i, G2 + h)
                    elif more and h == SPLIT_X:
                        a.scalar(eng, i + 1)
                    elif more and h in (SPLIT_Q, SPLIT_K):
                        parts(i + 1, h - SPLIT_Q)
                    eng.wait_ge(dist_ready, i * 48 + 3 * h + 3)
                    v = wts[:, (h // G2) % 2, h % G2, :]
                    nc.scalar.activation(v, v, ACT.Exp, scale=decay[:, h:h + 1]).then_inc(exp_ready, 1)
                    if h in (9, 13):
                        context(i, (h - 9) // G2)
                context(i, NG2 - 2)
                if more:
                    for r in range(G2):
                        rounded(i + 1, r)
                context(i, NG2 - 1)
                z.free(eng, i)
                for j in range(2):
                    eng.wait_ge(o_psum, i * 2 + j + 1)
                    nc.scalar.copy(o[:, 2 * j:2 * j + 2, :], psA[j][:, :]).then_inc(o_ready, 1)

            def context(i, k):
                eng.wait_ge(ctx_psum, i * NG2 + k + 1)
                nc.scalar.copy(ctxT[:, k, :], psC[k % 2][:, :]).then_inc(ctx_ready, 1)

            eng.wait_ge(g.weights[w["sem"]], w["count"])
            eng.wait_ge(const, 4)
            a.scalar(eng, 0)
            for side in range(2):
                parts(0, side)
            for r in range(G2):
                rounded(0, r)
            each_batch(eng, body)

        @block.tensor
        def _(eng):
            eng.wait_ge(g.weights[w["sem"]], w["count"])
            eng.wait_ge(const, 4)
            te = nc.tensor

            def project(i, side):
                if side:
                    eng.wait_ge(lo_ready, i * 4 + 2)
                W = w["Wk"] if side else w["Wq"]
                for f in range(EC):
                    for c in range(EC):
                        mm = te.matmul(psA[f][:, :], W[:, c, f * P:(f + 1) * P], xnT[:, c, 1:T + 1],
                                       start=c == 0, stop=c == EC - 1)
                    mm.then_inc(qk_psum, 1)

            def replicate(i, r):
                side, p = (r // 2) % 2, 2 * (r // 4) + r % 2
                c, k = divmod(p, 4)
                if r >= 2:
                    eng.wait_ge(aug_ready, i * 16 + r - 1)
                if r == 0:
                    eng.wait_ge(lo_ready, i * 4 + 4)
                    eng.wait_ge(sq_lo_ready, i * 4 + 4)
                place = select[:, k * P:(k + 1) * P]
                norm = select[:, (4 + 4 * side + k) * P:(5 + 4 * side + k) * P]
                te.matmul(psA[r % 2][:, :], place, hi[side][:, c, :], start=True, stop=False)
                te.matmul(psA[r % 2][:, :], place, lo[side][:, c, :], start=False, stop=False)
                te.matmul(psA[r % 2][:, :], norm, sq_hi[side][:, c, :], start=False, stop=False)
                te.matmul(psA[r % 2][:, :], norm, sq_lo[side][:, c, :], start=False, stop=True).then_inc(rep_psum, 1)

            def values(i):
                for t in range(TT):
                    for c in range(EC):
                        mm = te.matmul(psA[t // 2][:, (t % 2) * E:(t % 2 + 1) * E], xnT[:, c, 1 + t * P:1 + (t + 1) * P],
                                       w["Wv"][:, c, :], start=c == 0, stop=c == EC - 1)
                    if t % 2:
                        mm.then_inc(v_psum, 1)

            def scores(i, h):
                base, at = SLOT * (h % 2), 2 * ((h // G2) % 2) + (h // 2) % 2
                if h % G2 == 0:
                    eng.wait_ge(aug_ready, i * 16 + G2 * (h // G2) + G2)
                for j in range(3):
                    r = 3 * h + j
                    if r >= 4:
                        eng.wait_ge(dist_ready, i * 48 + r - 3)
                    for t in REGIONS[j]:
                        first = T_COL[t][0] - region(j).start
                        mm = te.matmul(psS[r % 4][:, first:first + T_COL[t][1]],
                                       aug[1][base:base + SLOT, at, t * P:(t + 1) * P],
                                       aug[0][base:base + SLOT, at, 0:T_COL[t][1]], start=True, stop=True)
                    mm.then_inc(s_psum, 1)

            def contexts(i, k):
                eng.wait_ge(masked, i * 12 + 3 * k + 3)
                if k >= 2:
                    eng.wait_ge(ctx_ready, i * NG2 + k - 1)
                for t in (3, 2, 1, 0):
                    for j in range(G2):
                        mm = te.matmul(psC[k % 2][32 * j:32 * j + 32, 0:T_COL[t][1]], v_pad[:, t, G2 * k + j, :],
                                       wts[:, k % 2, j, cols(t)], start=t == 3, stop=t == 0, skip_group_check=True)
                mm.then_inc(ctx_psum, 1)

            def body(i, more):
                values(i)
                eng.wait_ge(v_ready, i * 2 + 2)
                for h in range(H2):
                    if h < H2 - G2:
                        replicate(i, G2 + h)
                    elif more and h == SPLIT_X:
                        eng.wait_ge(aug_ready, i * 16 + 16)
                        a.tensor(eng, i + 1)
                    elif more and h == SPLIT_Q:
                        eng.wait_ge(a.ready, i * EC + 2 * EC)
                        project(i + 1, 0)
                    elif more and h == SPLIT_K:
                        project(i + 1, 1)
                    scores(i, h)
                    if h % G2 == G2 - 1 and h > G2:
                        contexts(i, h // G2 - 1)
                if more:
                    for r in range(G2):
                        replicate(i + 1, r)
                contexts(i, NG2 - 1)
                eng.wait_ge(ctx_ready, i * NG2 + NG2)
                if more:
                    eng.wait_ge(aug_ready, i * 16 + 16 + G2)
                for t in range(TT):
                    for k in range(NG2):
                        mm = te.matmul(psA[t // 2][:, (t % 2) * E:(t % 2 + 1) * E], ctxT[:, k, t * P:(t + 1) * P],
                                       w["Wo"][:, k, :], start=k == 0, stop=k == NG2 - 1)
                    if t % 2:
                        mm.then_inc(o_psum, 1)
                if more:
                    eng.wait_ge(o_ready, i * 2 + 2)

            a.tensor(eng, 0)
            eng.wait_ge(a.ready, EC)
            for side in range(2):
                project(0, side)
            for r in range(G2):
                replicate(0, r)
            eng.wait_ge(aug_ready, G2)
            each_batch(eng, body)


H3 = 16
D3 = 64
HALF = H3 * D3 // 2
PI_4 = 0.7853981633974483


def angular_attention(nc, g, tag, w):
    with ExitStack() as ctx:
        s = Common(nc, ctx, g.sems)
        a, z = NormIn(g, s, tag), NormOut(g, s, tag)
        xnT = a.xnT
        th = s.sb(tag + "th", [P, TT, 2 * H3])
        trig = s.sb(tag + "trig", [P, 2, TT, 2 * H3])
        cos, sin = trig[:, 0, :, :], trig[:, 1, :, :]
        d1 = s.sb(tag + "d1", [P, TT, H3])
        d2 = s.sb(tag + "d2", [P, TT, H3])
        d3 = s.sb(tag + "d3", [P, TT, H3])
        d4 = s.sb(tag + "d4", [P, TT, H3])
        cos_q = s.sb(tag + "cos_q", [P, TT, H3])
        sin_q = s.sb(tag + "sin_q", [P, TT, H3])
        half_pi = s.sb(tag + "half_pi", [P, 1])
        kv = [s.sb(tag + f"kv{j}", [P, 2, HALF]) for j in range(2)]
        kv_hi = [s.sb(tag + f"kv_hi{j}", [P, 2, 2, HALF], F32R) for j in range(3)]
        kv_lo = [s.sb(tag + f"kv_lo{j}", [P, 2, 2, HALF], F32R) for j in range(3)]
        tri = s.sb(tag + "tri", [P, P], F32R)
        rest = s.sb(tag + "rest", [P, P], F32R)
        wsum = s.sb(tag + "wsum", [P, 2, 2, HALF])
        heads = s.sb(tag + "heads", [P, TT, 2 * HALF])
        headsT = s.sb(tag + "headsT", [P, 2, 8, P])
        o = s.sb(tag + "o", [P, TT, E])
        psC = [s.ps(tag + f"psC{j}") for j in range(4)]
        psV = [s.ps(tag + "psV"), a.psT[0]]
        psQ = s.ps(tag + "psQ")
        const = s.sem(tag + "const")
        qk_psum = s.sem(tag + "qk_psum")
        tanh_ready = s.sem(tag + "tanh_ready")
        trig_ready = s.sem(tag + "trig_ready")
        den_psum = s.sem(tag + "den_psum")
        den = s.sem(tag + "den")
        v_psum = s.sem(tag + "v_psum")
        kv_ready = s.sem(tag + "kv_ready")
        kv_hi_ready = s.sem(tag + "kv_hi_ready")
        kv_lo_ready = s.sem(tag + "kv_lo_ready")
        cum_ready = s.sem(tag + "cum_ready")
        weighted = s.sem(tag + "weighted")
        heads_ready = s.sem(tag + "heads_ready")
        headsT_psum = s.sem(tag + "headsT_psum")
        headsT_ready = s.sem(tag + "headsT_ready")
        o_psum = s.sem(tag + "o_psum")
        o_ready = s.sem(tag + "o_ready")
        W_V, W_O = w["W_V"], w["W_O"]
        block = ctx.enter_context(nc.Block())
        N = 2 * TT

        def per_head(tile, t, half, first):
            v = tile[:, t, first + half * 8:first + half * 8 + 8]
            return v.unsqueeze(2).to_broadcast([P, 8, D3])

        def by_head(v):
            return v.rearrange("p (h d) -> p h d", d=D3)

        @block.vector
        def _(eng):
            ve = nc.vector

            def key_values(i, n):
                t, half = divmod(n, 2)
                eng.wait_ge(v_psum, i * N + n + 1)
                if n >= 2:
                    eng.wait_ge(kv_lo_ready, i * N + n - 1)
                for j, factor in enumerate((cos, sin)):
                    ve.tensor_tensor(by_head(kv[n % 2][:, j, :]), by_head(psV[n % 2][:, :]),
                                     per_head(factor, t, half, H3), ALU.mult).then_inc(kv_ready, 1)

            def weigh(i, n):
                t, half = divmod(n, 2)
                eng.wait_ge(cum_ready, i * N + n + 1)
                if n >= 2:
                    eng.wait_ge(heads_ready, i * N + n - 1)
                for j, factor in enumerate((cos_q, sin_q)):
                    ve.tensor_tensor(by_head(wsum[:, n % 2, j, :]), by_head(psC[2 * half + j][:, :]),
                                     per_head(factor, t, half, 0), ALU.mult).then_inc(weighted, 1)

            def denominators(i):
                eng.wait_ge(den_psum, i + 1)
                sums = psQ[:, 128:256].rearrange("p (t j) -> p t j", t=TT)
                steps = [
                    lambda: ve.tensor_tensor(d1[:, :, :], sums[:, :, 0:H3], cos[:, :, 0:H3], ALU.mult),
                    lambda: ve.tensor_tensor(d2[:, :, :], sums[:, :, H3:2 * H3], sin[:, :, 0:H3], ALU.mult),
                    lambda: ve.tensor_tensor(d3[:, :, :], d1[:, :, :], d2[:, :, :], ALU.add),
                    lambda: ve.tensor_scalar_add(d4[:, :, :], d3[:, :, :], 1e-6),
                    lambda: ve.reciprocal(d1[:, :, :], d4[:, :, :]),
                    lambda: ve.tensor_tensor(cos_q[:, :, :], cos[:, :, 0:H3], d1[:, :, :], ALU.mult),
                    lambda: ve.tensor_tensor(sin_q[:, :, :], sin[:, :, 0:H3], d1[:, :, :], ALU.mult),
                ]
                for k, step in enumerate(steps):
                    if k:
                        eng.wait_ge(den, i * 7 + k)
                    step().then_inc(den, 1)
                eng.wait_ge(den, i * 7 + 7)

            def body(i, more):
                eng.wait_ge(trig_ready, i * 2 + 2)
                for n in range(N):
                    key_values(i, n)
                    if n >= 3:
                        weigh(i, n - 3)
                    if n == 1:
                        denominators(i)
                for n in range(N - 3, N):
                    weigh(i, n)
                if more:
                    a.vector(eng, i + 2)
                z.vector(eng, i, lambda t: o[:, t, :], o_ready, TT)
                eng.wait_ge(heads_ready, i * N + N)
                eng.wait_ge(kv_lo_ready, i * N + N)

            eng.wait_ge(g.weights[w["sem"]], w["count"])
            ve.tensor_copy(tri[:, :], w["tri"]).then_inc(const, 1)
            ve.tensor_copy(rest[:, :], w["rest"]).then_inc(const, 1)
            ve.memset(half_pi[:, :], 2 * PI_4).then_inc(const, 1)
            ve.memset(xnT[:, :, 0:1], 0.0).then_inc(const, 1)
            a.vector(eng, 0, first=True)
            a.vector(eng, 1)
            each_batch(eng, body, 2)

        @block.sync
        def _(eng):
            g.look_ahead(eng, z)

        @block.gpsimd
        def _(eng):
            def rest_of_rounded(i, n):
                t, half = divmod(n, 2)
                eng.wait_ge(kv_hi_ready, i * N + n + 1)
                nc.gpsimd.tensor_tensor(kv_lo[t % 3][:, half, :, :], kv[n % 2][:, :, :],
                                        kv_hi[t % 3][:, half, :, :].bitcast(F32), ALU.subtract).then_inc(kv_lo_ready, 1)

            def add(i, n):
                t, half = divmod(n, 2)
                eng.wait_ge(weighted, i * 2 * N + 2 * n + 2)
                nc.gpsimd.tensor_tensor(heads[:, t, half * HALF:(half + 1) * HALF], wsum[:, n % 2, 0, :],
                                        wsum[:, n % 2, 1, :], ALU.add).then_inc(heads_ready, 1)

            def body(i, more):
                for n in range(N):
                    rest_of_rounded(i, n)
                    if n >= 3:
                        add(i, n - 3)
                for n in range(N - 3, N):
                    add(i, n)
                if more:
                    a.gpsimd(eng, i + 2)
                z.gpsimd(eng, i)
            z.gpsimd_start(eng)
            a.gpsimd(eng, 0)
            a.gpsimd(eng, 1)
            each_batch(eng, body, 2)

        @block.scalar
        def _(eng):
            def trigonometry(n):
                eng.wait_ge(qk_psum, n + 1)
                flat = "p t j -> p (t j)"
                nc.scalar.activation(th[:, :, :].rearrange(flat), psQ[:, 0:128], ACT.Tanh).then_inc(tanh_ready, 1)
                eng.wait_ge(tanh_ready, n + 1)
                nc.scalar.activation(cos[:, :, :], th[:, :, :], ACT.Sin, scale=PI_4,
                                     bias=half_pi[:, 0:1]).then_inc(trig_ready, 1)
                nc.scalar.activation(sin[:, :, :], th[:, :, :], ACT.Sin, scale=PI_4).then_inc(trig_ready, 1)

            def round_parts(i, n):
                t, half = divmod(n, 2)
                eng.wait_ge(kv_ready, i * 2 * N + 2 * n + 2)
                if n >= 6:
                    eng.wait_ge(cum_ready, i * N + n - 3)
                nc.scalar.copy(kv_hi[t % 3][:, half, :, :], kv[n % 2][:, :, :]).then_inc(kv_hi_ready, 1)

            def output(i, t):
                eng.wait_ge(o_psum, i * TT + t + 1)
                nc.scalar.copy(o[:, t, :], psC[t][:, 0:E]).then_inc(o_ready, 1)

            def body(i, more):
                for n in range(N):
                    round_parts(i, n)
                if more:
                    a.scalar(eng, i + 1)
                for t in range(TT):
                    if t == 1 and more:
                        trigonometry(i + 1)
                    if t >= 2:
                        eng.wait_ge(o_psum, i * TT + t - 1)
                    for k in range(2):
                        eng.wait_ge(headsT_psum, i * N + 2 * t + k + 1)
                        nc.scalar.copy(headsT[:, t % 2, 4 * k:4 * k + 4, :], a.psT[k][:, :]).then_inc(headsT_ready, 1)
                    if t:
                        output(i, t - 1)
                output(i, TT - 1)
            eng.wait_ge(const, 4)
            a.scalar(eng, 0)
            trigonometry(0)
            each_batch(eng, body)

        @block.tensor
        def _(eng):
            eng.wait_ge(g.weights[w["sem"]], w["count"])

            def queries_keys(n):
                eng.wait_ge(a.ready, n * EC + EC)
                for t in range(TT):
                    for c in range(EC):
                        mm = nc.tensor.matmul(psQ[:, t * 32:t * 32 + 32], xnT[:, c, 1 + t * P:1 + (t + 1) * P],
                                              w["W_QK"][:, c, :], start=c == 0, stop=c == EC - 1)
                mm.then_inc(qk_psum, 1)

            def values(i, n):
                t, half = divmod(n, 2)
                if n >= 2:
                    eng.wait_ge(kv_ready, i * 2 * N + 2 * n - 2)
                for c in range(EC):
                    mm = nc.tensor.matmul(psV[n % 2][:, :], xnT[:, c, 1 + t * P:1 + (t + 1) * P],
                                          W_V[:, c, half * HALF:(half + 1) * HALF], start=c == 0, stop=c == EC - 1)
                mm.then_inc(v_psum, 1)

            def denominators(i):
                eng.wait_ge(trig_ready, i * 2 + 2)
                for t in range(TT):
                    for u in range(t + 1):
                        mm = nc.tensor.matmul(psQ[:, 128 + t * 32:128 + (t + 1) * 32],
                                              w["tri"][:, :] if u == t else w["ones"][:, :],
                                              trig[:, :, u, H3:2 * H3], start=u == 0, stop=u == t)
                mm.then_inc(den_psum, 1)

            def running_sum(i, n):
                t, half = divmod(n, 2)
                eng.wait_ge(kv_lo_ready, i * N + n + 1)
                if t:
                    eng.wait_ge(weighted, i * 2 * N + 2 * n - 2)
                for j in range(2):
                    sums = psC[2 * half + j][:, :]
                    if t:
                        for part in (kv_hi, kv_lo):
                            nc.tensor.matmul(sums, rest[:, :], part[(t - 1) % 3][:, half, j, :],
                                             start=False, stop=True, skip_group_check=True)
                    for part in (kv_hi, kv_lo):
                        mm = nc.tensor.matmul(sums, tri[:, :], part[t % 3][:, half, j, :],
                                              start=t == 0 and part is kv_hi, stop=True, skip_group_check=True)
                mm.then_inc(cum_ready, 1)

            def turn_heads(i, t):
                eng.wait_ge(heads_ready, i * N + 2 * t + 2)
                if t:
                    eng.wait_ge(headsT_ready, i * N + 2 * t)
                for k in range(8):
                    mm = nc.tensor.transpose(a.psT[k // 4][:, (k % 4) * P:(k % 4 + 1) * P],
                                             heads[:, t, k * P:(k + 1) * P], g.ident[:, :])
                    if k % 4 == 3:
                        mm.then_inc(headsT_psum, 1)

            def project(i, t):
                eng.wait_ge(headsT_ready, i * N + 2 * t + 2)
                if t == 0:
                    eng.wait_ge(weighted, (i + 1) * 2 * N)
                for k in range(8):
                    mm = nc.tensor.matmul(psC[t][:, 0:E], headsT[:, t % 2, k, :], W_O[:, k, :],
                                          start=k == 0, stop=k == 7)
                mm.then_inc(o_psum, 1)

            def body(i, more):
                values(i, 0)
                denominators(i)
                values(i, 1)
                for n in range(2, N):
                    values(i, n)
                    running_sum(i, n - 2)
                running_sum(i, N - 2)
                if more:
                    eng.wait_ge(kv_ready, (i + 1) * 2 * N)
                    a.tensor(eng, i + 1)
                running_sum(i, N - 1)
                if more:
                    eng.wait_ge(a.ready, i * EC + 2 * EC)
                turn_heads(i, 0)
                if more:
                    queries_keys(i + 1)
                for t in range(TT):
                    if t + 1 < TT:
                        turn_heads(i, t + 1)
                    project(i, t)
                eng.wait_ge(headsT_ready, i * N + N)
                eng.wait_ge(o_ready, i * TT + TT)
            a.tensor(eng, 0)
            queries_keys(0)
            each_batch(eng, body)


WEIGHTS = [
    [("Wq", "mat", (E, E)), ("Wk", "mat", (E, E)), ("Wv", "mat", (E, E)), ("Wo", "mat", (E, E)),
     ("bq", "flat", (P, EC)), ("bk", "flat", (P, EC)), ("bv", "flat", (P, EC)), ("bo", "flat", (P, 2 * E)),
     ("head8", "flat", (P, 8)), ("head16", "flat", (P, EC * H0))],
    [("W1", "mat", (E, FF)), ("W2", "mat", (FF, E)), ("b1", "flat", (P, FT)), ("b2", "flat", (P, 2 * E))],
    [("W_in", "mat", (E, 2048 + HS)), ("W_out", "mat", (HS * DS, E)), ("conv_w", "flat", (P, NPAIR * TAPS)),
     ("conv_b", "flat", (P, NPAIR)), ("A_log", "flat", (P, NPAIR)), ("D", "flat", (P, NPAIR)),
     ("dt_bias", "flat", (P, TT * HS)), ("onehot", "flat", (P, NPAIR * P)), ("same_head", "flat", (P, P)),
     ("masks", "flat", (P, MASKED * 64))],
    [("W_r", "mat", (E, E)), ("W_k", "mat", (E, E)), ("W_v", "mat", (E, E)), ("mu_r", "flat", (P, EC)), ("mu_k", "flat", (P, EC))],
    [("Wq", "mat", (E, E)), ("Wk", "mat", (E, E)), ("Wv", "mat", (E, E)), ("Wo", "mat", (2 * E, E)),
     ("gamma", "flat", (P, H2)), ("rows", "flat", (P, 4)), ("select", "flat", (P, 12 * P))],
    [("W_r", "mat", (E, E)), ("W_k", "mat", (E, E)), ("W_v", "mat", (E, E)), ("mu_r", "flat", (P, EC)), ("mu_k", "flat", (P, EC))],
    [("W_QK", "mat", (E, 2 * H3)), ("W_V", "mat", (E, H3 * D3)), ("W_O", "mat", (H3 * D3, E)),
     ("tri", "flat", (P, P)), ("rest", "flat", (P, P)), ("ones", "flat", (P, P))],
    [("W1", "mat", (E, FF)), ("W2", "mat", (FF, E))],
]
ARENA = (6200, 4640)
SUBLAYERS = [windowed_attention, gelu_mlp, state_space, rwkv_mix, distance_attention, rwkv_mix, angular_attention, spiking_mlp]


def build(nc, d, out, subs=tuple(range(8))):
    with ExitStack() as ctx:
        lasting = Semaphores()
        ctx.enter_context(lasting.stack)
        g = Common(nc, ctx, lasting)
        g.x = g.sb("x", [P, NB * TT, E])
        g.ident = g.sb("ident", [P, P])
        g.minus_half = g.sb("minus_half", [P, TT])
        first_loaded = g.sem("first_loaded")
        g.x_loaded = g.sem("x_loaded")
        g.const_ready = g.sem("const_ready")
        out_stored = g.sem("out_stored")
        g.weights = [g.sem(f"weights{k}") for k in range(8)]
        arena = [g.sb(f"arena{j}", [P, ARENA[j]]) for j in range(2)]
        loads, tiles = [[] for _ in range(8)], [{} for _ in range(8)]
        for k in subs:
            at = 0
            for name, kind, size in WEIGHTS[k]:
                src = d[f"l{k}_{name}"]
                width = size[0] // P * size[1] if kind == "mat" else size[1]
                tile = arena[k % 2][0:P if kind == "mat" else size[0], at:at + width]
                at += width + width % 2
                if kind == "mat":
                    tile = tile.rearrange("p (c n) -> p c n", n=size[1])
                    src = src.rearrange("(c p) n -> p c n", p=P)
                loads[k].append((tile, src))
                tiles[k][name] = tile
            assert at <= ARENA[k % 2], (k, at)
            tiles[k]["sem"], tiles[k]["count"] = k, 16 * len(loads[k])

        def load_weights(eng, k):
            for tile, src in loads[k]:
                eng.dma_start(tile, src).then_inc(g.weights[k], 16)

        with nc.Block() as block:
            @block.sync
            def _(eng):
                eng.dma_start(g.ident[:, :], d["ident"]).then_inc(first_loaded, 16)
                for b in range(NB):
                    eng.dma_start(g.x[:, b * TT:(b + 1) * TT, :], d["x"][b].rearrange("(t p) e -> p t e", p=P)
                                  ).then_inc(g.x_loaded if b else first_loaded, 16)
                    if b == 0:
                        load_weights(eng, subs[0])

            @block.vector
            def _(eng):
                nc.vector.memset(g.minus_half[:, :], -0.5).then_inc(g.const_ready, 1)
                eng.wait_ge(g.const_ready, 1)
                eng.wait_ge(first_loaded, 16 * 2)

        before = Semaphores()
        for k, after in zip(subs, list(subs[1:]) + [None]):
            def look_ahead(eng, z, cleared=before.all, after=after):
                if after is not None:
                    load_weights(eng, after)
                for sem in cleared:
                    eng.sem_clear(sem)
                if after is None:
                    with eng.Fori(0, NB) as i:
                        eng.wait_ge(z.added, i * TT + 2 * TT)
                        eng.dma_start(out[bass.ds(i, 1)].rearrange("b (t p) e -> p (b t) e", p=P),
                                      g.x[:, bass.ds(i * TT, TT), :]).then_inc(out_stored, 16)
                    eng.wait_ge(out_stored, 16 * NB)
            g.sems, g.look_ahead, g.loading = Semaphores(), look_ahead, k == subs[0]
            SUBLAYERS[k](nc, g, f"l{k}_", tiles[k])
            before.stack.close()
            before = g.sems
        before.stack.close()


def state_space_layout(np, v, col):
    W = v["L1_attn_W_in"]
    inner = HS * DS
    heads = W[2 * inner:].reshape(HS, 2 * DS + 1, E)
    parts = [W[:2 * inner], heads[:, :DS].reshape(inner, E), heads[:, DS:2 * DS].reshape(inner, E), heads[:, 2 * DS]]
    same = np.kron(np.eye(2), np.ones((DS, DS))).astype(np.float32)
    onehot = np.zeros((P, NPAIR, 2, DS), np.float32)
    for hd in range(HS):
        onehot[hd, hd // 2, hd % 2] = 1.0
    masks = np.zeros((P, MASKED, 64), np.float32)
    for L in range(MASKED):
        m = 1 << L
        for n in range(64):
            k = n // m
            masks[2 * m * k:2 * m * k + m, L, n] = 1.0
    return {
        "W_in": np.concatenate(parts).T, "W_out": v["L1_attn_W_out"].T,
        "conv_w": v["L1_attn_conv_w"][:, 0].reshape(NPAIR, P, TAPS).transpose(1, 0, 2).reshape(P, NPAIR * TAPS),
        "conv_b": col(v["L1_attn_conv_b"]), "A_log": col(v["L1_attn_A_log"].reshape(-1)),
        "D": col(np.repeat(v["L1_attn_D"], DS)),
        "dt_bias": np.broadcast_to(np.tile(v["L1_attn_dt_bias"], TT), (P, TT * HS)),
        "onehot": onehot.reshape(P, NPAIR * P), "same_head": same, "masks": masks.reshape(P, MASKED * 64),
    }


def split_rows(np):
    rows = np.zeros((P, 4), np.float32)
    select = np.zeros((P, 12, P), np.float32)
    for side, low, ones, norm in ((0, slice(32, 48), 50, 48), (1, slice(16, 32), 48, 50)):
        for slot in (0, SLOT):
            r = rows[slot:slot + SLOT]
            r[low, side] = -1.0
            r[norm + 1, side] = -1.0
            r[ones:ones + 2, side] = 1.0
            r[ones:ones + 2, 2 + side] = 1.0
    for k in range(4):
        for b in range(2):
            for j in range(D2):
                src = (2 * k + b) * D2 + j
                for copy in range(3):
                    select[src, k, b * SLOT + copy * D2 + j] = 1.0
                for side, norm in ((0, 48), (1, 50)):
                    select[src, 4 + 4 * side + k, b * SLOT + norm:b * SLOT + norm + 2] = 1.0
    return rows, select.reshape(P, 12 * P)


def layouts(v):
    import numpy as np

    def col(a):
        return a.reshape(-1, P).T

    def row(a):
        return np.broadcast_to(np.concatenate([a, a]), (P, 2 * E))

    d = {"x": v["L0_attn_hidden_states"], "ident": np.eye(P, dtype=np.float32)}
    for key, a in state_space_layout(np, v, col).items():
        d["l2_" + key] = a
    for k, layer in ((3, "L1_ffn_"), (5, "L2_ffn_")):
        for name in ("W_r", "W_k", "W_v"):
            d[f"l{k}_{name}"] = v[layer + name].T
        for name in ("mu_r", "mu_k"):
            d[f"l{k}_{name}"] = col(v[layer + name])
    for name in ("Wq", "Wk", "Wv", "Wo"):
        d["l0_" + name] = v["L0_attn_" + name]
    for name in ("bq", "bk", "bv"):
        d["l0_" + name] = col(v["L0_attn_" + name])
    d["l0_bo"] = row(v["L0_attn_bo"])
    head8 = np.repeat(np.eye(8, dtype=np.float32), D0, axis=0)
    d["l0_head8"] = head8
    head16 = np.zeros((P, EC, H0), np.float32)
    for c in range(EC):
        head16[:, c, 8 * c:8 * c + 8] = head8
    d["l0_head16"] = head16.reshape(P, EC * H0)
    d["l1_W1"], d["l1_W2"] = v["L0_ffn_W1"].T, v["L0_ffn_W2"].T
    d["l1_b1"] = col(v["L0_ffn_b1"])
    d["l1_b2"] = row(v["L0_ffn_b2"])
    for name in ("Wq", "Wk", "Wv"):
        d["l4_" + name] = v["L2_attn_" + name]
    wo = np.zeros((H2, 2 * D2, E), np.float32)
    wo[:, :D2] = v["L2_attn_Wo"].reshape(H2, D2, E)
    d["l4_Wo"] = wo.reshape(2 * E, E)
    d["l4_gamma"] = np.broadcast_to(v["L2_attn_gamma"], (P, H2))
    d["l4_rows"], d["l4_select"] = split_rows(np)
    tri = np.triu(np.ones((P, P), np.float32))
    d["l6_W_QK"] = np.concatenate([v["L3_attn_W_Q"][:, :, 0], v["L3_attn_W_K"][:, :, 0]]).T
    d["l6_W_V"] = v["L3_attn_W_V"].transpose(1, 0, 2).reshape(E, -1)
    d["l6_W_O"] = v["L3_attn_W_O"].transpose(2, 1, 0).reshape(-1, E)
    d["l6_tri"], d["l6_rest"], d["l6_ones"] = tri, np.tril(np.ones((P, P), np.float32), -1), np.ones((P, P), np.float32)
    d["l7_W1"], d["l7_W2"] = v["L3_ffn_W_fc"].T, v["L3_ffn_W_proj"].T
    return {k: np.ascontiguousarray(a) for k, a in d.items()}


def kernel(**inputs):
    import numpy as np
    import concourse.bacc as bacc
    from concourse.bass_utils import run_bass_kernel_spmd

    arrays = layouts({k: np.asarray(a) for k, a in inputs.items()})
    nc = bacc.Bacc("TRN2", target_bir_lowering=False, num_devices=1)
    dram = {k: nc.dram_tensor(k + "_dram", a.shape, mybir.dt.from_np(a.dtype), kind="ExternalInput").ap()
            for k, a in arrays.items()}
    out = nc.dram_tensor("out_dram", (NB, T, E), F32, kind="ExternalOutput").ap()
    build(nc, dram, out)
    r = run_bass_kernel_spmd(nc, [{k + "_dram": a for k, a in arrays.items()}], core_ids=[0])
    return r.results[0]["out_dram"]
```
